# Optimizing a Trainium2 kernel written in Bass

```python
import numpy as np
import jax
import jax.numpy as jnp

def _softmax(x, axis=-1):
    return jax.nn.softmax(x, axis=axis)

def _gelu(x):
    return jax.nn.gelu(x, approximate=True)

def _silu(x):
    return jax.nn.silu(x)

def _sigmoid(x):
    return jax.nn.sigmoid(x)

def _layernorm(x, axis=-1, eps=1e-05):
    m = jnp.mean(x, axis=axis, keepdims=True)
    v = jnp.var(x, axis=axis, keepdims=True)
    return (x - m) / jnp.sqrt(v + eps)

def _scatter_add(tgt, idx, src, axis=0):
    return tgt.at[idx].add(src)

def _segment_sum(src, seg, n):
    return jax.ops.segment_sum(src, seg, n)
kernel_name = 'mk_macaron_d2_jaxref_r8_654941'

def setup_inputs(seed: int=0):
    np.random.seed(seed)
    _w = jnp.asarray

    def _L0_attn_setup():
        import jax, jax.numpy as jnp
        import numpy as np
        B, T, C = (4, 256, 128)
        H, D = (16, 64)
        MAX_REL = 16
        NUM_BUCKETS = 2 * MAX_REL + 1
        key = jax.random.key(seed)
        ks = jax.random.split(key, 7)
        x = jax.random.normal(ks[0], (B, T, C), dtype=jnp.float32)
        Wq = jax.random.normal(ks[1], (H, C, D), dtype=jnp.float32) * 0.02
        Wk = jax.random.normal(ks[2], (H, C, D), dtype=jnp.float32) * 0.02
        Wv = jax.random.normal(ks[3], (H, C, D), dtype=jnp.float32) * 0.02
        Wp = jax.random.normal(ks[4], (H * D, C), dtype=jnp.float32) * 0.02
        bp = jnp.zeros((C,), dtype=jnp.float32)
        rel_table = jax.random.normal(ks[5], (NUM_BUCKETS, H), dtype=jnp.float32) * 0.02
        return {'x': x, 'Wq': Wq, 'Wk': Wk, 'Wv': Wv, 'Wp': Wp, 'bp': bp, 'rel_table': rel_table}
    _L0_attn_in = _L0_attn_setup()

    def _L0_ffn_setup():
        import jax, jax.numpy as jnp
        import numpy as np
        DIM = 128
        HIDDEN = 384
        SCALE = 1.0 / 127.0

        def _dequant(w_int, dtype):
            return w_int.astype(dtype) * jnp.asarray(SCALE, dtype)
        key = jax.random.key(seed)
        k_x, k_g, k_u, k_d = jax.random.split(key, 4)
        x = jax.random.normal(k_x, (4, 256, DIM), dtype=jnp.float32)
        w_gate = jax.random.randint(k_g, (HIDDEN, DIM), -127, 128, dtype=jnp.int32)
        w_up = jax.random.randint(k_u, (HIDDEN, DIM), -127, 128, dtype=jnp.int32)
        w_down = jax.random.randint(k_d, (DIM, HIDDEN), -127, 128, dtype=jnp.int32)
        return {'x': x, 'w_gate': w_gate, 'w_up': w_up, 'w_down': w_down}
    _L0_ffn_in = _L0_ffn_setup()

    def _L1_attn_setup():
        import jax, jax.numpy as jnp
        import numpy as np
        B, S, E, H = (2, 256, 128, 16)
        D = E // H
        NEG_INF = -1e+30

        def alibi_slopes(n_head):
            return jnp.asarray([2.0 ** (-8.0 * (i + 1) / n_head) for i in range(n_head)], dtype=jnp.float32)
        key = jax.random.key(seed)
        ks = jax.random.split(key, 5)
        scale = 0.02
        return {'x': jax.random.normal(ks[0], (B, S, E), dtype=jnp.float32), 'W_kqv': jax.random.normal(ks[1], (E, 3 * E), dtype=jnp.float32) * scale, 'b_kqv': jnp.zeros((3 * E,), dtype=jnp.float32), 'W_proj': jax.random.normal(ks[2], (E, E), dtype=jnp.float32) * scale, 'b_proj': jnp.zeros((E,), dtype=jnp.float32), 'slopes': alibi_slopes(H)}
    _L1_attn_in = _L1_attn_setup()

    def _L1_ffn_setup():
        import jax, jax.numpy as jnp
        import numpy as np
        D = 128
        H = 512
        E = 8
        TOPK = 2
        CAP_F = 1.25
        key = jax.random.key(seed)
        ks = jax.random.split(key, 6)
        sc = 0.02
        return {'x': jax.random.normal(ks[0], (4, 256, D), jnp.float32), 'Wg': jax.random.normal(ks[1], (D, E), jnp.float32) * sc, 'bg': jnp.zeros((E,), jnp.float32), 'W1': jax.random.normal(ks[2], (E, D, H), jnp.float32) * sc, 'W2': jax.random.normal(ks[3], (E, D, H), jnp.float32) * sc, 'W3': jax.random.normal(ks[4], (E, H, D), jnp.float32) * sc}
    _L1_ffn_in = _L1_ffn_setup()
    _d = {'L0_attn_x': _L0_attn_in['x'], 'L0_attn_Wq': _L0_attn_in['Wq'], 'L0_attn_Wk': _L0_attn_in['Wk'], 'L0_attn_Wv': _L0_attn_in['Wv'], 'L0_attn_Wp': _L0_attn_in['Wp'], 'L0_attn_bp': _L0_attn_in['bp'], 'L0_attn_rel_table': _L0_attn_in['rel_table'], 'L0_ffn_w_gate': _L0_ffn_in['w_gate'], 'L0_ffn_w_up': _L0_ffn_in['w_up'], 'L0_ffn_w_down': _L0_ffn_in['w_down'], 'L1_attn_W_kqv': _L1_attn_in['W_kqv'], 'L1_attn_b_kqv': _L1_attn_in['b_kqv'], 'L1_attn_W_proj': _L1_attn_in['W_proj'], 'L1_attn_b_proj': _L1_attn_in['b_proj'], 'L1_attn_slopes': _L1_attn_in['slopes'], 'L1_ffn_Wg': _L1_ffn_in['Wg'], 'L1_ffn_bg': _L1_ffn_in['bg'], 'L1_ffn_W1': _L1_ffn_in['W1'], 'L1_ffn_W2': _L1_ffn_in['W2'], 'L1_ffn_W3': _L1_ffn_in['W3']}
    _x0 = _d['L0_attn_x']
    _d['L0_attn_x'] = jax.random.normal(jax.random.fold_in(jax.random.key(seed), 1), (8, 512, 128), dtype=_x0.dtype)
    del _x0
    return _d

def reference(L0_attn_x, L0_attn_Wq, L0_attn_Wk, L0_attn_Wv, L0_attn_Wp, L0_attn_bp, L0_attn_rel_table, L0_ffn_w_gate, L0_ffn_w_up, L0_ffn_w_down, L1_attn_W_kqv, L1_attn_b_kqv, L1_attn_W_proj, L1_attn_b_proj, L1_attn_slopes, L1_ffn_Wg, L1_ffn_bg, L1_ffn_W1, L1_ffn_W2, L1_ffn_W3):

    def _L0_attn_ref(x, Wq, Wk, Wv, Wp, bp, rel_table):
        import jax, jax.numpy as jnp
        import numpy as np
        B, T, C = (4, 256, 128)
        H, D = (16, 64)
        MAX_REL = 16
        NUM_BUCKETS = 2 * MAX_REL + 1
        Tq = x.shape[1]
        pos = jnp.arange(Tq)
        rel = pos[None, :] - pos[:, None]
        idx = jnp.clip(rel + MAX_REL, 0, NUM_BUCKETS - 1)
        bias = rel_table[idx]
        bias = jnp.transpose(bias, (2, 0, 1))
        q = jnp.einsum('btc,hcd->bhtd', x, Wq)
        k = jnp.einsum('btc,hcd->bhtd', x, Wk)
        v = jnp.einsum('btc,hcd->bhtd', x, Wv)
        scale = 1.0 / jnp.sqrt(jnp.float32(D))
        scores = jnp.einsum('bhtd,bhsd->bhts', q, k) * scale + bias[None]
        causal = jnp.tril(jnp.ones((Tq, Tq), dtype=bool))
        scores = jnp.where(causal[None, None], scores, jnp.float32(-jnp.inf))
        w = jax.nn.softmax(scores, axis=-1)
        out = jnp.einsum('bhts,bhsd->bhtd', w, v)
        out = jnp.transpose(out, (0, 2, 1, 3)).reshape(x.shape[0], Tq, H * D)
        return out @ Wp + bp

    def _L0_ffn_ref(x, w_gate, w_up, w_down):
        import jax, jax.numpy as jnp
        import numpy as np
        DIM = 128
        HIDDEN = 384
        SCALE = 1.0 / 127.0

        def _dequant(w_int, dtype):
            return w_int.astype(dtype) * jnp.asarray(SCALE, dtype)
        wg = _dequant(w_gate, x.dtype)
        wu = _dequant(w_up, x.dtype)
        wd = _dequant(w_down, x.dtype)
        gate = jnp.einsum('bsd,hd->bsh', x, wg)
        up = jnp.einsum('bsd,hd->bsh', x, wu)
        h = jax.nn.silu(gate) * up
        return jnp.einsum('bsh,dh->bsd', h, wd)

    def _L1_attn_ref(x, W_kqv, b_kqv, W_proj, b_proj, slopes):
        import jax, jax.numpy as jnp
        import numpy as np
        B, S, E, H = (2, 256, 128, 16)
        D = E // H
        NEG_INF = -1e+30

        def alibi_slopes(n_head):
            return jnp.asarray([2.0 ** (-8.0 * (i + 1) / n_head) for i in range(n_head)], dtype=jnp.float32)
        b, s, e = x.shape
        kqv = x @ W_kqv + b_kqv
        k, q, v = jnp.split(kqv, 3, axis=-1)
        k = k.reshape(b, s, H, D)
        q = q.reshape(b, s, H, D)
        v = v.reshape(b, s, H, D)
        attn = jnp.einsum('bqhd,bkhd->bhqk', q, k) * (1.0 / jnp.sqrt(jnp.float32(D)))
        i = jnp.arange(s)[:, None]
        j = jnp.arange(s)[None, :]
        rel = (j - i).astype(jnp.float32)
        bias = slopes[:, None, None] * jnp.tril(rel)
        bias = jnp.where(j > i, NEG_INF, bias)
        attn = jax.nn.softmax(attn + bias[None], axis=-1)
        y = jnp.einsum('bhqk,bkhd->bqhd', attn, v).reshape(b, s, e)
        return y @ W_proj + b_proj

    def _L1_ffn_ref(x, Wg, bg, W1, W2, W3):
        import jax, jax.numpy as jnp
        import numpy as np
        D = 128
        H = 512
        E = 8
        TOPK = 2
        CAP_F = 1.25
        b, s, d = x.shape
        xt = x.reshape(-1, d)
        T = xt.shape[0]
        capacity = int(T / E * CAP_F)
        gate_logits = xt @ Wg + bg
        top_v, top_i = jax.lax.top_k(gate_logits, TOPK)
        expert_label = jax.nn.one_hot(top_i, E, dtype=xt.dtype).sum(axis=1)
        seq = jnp.cumsum(expert_label, axis=0) * expert_label
        valid = (seq > 0) & (seq <= capacity)
        slot = (seq - 1.0).astype(jnp.int32)
        flat_idx = jnp.where(valid, jnp.arange(E, dtype=jnp.int32)[None, :] * capacity + slot, E * capacity)
        src = jnp.broadcast_to(xt[:, None, :], (T, E, d)).reshape(-1, d)
        buf = jnp.zeros((E * capacity + 1, d), xt.dtype).at[flat_idx.reshape(-1)].set(src)
        disp = buf[:-1].reshape(E, capacity, d)
        h = jax.nn.silu(jnp.einsum('ecd,edh->ech', disp, W1)) * jnp.einsum('ecd,edh->ech', disp, W2)
        out = jnp.einsum('ech,ehd->ecd', h, W3)
        out_flat = jnp.concatenate([out.reshape(E * capacity, d), jnp.zeros((1, d), xt.dtype)], axis=0)
        all_expert_output = out_flat[flat_idx]
        sel = jnp.take_along_axis(all_expert_output, top_i[:, :, None], axis=1)
        routing_w = jax.nn.softmax(top_v, axis=-1)
        y = (routing_w[:, :, None] * sel).sum(axis=1)
        return y.reshape(b, s, d)
    x = L0_attn_x
    x = x + 0.5 * _L0_ffn_ref(_layernorm(x, axis=-1), L0_ffn_w_gate, L0_ffn_w_up, L0_ffn_w_down)
    x = x + _L0_attn_ref(_layernorm(x, axis=-1), L0_attn_Wq, L0_attn_Wk, L0_attn_Wv, L0_attn_Wp, L0_attn_bp, L0_attn_rel_table)
    x = x + 0.5 * _L0_ffn_ref(_layernorm(x, axis=-1), L0_ffn_w_gate, L0_ffn_w_up, L0_ffn_w_down)
    x = x + 0.5 * _L1_ffn_ref(_layernorm(x, axis=-1), L1_ffn_Wg, L1_ffn_bg, L1_ffn_W1, L1_ffn_W2, L1_ffn_W3)
    x = x + _L1_attn_ref(_layernorm(x, axis=-1), L1_attn_W_kqv, L1_attn_b_kqv, L1_attn_W_proj, L1_attn_b_proj, L1_attn_slopes)
    x = x + 0.5 * _L1_ffn_ref(_layernorm(x, axis=-1), L1_ffn_Wg, L1_ffn_bg, L1_ffn_W1, L1_ffn_W2, L1_ffn_W3)
    return x

_drawn_inputs = setup_inputs


def setup_inputs(seed=0):
    import zlib

    import numpy as np

    out = dict(_drawn_inputs(seed))
    spreads = {'L0_attn_bp': (0.0, 2.0),
     'L1_attn_b_kqv': (0.0, 2.0),
     'L1_attn_b_proj': (0.0, 2.0),
     'L1_ffn_bg': (0.0, 2.0)}
    factors = {'L0_attn_Wq': 8.0,
     'L0_attn_Wk': 8.0,
     'L0_attn_Wv': 8.0,
     'L0_attn_Wp': 8.0,
     'L0_attn_rel_table': 64.0,
     'L1_attn_W_kqv': 42.526,
     'L1_attn_W_proj': 38.77,
     'L1_attn_slopes': 54.947,
     'L1_ffn_Wg': 27.356,
     'L1_ffn_W1': 27.562,
     'L1_ffn_W2': 24.881,
     'L1_ffn_W3': 24.9}
    for name, (base, spread) in spreads.items():
        noise = np.random.default_rng([zlib.crc32(name.encode()), seed]).standard_normal(out[name].shape)
        drawn = base * np.exp(spread * noise) if base else spread * noise
        out[name] = jnp.asarray(drawn.astype(out[name].dtype))
    for name, factor in factors.items():
        out[name] = (out[name] * factor).astype(out[name].dtype)
    return out
```

```python
from contextlib import ExitStack

import concourse.bass as bass
import concourse.mybir as mybir
import numpy as np

F = mybir.dt.float32
FR = mybir.dt.float32r
I32 = mybir.dt.int32
ALU = mybir.AluOpType
ACT = mybir.ActivationFunctionType
AX = mybir.AxisListType

P = 128
B, S, C = 8, 512, 128
TOKENS = B * S
TILES = TOKENS // P
GROUPS = TOKENS // 512
QT = S // P
H = 16
D0, D1 = 64, 8
HID0 = 384
HC0 = HID0 // P
E, TOPK, HID1 = 8, 2, 512
HC1 = HID1 // P
CAP = int(TOKENS / E * 1.25)
ST = CAP // P
SLOTS = E * CAP
EPS = 1e-5
NEG = -1e30
BAND = 257

ORDER = (3, 2, 0, 1)
START = {3: 0, 2: 512, 0: 896, 1: 1024}
WIDTH = S * (QT + 1) // 2
TGROUPS = ((3,), (2, 0), (1,))


def program(nc, x_in, wqT, wkT, wvT, wp, bp, table, wg0, wu0, wd0,
            kqvT, b1, bq, wproj, bproj, slopes, wgate, bgate, W1, W2, W3, out):
    top = ExitStack()

    def sbuf(ctx, name, shape, dt=F):
        return ctx.enter_context(nc.sbuf_tensor(name, shape, dt))

    def banks(ctx, name, n):
        return [ctx.enter_context(nc.psum_tensor(f"{name}{i}", [P, 512], F)) for i in range(n)]

    def sems(ctx, tag, *names):
        made = [nc.alloc_semaphore(name=f"{tag}_{n}") for n in names]

        def clear():
            nc.clear_and_free_semaphores(made)
            nc.all_engine_barrier()
        ctx.callback(clear)
        return made

    slots_in = nc.dram_tensor("slots_in", [SLOTS + P, C], F).ap()
    slots_out = nc.dram_tensor("slots_out", [SLOTS + P, C], F).ap()
    skew = nc.dram_tensor("skew", [H, P, BAND], F)

    with top:
        x = sbuf(top, "x", [P, TILES, C])
        ident = sbuf(top, "ident", [P, P])
        XTh = sbuf(top, "XTh", [P, TOKENS], FR)
        XTl = sbuf(top, "XTl", [P, TOKENS], FR)
        half = sbuf(top, "half", [P, TILES])
        one = sbuf(top, "one", [P, 1])

        with ExitStack() as ctx:
            zeros = sbuf(ctx, "zeros", [P, C])
            loaded, made, zeroed = sems(ctx, "ld", "x", "made", "zeroed")
            with nc.Block() as block:
                @block.sync
                def _(sp):
                    sp.dma_start(x[:], x_in.rearrange("(t p) c -> p t c", p=P)).then_inc(loaded, 16)
                    sp.wait_ge(made, 2)
                    for n in range(SLOTS // P):
                        sp.dma_start(slots_in[n * P:(n + 1) * P, :], zeros[:]).then_inc(zeroed, 16)
                    sp.dma_start(slots_out[SLOTS:SLOTS + P, :], zeros[:]).then_inc(zeroed, 16)
                    sp.wait_ge(loaded, 16)
                    sp.wait_ge(zeroed, 16 * (SLOTS // P + 1))

                @block.gpsimd
                def _(pool):
                    nc.gpsimd.memset(ident[:], 0.0).then_inc(made, 1)
                    nc.gpsimd.memset(zeros[:], 0.0).then_inc(made, 1)
                    nc.gpsimd.memset(half[:], -0.5).then_inc(made, 1)
                    nc.gpsimd.memset(one[:], 1.0).then_inc(made, 1)
                    pool.wait_ge(made, 4)
                    nc.gpsimd.affine_select(out=ident[:], in_=ident[:], compare_op=ALU.not_equal, fill=1.0,
                                            base=0, pattern=[[-1, P]], channel_multiplier=1).then_inc(made, 1)
                    pool.wait_ge(made, 5)

        def layernorm(tag, keep=None):
            with ExitStack() as ctx:
                st = sbuf(ctx, f"{tag}st", [P, TILES, 6])
                mv = sbuf(ctx, f"{tag}mv", [P, TILES, 2])
                ve = sbuf(ctx, f"{tag}ve", [P, TILES])
                rs = sbuf(ctx, f"{tag}rs", [P, TILES])
                t1 = sbuf(ctx, f"{tag}t1", [P, TILES])
                rstd = sbuf(ctx, f"{tag}rstd", [P, TILES])
                xn = sbuf(ctx, f"{tag}xn", [P, 2, 4, C])
                tp = banks(ctx, f"{tag}tp", 2)
                ve_ok, rs_ok, chain, xn_ok, tp_ok, hi_ok, lo_ok, kept = sems(
                    ctx, tag, "ve_ok", "rs_ok", "chain", "xn_ok", "tp_ok", "hi_ok", "lo_ok", "kept")
                with nc.Block() as block:
                    @block.vector
                    def _(dve):
                        for t in range(TILES):
                            nc.vector.bn_stats(st[:, t, :], x[:, t, :]).then_inc(chain, 1)
                        dve.wait_ge(chain, TILES)
                        for t in range(TILES):
                            nc.vector.bn_aggr(mv[:, t, :], st[:, t, :]).then_inc(chain, 1)
                        dve.wait_ge(chain, 2 * TILES)
                        nc.vector.tensor_scalar(ve[:], mv[:, :, 1], EPS, None, ALU.add).then_inc(ve_ok, 1)
                        dve.wait_ge(rs_ok, 1)
                        nc.vector.tensor_tensor(t1[:], rs[:], rs[:], ALU.mult).then_inc(ve_ok, 1)
                        dve.wait_ge(ve_ok, 2)
                        nc.vector.tensor_tensor(t1[:], t1[:], ve[:], ALU.mult).then_inc(ve_ok, 1)
                        dve.wait_ge(ve_ok, 3)
                        nc.vector.tensor_scalar(t1[:], t1[:], -0.5, 1.5, ALU.mult, ALU.add).then_inc(ve_ok, 1)
                        dve.wait_ge(ve_ok, 4)
                        nc.vector.tensor_tensor(rstd[:], rs[:], t1[:], ALU.mult).then_inc(ve_ok, 1)
                        dve.wait_ge(ve_ok, 5)

                        def normalise(g, b):
                            for j in range(4):
                                n = nc.vector.tensor_scalar(
                                    xn[:, b, j, :], x[:, bass.ds(g * 4 + j, 1), :], mv[:, bass.ds(g * 4 + j, 1), 0],
                                    rstd[:, bass.ds(g * 4 + j, 1)], ALU.subtract, ALU.mult)
                            n.then_inc(xn_ok, 1)

                        def low(g, b):
                            dve.wait_ge(hi_ok, g + 1)
                            nc.vector.tensor_tensor(XTl[:, bass.ds(g * 512, 512)], tp[b][:],
                                                    XTh[:, bass.ds(g * 512, 512)].bitcast(F),
                                                    ALU.subtract).then_inc(lo_ok, 1)

                        normalise(0, 0)
                        normalise(1, 1)
                        low(0, 0)
                        low(1, 1)
                        with dve.Fori(1, GROUPS // 2) as m:
                            dve.wait_ge(tp_ok, 2 * m)
                            if keep is not None:
                                dve.wait_ge(kept, 2 * m)
                            normalise(2 * m, 0)
                            normalise(2 * m + 1, 1)
                            low(2 * m, 0)
                            low(2 * m + 1, 1)

                    @block.gpsimd
                    def _(pool):
                        pool.wait_ge(ve_ok, 1)
                        nc.gpsimd.tensor_tensor(rs[:], ve[:], half[:], ALU.pow).then_inc(rs_ok, 1)
                        if keep is not None:
                            with pool.Fori(0, GROUPS // 2) as m:
                                for b in range(2):
                                    pool.wait_ge(xn_ok, 2 * m + b + 1)
                                    nc.gpsimd.tensor_copy(keep[:, bass.ds(8 * m + 4 * b, 4), :],
                                                          xn[:, b, :, :]).then_inc(kept, 1)
                            pool.wait_ge(kept, GROUPS)

                    @block.tensor
                    def _(pe):
                        def turn(g, b):
                            pe.wait_ge(xn_ok, g + 1)
                            for j in range(4):
                                t = nc.tensor.transpose(tp[b][:, j * P:(j + 1) * P], xn[:, b, j, :], ident[:])
                            t.then_inc(tp_ok, 1)
                        turn(0, 0)
                        turn(1, 1)
                        with pe.Fori(1, GROUPS // 2) as m:
                            for b in range(2):
                                pe.wait_ge(lo_ok, 2 * m - 1 + b)
                                turn(2 * m + b, b)

                    @block.scalar
                    def _(act):
                        with act.Fori(0, GROUPS // 2) as m:
                            for b in range(2):
                                act.wait_ge(tp_ok, 2 * m + b + 1)
                                nc.scalar.activation(XTh[:, bass.ds(1024 * m + 512 * b, 512)], tp[b][:],
                                                     ACT.Copy).then_inc(hi_ok, 1)

        def ffn0(tag):
            with ExitStack() as ctx:
                wi = sbuf(ctx, f"{tag}wi", [P, 3, HID0], I32)
                wf = sbuf(ctx, f"{tag}wf", [P, 3, HID0])
                wh = sbuf(ctx, f"{tag}wh", [P, 2, HID0], FR)
                wl = sbuf(ctx, f"{tag}wl", [P, 2, HID0], FR)
                act_sb = sbuf(ctx, f"{tag}act", [P, 2, 512])
                hid = sbuf(ctx, f"{tag}hid", [P, 2, HC0, 512])
                pg = banks(ctx, f"{tag}pg", 2)
                pu = banks(ctx, f"{tag}pu", 2)
                po = banks(ctx, f"{tag}po", 2)
                w_in, w_ok, up_ok, silu_ok, hid_ok, down_ok, x_ok = sems(
                    ctx, tag, "w_in", "w_ok", "up_ok", "silu_ok", "hid_ok", "down_ok", "x_ok")
                with nc.Block() as block:
                    @block.sync
                    def _(sp):
                        sp.dma_start(wi[:, 0, :], wg0).then_inc(w_in, 16)
                        sp.dma_start(wi[:, 1, :], wu0).then_inc(w_in, 16)
                        sp.dma_start(wi[:, 2, :].rearrange("p (c d) -> p c d", c=HC0),
                                     wd0.rearrange("(c p) d -> p c d", p=P)).then_inc(w_in, 16)
                        sp.wait_ge(w_in, 48)

                    @block.tensor
                    def _(pe):
                        pe.wait_ge(w_ok, 3)

                        def up(g, p):
                            for c in range(HC0):
                                b = (HC0 * p + c) % 2
                                cols = bass.ds(g * 512, 512)
                                if isinstance(g, int):
                                    if HC0 * g + c >= 2:
                                        pe.wait_ge(hid_ok, HC0 * g + c - 1)
                                else:
                                    pe.wait_ge(hid_ok, HC0 * g + c - 1)
                                w = slice(c * P, (c + 1) * P)
                                for i, bank in ((0, pg[b]), (1, pu[b])):
                                    nc.tensor.matmul(bank[:], wh[:, i, w], XTh[:, cols], start=True, stop=False)
                                    nc.tensor.matmul(bank[:], wl[:, i, w], XTh[:, cols], start=False, stop=False)
                                    nc.tensor.matmul(bank[:], wh[:, i, w], XTl[:, cols], start=False,
                                                     stop=True).then_inc(up_ok, 1)

                        def down(g, p):
                            pe.wait_ge(hid_ok, HC0 * g + HC0)
                            if not isinstance(g, int) or g >= 2:
                                pe.wait_ge(x_ok, g - 1)
                            for j in range(4):
                                for c in range(HC0):
                                    n = nc.tensor.matmul(po[p][:, j * P:(j + 1) * P], hid[:, p, c, j * P:(j + 1) * P],
                                                         wf[:, 2, c * P:(c + 1) * P], start=(c == 0), stop=(c == HC0 - 1))
                            n.then_inc(down_ok, 1)

                        up(0, 0)
                        up(1, 1)
                        down(0, 0)
                        up(2, 0)
                        down(1, 1)
                        with pe.Fori(1, GROUPS // 2 - 1) as m:
                            up(2 * m + 1, 1)
                            down(2 * m, 0)
                            up(2 * m + 2, 0)
                            down(2 * m + 1, 1)
                        up(GROUPS - 1, 1)
                        down(GROUPS - 2, 0)
                        down(GROUPS - 1, 1)

                    @block.scalar
                    def _(act):
                        def silu(g, p):
                            for c in range(HC0):
                                b = (HC0 * p + c) % 2
                                act.wait_ge(up_ok, 2 * (HC0 * g + c) + 1)
                                if not isinstance(g, int) or HC0 * g + c >= 2:
                                    act.wait_ge(hid_ok, HC0 * g + c - 1)
                                nc.scalar.activation(act_sb[:, b, :], pg[b][:], ACT.Silu).then_inc(silu_ok, 1)
                        silu(0, 0)
                        silu(1, 1)
                        with act.Fori(1, GROUPS // 2) as m:
                            silu(2 * m, 0)
                            silu(2 * m + 1, 1)

                    @block.vector
                    def _(dve):
                        dve.wait_ge(w_in, 48)
                        nc.vector.tensor_scalar(wf[:], wi[:], float(np.float32(1.0 / 127.0)), None, ALU.mult).then_inc(w_ok, 1)
                        dve.wait_ge(w_ok, 1)
                        nc.vector.tensor_copy(wh[:], wf[:, 0:2, :]).then_inc(w_ok, 1)
                        dve.wait_ge(w_ok, 2)
                        nc.vector.tensor_tensor(wl[:], wf[:, 0:2, :], wh[:].bitcast(F), ALU.subtract).then_inc(w_ok, 1)

                        def gated(g, p):
                            for c in range(HC0):
                                b = (HC0 * p + c) % 2
                                dve.wait_ge(silu_ok, HC0 * g + c + 1)
                                dve.wait_ge(up_ok, 2 * (HC0 * g + c) + 2)
                                if c == 0 and (not isinstance(g, int) or g >= 2):
                                    dve.wait_ge(down_ok, g - 1)
                                nc.vector.tensor_tensor(hid[:, p, c, :], act_sb[:, b, :], pu[b][:],
                                                        ALU.mult).then_inc(hid_ok, 1)

                        def add(g, p):
                            dve.wait_ge(down_ok, g + 1)
                            rows = x[:, bass.ds(g * 4, 4), :]
                            nc.vector.scalar_tensor_tensor(rows, po[p][:].rearrange("p (j c) -> p j c", j=4), 0.5, rows,
                                                           ALU.mult, ALU.add).then_inc(x_ok, 1)

                        gated(0, 0)
                        gated(1, 1)
                        add(0, 0)
                        with dve.Fori(1, GROUPS // 2) as m:
                            gated(2 * m, 0)
                            add(2 * m - 1, 1)
                            gated(2 * m + 1, 1)
                            add(2 * m, 0)
                        add(GROUPS - 1, 1)

        def attention(tag, d, scale, q_w, k_w, v_w, p_w, q_bias, v_bias, p_full, p_bias, relative, slope):
            STEPS = B * H
            with ExitStack() as ctx:
                Mh = sbuf(ctx, f"{tag}Mh", [P, H, C], FR)
                Ml = sbuf(ctx, f"{tag}Ml", [P, H, C], FR)
                Nh = sbuf(ctx, f"{tag}Nh", [P, H, C], FR)
                Nl = sbuf(ctx, f"{tag}Nl", [P, H, C], FR)
                gb = sbuf(ctx, f"{tag}gb", [P, H])
                bias = sbuf(ctx, f"{tag}bias", [P, H, S])

                with ExitStack() as pre:
                    wq_sb = sbuf(pre, f"{tag}wq", [d, H, C])
                    wk_sb = sbuf(pre, f"{tag}wk", [d, H, C])
                    wv_sb = sbuf(pre, f"{tag}wv", [d, H, C])
                    wp_sb = sbuf(pre, f"{tag}wp", [d, H, C])
                    row = sbuf(pre, f"{tag}row", [P, C])
                    rel = sbuf(pre, f"{tag}rel", [P, 33 * H if relative is not None else H])
                    dist = sbuf(pre, f"{tag}dist", [P, S])
                    pm = banks(pre, f"{tag}pm", 2)
                    pn = banks(pre, f"{tag}pn", 2)
                    pb = banks(pre, f"{tag}pb", 1)[0]
                    w_in, r_in, mat_ok, hi_ok, lo_ok, b_ok, sk_out, sk_in = sems(
                        pre, f"{tag}p", "w_in", "r_in", "mat_ok", "hi_ok", "lo_ok", "b_ok", "sk_out", "sk_in")
                    if v_bias is not None:
                        bq_sb = sbuf(pre, f"{tag}bq", [d, H])
                        bv_sb = sbuf(pre, f"{tag}bv", [P, 1])
                        bvx = sbuf(pre, f"{tag}bvx", [P, P])
                        pf_sb = sbuf(pre, f"{tag}pf", [P, C])
                    if relative is not None:
                        rows = sbuf(pre, f"{tag}rows", [P, H, BAND])
                    n_w = 4 + (3 if v_bias is not None else 0)
                    with nc.Block() as block:
                        @block.sync
                        def _(sp):
                            for dst, src in ((wq_sb, q_w), (wk_sb, k_w), (wv_sb, v_w), (wp_sb, p_w)):
                                sp.dma_start(dst[:], src).then_inc(w_in, 16)
                            if v_bias is not None:
                                sp.dma_start(bq_sb[:], q_bias).then_inc(w_in, 16)
                                sp.dma_start(bv_sb[:], v_bias).then_inc(w_in, 16)
                                sp.dma_start(pf_sb[:], p_full).then_inc(w_in, 16)
                            sp.dma_start(row[:], p_bias.broadcast_to([P, C])).then_inc(r_in, 16)
                            src = relative if relative is not None else slope
                            sp.dma_start(rel[:], src.broadcast_to([P, src.shape[1]])).then_inc(r_in, 16)
                            sp.wait_ge(r_in, 32)
                            sp.wait_ge(w_in, 16 * n_w)
                            if relative is not None:
                                sp.wait_ge(b_ok, 2)
                                sp.dma_start(skew.ap().rearrange("h p c -> p h c"), rows[:]).then_inc(sk_out, 16)
                                sp.wait_ge(sk_out, 16)
                                shifted = bass.AP(skew, 0, [[BAND - 1, P], [P * BAND, H], [1, BAND - 1]])
                                sp.dma_start(bias[:, :, S - BAND + 1:S], shifted).then_inc(sk_in, 16)
                                sp.wait_ge(sk_in, 16)

                        @block.tensor
                        def _(pe):
                            pe.wait_ge(w_in, 16 * n_w)
                            for h in range(H):
                                b = h % 2
                                if h >= 2:
                                    pe.wait_ge(lo_ok, 2 * (h - 1) + 1)
                                nc.tensor.matmul(pm[b][:, 0:C], wq_sb[:, h, :], wk_sb[:, h, :], start=True,
                                                 stop=True).then_inc(mat_ok, 1)
                                nc.tensor.matmul(pn[b][:, 0:C], wv_sb[:, h, :], wp_sb[:, h, :], start=True,
                                                 stop=True).then_inc(mat_ok, 1)
                            if v_bias is not None:
                                for h in range(H):
                                    nc.tensor.matmul(pb[:, C + h:C + h + 1], wk_sb[:, h, :], bq_sb[:, h:h + 1],
                                                     start=True, stop=True)
                                pe.wait_ge(b_ok, 3)
                                nc.tensor.matmul(pb[:, 0:C], bvx[:], pf_sb[:], start=True, stop=True).then_inc(mat_ok, 1)

                        @block.scalar
                        def _(act):
                            for h in range(H):
                                b = h % 2
                                act.wait_ge(mat_ok, 2 * h + 1)
                                nc.scalar.activation(Mh[:, h, :], pm[b][:, 0:C], ACT.Copy, scale=scale).then_inc(hi_ok, 1)
                                act.wait_ge(mat_ok, 2 * h + 2)
                                nc.scalar.activation(Nh[:, h, :], pn[b][:, 0:C], ACT.Copy).then_inc(hi_ok, 1)

                        @block.vector
                        def _(dve):
                            dve.wait_ge(r_in, 32)
                            if relative is not None:
                                tab = rel[:].rearrange("p (j h) -> p h j", h=H)
                                nc.vector.tensor_copy(rows[:], tab[:, :, 0:1].broadcast_to([P, H, BAND])).then_inc(b_ok, 1)
                                nc.vector.tensor_copy(bias[:, :, 0:S - BAND + 1],
                                                      tab[:, :, 0:1].broadcast_to([P, H, S - BAND + 1])).then_inc(lo_ok, 1)
                                dve.wait_ge(b_ok, 1)
                                nc.vector.tensor_copy(rows[:, :, P - 16 + 1:P + 1], tab[:, :, 1:17]).then_inc(b_ok, 1)
                            else:
                                dve.wait_ge(b_ok, 1)
                                for h in range(H):
                                    nb = nc.vector.tensor_scalar(bias[:, h, :], dist[:], rel[:, h:h + 1], None, ALU.mult)
                                nb.then_inc(b_ok, 1)
                                dve.wait_ge(w_in, 16 * n_w)
                                nc.vector.tensor_copy(bvx[:], bv_sb[:].broadcast_to([P, P])).then_inc(b_ok, 1)
                                nc.vector.tensor_scalar(gb[:, 0:1], row[:, 0:1], 0.0, None, ALU.mult).then_inc(lo_ok, 1)
                            for h in range(H):
                                b = h % 2
                                dve.wait_ge(hi_ok, 2 * h + 1)
                                nc.vector.scalar_tensor_tensor(Ml[:, h, :], pm[b][:, 0:C], scale, Mh[:, h, :].bitcast(F),
                                                               ALU.mult, ALU.subtract).then_inc(lo_ok, 1)
                                dve.wait_ge(hi_ok, 2 * h + 2)
                                nc.vector.tensor_tensor(Nl[:, h, :], pn[b][:, 0:C], Nh[:, h, :].bitcast(F),
                                                        ALU.subtract).then_inc(lo_ok, 1)
                            if v_bias is not None:
                                dve.wait_ge(lo_ok, 1)
                                dve.wait_ge(mat_ok, 2 * H + 1)
                                nc.vector.tensor_scalar(gb[:], pb[:, C:C + H], scale, None, ALU.mult).then_inc(lo_ok, 1)
                                nc.vector.tensor_tensor(row[:], row[:], pb[:, 0:C], ALU.add).then_inc(lo_ok, 1)
                            else:
                                nc.vector.memset(gb[:], 0.0).then_inc(lo_ok, 1)
                                nc.vector.tensor_scalar(row[:], row[:], 1.0, None, ALU.mult).then_inc(lo_ok, 1)
                            dve.wait_ge(lo_ok, 2 * H + 3)
                            nc.vector.tensor_tensor(x[:], x[:], row[:].unsqueeze(1).broadcast_to([P, TILES, C]),
                                                    ALU.add).then_inc(lo_ok, 1)

                        @block.gpsimd
                        def _(pool):
                            if relative is None:
                                nc.gpsimd.iota(dist[:], [[1, S]], base=-(S - P), channel_multiplier=-1,
                                               allow_small_or_imprecise_dtypes=True).then_inc(b_ok, 1)
                                pool.wait_ge(b_ok, 2)
                            else:
                                pool.wait_ge(sk_in, 16)
                            nc.gpsimd.affine_select(out=bias[:, :, S - P:S], in_=bias[:, :, S - P:S], compare_op=ALU.is_ge,
                                                    fill=NEG, base=0, pattern=[[0, H], [-1, P]],
                                                    channel_multiplier=1).then_inc(b_ok, 1)

                Mc = [sbuf(ctx, f"{tag}Mc{i}", [P, 2, C], FR) for i in range(2)]
                XTc = sbuf(ctx, f"{tag}XTc", [P, 2, S], FR)
                Gh = sbuf(ctx, f"{tag}Gh", [P, S], FR)
                Gl = sbuf(ctx, f"{tag}Gl", [P, S], FR)
                bc = [sbuf(ctx, f"{tag}bc{i}", [P, S]) for i in range(2)]
                prob = [sbuf(ctx, f"{tag}prob{i}", [P, WIDTH]) for i in range(2)]
                negmax = [sbuf(ctx, f"{tag}nm{i}", [P, QT]) for i in range(2)]
                total = [sbuf(ctx, f"{tag}tot{i}", [P, QT]) for i in range(2)]
                inv = [sbuf(ctx, f"{tag}inv{i}", [P, QT]) for i in range(2)]
                V = [sbuf(ctx, f"{tag}V{i}", [P, QT, 2, C]) for i in range(2)]
                PT = sbuf(ctx, f"{tag}PT", [P, WIDTH])
                tick = sbuf(ctx, f"{tag}tick", [1, 4])
                ps = banks(ctx, f"{tag}ps", 3)
                pt = banks(ctx, f"{tag}pt", 2)
                pg, pv, py = banks(ctx, f"{tag}pg", 3)
                names = ("bc_ok", "m_ok", "xt_ok", "g_ok", "gh_ok", "gl_ok", "s_ok", "max_ok", "exp_ok", "v_ok", "vc_ok",
                         "t_ok", "tc_ok", "y_ok", "inv_ok", "x_ok")
                (bc_ok, m_ok, xt_ok, g_ok, gh_ok, gl_ok, s_ok, max_ok, exp_ok, v_ok, vc_ok,
                 t_ok, tc_ok, y_ok, inv_ok, x_ok) = sems(ctx, tag, *names)
                bank_of = {3: (ps[0], 0), 2: (ps[1], 0), 0: (ps[1], 384), 1: (ps[2], 0)}

                def first(n, k=1):
                    return isinstance(n, int) and n < k

                with nc.Block() as block:
                    @block.gpsimd
                    def _(pool):
                        def copy(dst, src):
                            return nc.gpsimd.tensor_tensor(dst, src, one[:].broadcast_to([P, dst.shape[-1]]), ALU.mult)

                        def matrix(n, p):
                            if not first(n, 2):
                                pool.wait_ge(g_ok, n - 1)
                            for i, m in enumerate((Mh, Ml)):
                                c = copy(Mc[p][:, i, :], m[:, bass.ds(n % H, 1), :].squeeze(1).bitcast(F))
                            c.then_inc(m_ok, 1)

                        def batch(b):
                            if not first(b):
                                pool.wait_ge(v_ok, b * H)
                            copy(XTc[:, 0, :], XTh[:, bass.ds(b * S, S)].bitcast(F))
                            copy(XTc[:, 1, :], XTl[:, bass.ds(b * S, S)].bitcast(F)).then_inc(xt_ok, 1)

                        def step(n, p, last=False):
                            if not last:
                                matrix(n + 1, 1 - p)
                            if not first(n, 2):
                                pool.wait_ge(max_ok, 4 * n - 4)
                            copy(bc[p][:], bias[:, bass.ds(n % H, 1), :].squeeze(1)).then_inc(bc_ok, 1)

                        def rest(b, to):
                            with pool.Fori(1, to) as k:
                                step(b * H + 2 * k, 0)
                                step(b * H + 2 * k + 1, 1)

                        matrix(0, 0)
                        batch(0)
                        step(0, 0)
                        step(1, 1)
                        rest(0, H // 2)
                        with pool.Fori(1, B - 1) as b:
                            batch(b)
                            step(b * H, 0)
                            step(b * H + 1, 1)
                            rest(b, H // 2)
                        b = B - 1
                        batch(b)
                        step(b * H, 0)
                        step(b * H + 1, 1)
                        rest(b, H // 2 - 1)
                        step(STEPS - 2, 0)
                        step(STEPS - 1, 1, last=True)

                    @block.tensor
                    def _(pe):
                        def queries(n, p):
                            pe.wait_ge(m_ok, n + 1)
                            if not first(n):
                                pe.wait_ge(gl_ok, n)
                            cols = bass.ds((n // H) * S, S)
                            nc.tensor.matmul(pg[:], Mc[p][:, 0, :], XTh[:, cols], start=True, stop=False)
                            nc.tensor.matmul(pg[:], Mc[p][:, 1, :], XTh[:, cols], start=False, stop=False)
                            nc.tensor.matmul(pg[:], Mc[p][:, 0, :], XTl[:, cols], start=False, stop=True).then_inc(g_ok, 1)

                        def scores(n):
                            pe.wait_ge(gl_ok, n + 1)
                            for i in ORDER:
                                if not first(n) and i != 0:
                                    pe.wait_ge(max_ok, 4 * n - {3: 3, 2: 1, 1: 0}[i])
                                bank, at = bank_of[i]
                                q, w = slice(i * P, (i + 1) * P), (i + 1) * P
                                cols = bass.ds((n // H) * S, w)
                                o = bank[:, at:at + w]
                                nc.tensor.matmul(o, Gh[:, q], XTh[:, cols], start=True, stop=False)
                                nc.tensor.matmul(o, Gl[:, q], XTh[:, cols], start=False, stop=False)
                                s = nc.tensor.matmul(o, Gh[:, q], XTl[:, cols], start=False, stop=True)
                                if i != 2:
                                    s.then_inc(s_ok, 1)

                        def values(k, half):
                            pe.wait_ge(xt_ok, k // H + 1)
                            if not first(k):
                                pe.wait_ge(vc_ok, k)
                            h = bass.ds((k // 2 * 2) % H, 2)
                            for j in (2 * half, 2 * half + 1):
                                t = slice(j * P, (j + 1) * P)
                                o = pv[:, (j % 2) * 2 * C:(j % 2 + 1) * 2 * C]
                                nc.tensor.matmul(o, XTc[:, 0, t], Nh[:, h, :], start=True, stop=False)
                                nc.tensor.matmul(o, XTc[:, 1, t], Nh[:, h, :], start=False, stop=False)
                                v = nc.tensor.matmul(o, XTc[:, 0, t], Nl[:, h, :], start=False, stop=True)
                            v.then_inc(v_ok, 1)

                        def turn(n, p, k):
                            pe.wait_ge(exp_ok, 4 * n + (1, 3, 4)[k])
                            if k == 2 or not first(n):
                                pe.wait_ge(tc_ok, 3 * n + (0, 0, 1)[k])
                            o = 0
                            for i in TGROUPS[k]:
                                for j in range(i + 1):
                                    t = nc.tensor.transpose(pt[k % 2][:, o:o + P],
                                                            prob[p][:, START[i] + j * P:START[i] + (j + 1) * P], ident[:])
                                    o += P
                            t.then_inc(t_ok, 1)

                        def mix(n, p, vp, k):
                            if k == 0:
                                pe.wait_ge(vc_ok, n // 2 * 2 + 2)
                                if not first(n):
                                    pe.wait_ge(x_ok, n)
                            pe.wait_ge(tc_ok, 3 * n + k + 1)
                            for i in TGROUPS[k]:
                                o = py[:, i * C:(i + 1) * C]
                                for j in range(i + 1):
                                    b = slice(START[i] + j * P, START[i] + (j + 1) * P)
                                    y = nc.tensor.matmul(o, PT[:, b], V[vp][:, j, p, :], start=(j == 0), stop=(j == i))
                            if k == 2:
                                y.then_inc(y_ok, 1)

                        def step(n, r, last=False):
                            p, q, vp = r % 2, (r - 1) % 2, (r - 1) % 4 // 2
                            scores(n)
                            turn(n - 1, q, 0)
                            turn(n - 1, q, 1)
                            if not last:
                                queries(n + 1, 1 - p)
                            mix(n - 1, q, vp, 0)
                            turn(n - 1, q, 2)
                            if not last:
                                values(n + 1, 1 - p)
                            mix(n - 1, q, vp, 1)
                            mix(n - 1, q, vp, 2)

                        queries(0, 0)
                        scores(0)
                        queries(1, 1)
                        values(0, 0)
                        values(1, 1)
                        for n in range(1, 4):
                            step(n, n)
                        with pe.Fori(1, STEPS // 4 - 1) as m:
                            for r in range(4):
                                step(4 * m + r, r)
                        for r in range(4):
                            step(STEPS - 4 + r, r, last=(r == 3))
                        n = STEPS - 1
                        turn(n, 1, 0)
                        turn(n, 1, 1)
                        mix(n, 1, 1, 0)
                        turn(n, 1, 2)
                        mix(n, 1, 1, 1)
                        mix(n, 1, 1, 2)

                    @block.scalar
                    def _(act):
                        def query_hi(n):
                            act.wait_ge(g_ok, n + 1)
                            nc.scalar.activation(Gh[:], pg[:], ACT.Identity, bias=gb[:, bass.ds(n % H, 1)]).then_inc(gh_ok, 1)

                        def values(k, vp, half):
                            act.wait_ge(v_ok, k + 1)
                            nc.scalar.activation(V[vp][:, 2 * half:2 * half + 2, :, :].rearrange("p j h c -> p (j h c)"),
                                                 pv[:], ACT.Copy).then_inc(vc_ok, 1)

                        def exponentials(n, p, tiles):
                            for i in tiles:
                                act.wait_ge(max_ok, 4 * n + ORDER.index(i) + 1)
                                if i == 3 and not first(n, 2):
                                    act.wait_ge(inv_ok, n - 1)
                                s = prob[p][:, START[i]:START[i] + (i + 1) * P]
                                nc.scalar.activation(s, s, ACT.Exp, bias=negmax[p][:, i:i + 1], scale=-1.0,
                                                     accum_out=total[p][:, i:i + 1]).then_inc(exp_ok, 1)

                        def turned(n, k):
                            act.wait_ge(t_ok, 3 * n + k + 1)
                            w = sum(i + 1 for i in TGROUPS[k]) * P
                            o = START[TGROUPS[k][0]]
                            nc.scalar.activation(PT[:, o:o + w], pt[k % 2][:, 0:w], ACT.Copy).then_inc(tc_ok, 1)

                        def step(n, r, last=False):
                            p = r % 2
                            exponentials(n, p, (3,))
                            turned(n - 1, 0)
                            turned(n - 1, 1)
                            exponentials(n, p, (2,))
                            if not last:
                                query_hi(n + 1)
                            exponentials(n, p, (0, 1))
                            turned(n - 1, 2)
                            if not last:
                                values(n + 1, (r + 1) % 4 // 2, 1 - p)

                        query_hi(0)
                        query_hi(1)
                        exponentials(0, 0, (3, 2))
                        values(0, 0, 0)
                        values(1, 0, 1)
                        exponentials(0, 0, (0, 1))
                        for n in range(1, 4):
                            step(n, n)
                        with act.Fori(1, STEPS // 4 - 1) as m:
                            for r in range(4):
                                step(4 * m + r, r)
                        for r in range(4):
                            step(STEPS - 4 + r, r, last=(r == 3))
                        for k in range(3):
                            turned(STEPS - 1, k)

                    @block.vector
                    def _(dve):
                        def query_lo(n):
                            dve.wait_ge(gh_ok, n + 1)
                            nc.vector.scalar_tensor_tensor(Gl[:], pg[:], gb[:, bass.ds(n % H, 1)], Gh[:].bitcast(F),
                                                           ALU.add, ALU.subtract).then_inc(gl_ok, 1)

                        def maxima(n, p, tiles=ORDER):
                            if tiles[0] == 3:
                                dve.wait_ge(bc_ok, n + 1)
                            for i in tiles:
                                bank, at = bank_of[i]
                                w = (i + 1) * P
                                if i != 0:
                                    dve.wait_ge(s_ok, 3 * n + {3: 1, 2: 2, 1: 3}[i])
                                    nc.vector.memset(tick[:, i:i + 1], 0.0)
                                nc.vector.tensor_tensor_reduce(
                                    out=prob[p][:, START[i]:START[i] + w], in0=bank[:, at:at + w],
                                    in1=bc[p][:, S - w:S], scale=-1.0, scalar=3e38,
                                    op0=ALU.add, op1=ALU.min, accum_out=negmax[p][:, i:i + 1]).then_inc(max_ok, 1)

                        def inverse(n, p):
                            dve.wait_ge(exp_ok, 4 * n + 4)
                            nc.vector.reciprocal(inv[p][:], total[p][:]).then_inc(inv_ok, 1)

                        def add(n, p):
                            dve.wait_ge(inv_ok, n + 1)
                            dve.wait_ge(y_ok, n + 1)
                            for i in range(QT):
                                r = x[:, bass.ds((n // H) * QT + i, 1), :]
                                a = nc.vector.scalar_tensor_tensor(r, py[:, i * C:(i + 1) * C], inv[p][:, i:i + 1], r,
                                                                   ALU.mult, ALU.add)
                            a.then_inc(x_ok, 1)

                        def step(n, p, last=False):
                            maxima(n, p, ORDER[:1])
                            if not first(n, 2):
                                add(n - 2, p)
                            maxima(n, p, ORDER[1:])
                            inverse(n - 1, 1 - p)
                            if not last:
                                query_lo(n + 1)

                        query_lo(0)
                        maxima(0, 0)
                        query_lo(1)
                        step(1, 1)
                        with dve.Fori(1, STEPS // 2 - 1) as m:
                            step(2 * m, 0)
                            step(2 * m + 1, 1)
                        step(STEPS - 2, 0)
                        step(STEPS - 1, 1, last=True)
                        add(STEPS - 2, 0)
                        inverse(STEPS - 1, 1)
                        add(STEPS - 1, 1)

        def moe(tag):
            with ExitStack() as ctx:
                idx = sbuf(ctx, f"{tag}idx", [P, TOPK, TILES], I32)
                wts = sbuf(ctx, f"{tag}wts", [P, TOPK, TILES])
                with ExitStack() as pre:
                    xn = sbuf(pre, f"{tag}rows", [P, TILES, C])
                    layernorm(f"{tag}n", keep=xn)
                    route(tag, pre, idx, wts)
                    dispatch(tag, idx, xn)
                experts(tag)
                combine(tag, idx, wts)

        def route(tag, ctx, idx, wts):
            wg = sbuf(ctx, f"{tag}wg", [P, P])
            wgh = sbuf(ctx, f"{tag}wgh", [P, P], FR)
            wgl = sbuf(ctx, f"{tag}wgl", [P, P], FR)
            bg = sbuf(ctx, f"{tag}bg", [P, E])
            lgT = sbuf(ctx, f"{tag}lgT", [P, 2, 512])
            shape = [P, TILES, E]
            LG, L2, EQ, OH1, OH2, LAB, SEQ, POS, TMP = (
                sbuf(ctx, f"{tag}{n}", shape) for n in ("LG", "L2", "EQ", "OH1", "OH2", "LAB", "SEQ", "POS", "TMP"))
            INC = sbuf(ctx, f"{tag}INC", shape)
            rank = sbuf(ctx, f"{tag}rank", [P, E])
            base = sbuf(ctx, f"{tag}base", [P, E])
            dump = sbuf(ctx, f"{tag}dump", [P, 1])
            upto = sbuf(ctx, f"{tag}upto", [P, P])
            ones = sbuf(ctx, f"{tag}ones", [P, P])
            m1, m2, r1, ex, s1 = (sbuf(ctx, f"{tag}{n}", [P, TILES]) for n in ("m1", "m2", "r1", "ex", "s1"))
            lt = banks(ctx, f"{tag}lt", 2)
            tl = banks(ctx, f"{tag}tl", 2)
            pc = banks(ctx, f"{tag}pc", 1)[0]
            w_in, made, w_ok, l_ok, lc_ok, t_ok, lg_ok, lab_ok, cum_ok, d_ok, e_ok, chain = sems(
                ctx, f"{tag}r", "w_in", "made", "w_ok", "l_ok", "lc_ok", "t_ok", "lg_ok", "lab_ok", "cum_ok", "d_ok",
                "e_ok", "chain")
            with nc.Block() as block:
                @block.sync
                def _(sp):
                    sp.wait_ge(made, 1)
                    sp.dma_start(wg[:, 0:E], wgate).then_inc(w_in, 16)
                    sp.dma_start(bg[:], bgate.broadcast_to([P, E])).then_inc(w_in, 16)
                    sp.wait_ge(w_in, 32)

                @block.gpsimd
                def _(pool):
                    nc.gpsimd.memset(wg[:], 0.0).then_inc(made, 1)
                    nc.gpsimd.memset(ones[:], 1.0).then_inc(made, 1)
                    nc.gpsimd.iota(rank[:], [[-1, E]], base=E, channel_multiplier=0,
                                   allow_small_or_imprecise_dtypes=True).then_inc(made, 1)
                    nc.gpsimd.iota(base[:], [[CAP, E]], base=-1, channel_multiplier=0,
                                   allow_small_or_imprecise_dtypes=True).then_inc(made, 1)
                    nc.gpsimd.iota(dump[:], [[0, 1]], base=SLOTS, channel_multiplier=1,
                                   allow_small_or_imprecise_dtypes=True).then_inc(made, 1)
                    pool.wait_ge(made, 2)
                    nc.gpsimd.affine_select(out=upto[:], in_=ones[:], compare_op=ALU.is_ge, fill=0.0, base=0,
                                            pattern=[[1, P]], channel_multiplier=-1).then_inc(made, 1)
                    pool.wait_ge(made, 6)

                @block.tensor
                def _(pe):
                    pe.wait_ge(w_ok, 2)

                    def logits(g, b):
                        if not isinstance(g, int) or g >= 2:
                            pe.wait_ge(lc_ok, g - 1)
                        cols = bass.ds(g * 512, 512)
                        nc.tensor.matmul(lt[b][:], wgh[:], XTh[:, cols], start=True, stop=False)
                        nc.tensor.matmul(lt[b][:], wgl[:], XTh[:, cols], start=False, stop=False)
                        nc.tensor.matmul(lt[b][:], wgh[:], XTl[:, cols], start=False, stop=True).then_inc(l_ok, 1)

                    def turn(g, b):
                        pe.wait_ge(lc_ok, g + 1)
                        if not isinstance(g, int) or g >= 2:
                            pe.wait_ge(lg_ok, g - 1)
                        for j in range(4):
                            t = nc.tensor.transpose(tl[b][:, j * P:(j + 1) * P], lgT[:, b, j * P:(j + 1) * P], ident[:])
                        t.then_inc(t_ok, 1)

                    logits(0, 0)
                    logits(1, 1)
                    turn(0, 0)
                    turn(1, 1)
                    with pe.Fori(1, GROUPS // 2) as m:
                        logits(2 * m, 0)
                        logits(2 * m + 1, 1)
                        turn(2 * m, 0)
                        turn(2 * m + 1, 1)
                    pe.wait_ge(lab_ok, 1)
                    pe.wait_ge(made, 6)
                    lab = LAB[:].rearrange("p t e -> p (t e)")
                    nc.tensor.matmul(pc[:, 0:256], upto[:], lab, start=True, stop=True)
                    nc.tensor.matmul(pc[:, 256:512], ones[:], lab, start=True, stop=True).then_inc(cum_ok, 1)

                @block.scalar
                def _(act):
                    with act.Fori(0, GROUPS // 2) as m:
                        for b in range(2):
                            act.wait_ge(l_ok, 2 * m + b + 1)
                            nc.scalar.activation(lgT[:, b, :], lt[b][:], ACT.Copy).then_inc(lc_ok, 1)
                    act.wait_ge(d_ok, 1)
                    nc.scalar.activation(ex[:], s1[:], ACT.Exp).then_inc(e_ok, 1)

                @block.vector
                def _(dve):
                    dve.wait_ge(w_in, 32)
                    nc.vector.tensor_copy(wgh[:], wg[:]).then_inc(w_ok, 1)
                    dve.wait_ge(w_ok, 1)
                    nc.vector.tensor_tensor(wgl[:], wg[:], wgh[:].bitcast(F), ALU.subtract).then_inc(w_ok, 1)
                    with dve.Fori(0, GROUPS // 2) as m:
                        for b in range(2):
                            dve.wait_ge(t_ok, 2 * m + b + 1)
                            nc.vector.tensor_tensor(LG[:, bass.ds(8 * m + 4 * b, 4), :],
                                                    tl[b][:].rearrange("p (j e) -> p j e", j=4)[:, :, 0:E],
                                                    bg[:].unsqueeze(1).broadcast_to([P, 4, E]), ALU.add).then_inc(lg_ok, 1)
                    dve.wait_ge(lg_ok, GROUPS)
                    dve.wait_ge(made, 6)
                    done = [0]

                    def link(ins):
                        done[0] += 1
                        ins.then_inc(chain, 1)
                        dve.wait_ge(chain, done[0])

                    def wide(v):
                        return v[:].unsqueeze(2).broadcast_to(shape)

                    def each(v):
                        return v[:].unsqueeze(1).broadcast_to(shape)

                    def best(L, m, OH):
                        link(nc.vector.tensor_reduce(m[:], L[:], AX.X, ALU.max))
                        link(nc.vector.tensor_tensor(EQ[:], L[:], wide(m), ALU.is_equal))
                        link(nc.vector.tensor_tensor(EQ[:], EQ[:], each(rank), ALU.mult))
                        link(nc.vector.tensor_reduce(r1[:], EQ[:], AX.X, ALU.max))
                        link(nc.vector.tensor_tensor(OH[:], EQ[:], wide(r1), ALU.is_equal))

                    best(LG, m1, OH1)
                    link(nc.vector.scalar_tensor_tensor(L2[:], OH1[:], -3e38, LG[:], ALU.mult, ALU.add))
                    best(L2, m2, OH2)
                    nc.vector.tensor_tensor(LAB[:], OH1[:], OH2[:], ALU.add).then_inc(lab_ok, 1)
                    nc.vector.tensor_tensor(s1[:], m2[:], m1[:], ALU.subtract).then_inc(d_ok, 1)
                    dve.wait_ge(e_ok, 1)
                    link(nc.vector.tensor_scalar(s1[:], ex[:], 1.0, None, ALU.add))
                    link(nc.vector.reciprocal(r1[:], s1[:]))
                    link(nc.vector.tensor_scalar(wts[:, 0, :], r1[:], 0.5, None, ALU.mult))
                    link(nc.vector.tensor_tensor(wts[:, 1, :], wts[:, 0, :], ex[:], ALU.mult))
                    dve.wait_ge(cum_ok, 1)
                    cum = pc[:, 0:256].rearrange("p (t e) -> p t e", e=E)
                    tot = pc[:, 256:512].rearrange("p (t e) -> p t e", e=E)
                    for e in range(E):
                        s = nc.vector.tensor_tensor_scan(INC[:, :, e], one[:].broadcast_to([P, TILES]), tot[:, :, e],
                                                         0.0, ALU.mult, ALU.add)
                    link(s)
                    link(nc.vector.tensor_tensor(SEQ[:], INC[:], cum, ALU.add))
                    link(nc.vector.tensor_tensor(SEQ[:], SEQ[:], tot, ALU.subtract))
                    link(nc.vector.tensor_tensor(POS[:], SEQ[:], each(base), ALU.add))
                    link(nc.vector.tensor_scalar(POS[:], POS[:], dump[:], None, ALU.subtract))
                    link(nc.vector.scalar_tensor_tensor(POS[:], SEQ[:], float(CAP), POS[:], ALU.is_le, ALU.mult))
                    link(nc.vector.tensor_scalar(POS[:], POS[:], dump[:], None, ALU.add))
                    for k, OH in ((0, OH1), (1, OH2)):
                        link(nc.vector.tensor_tensor(TMP[:], OH[:], POS[:], ALU.mult))
                        link(nc.vector.tensor_reduce(r1[:], TMP[:], AX.X, ALU.add))
                        link(nc.vector.tensor_copy(idx[:, k, :], r1[:]))

        def dispatch(tag, idx, xn):
            with ExitStack() as ctx:
                (sent,) = sems(ctx, f"{tag}d", "sent")
                with nc.Block() as block:
                    @block.gpsimd
                    def _(pool):
                        for t in range(TILES):
                            for k in range(TOPK):
                                nc.gpsimd.indirect_dma_start(
                                    slots_in, bass.IndirectOffsetOnAxis(ap=idx[:, k, t:t + 1], axis=0), xn[:, t, :], None,
                                    bounds_check=SLOTS - 1, oob_is_err=False).then_inc(sent, 16)
                        pool.wait_ge(sent, 16 * TILES * TOPK)

        def experts(tag):
            HALF = CAP // 2
            with ExitStack() as ctx:
                rows = [sbuf(ctx, f"{tag}in{i}", [P, ST, C]) for i in range(2)]
                DT = [sbuf(ctx, f"{tag}DT{i}", [P, CAP]) for i in range(2)]
                w1 = [sbuf(ctx, f"{tag}w1{i}", [P, HID1]) for i in range(2)]
                w2 = [sbuf(ctx, f"{tag}w2{i}", [P, HID1]) for i in range(2)]
                w3 = [sbuf(ctx, f"{tag}w3{i}", [P, HC1, C]) for i in range(2)]
                gate = sbuf(ctx, f"{tag}gate", [P, 2, HALF])
                hid = sbuf(ctx, f"{tag}hid", [P, HC1, CAP])
                res = [sbuf(ctx, f"{tag}res{i}", [P, ST, C]) for i in range(2)]
                pg = banks(ctx, f"{tag}pg", 2)
                pu = banks(ctx, f"{tag}pu", 2)
                pt = ctx.enter_context(nc.psum_tensor(f"{tag}pt", [P, 1024], F))
                po = ctx.enter_context(nc.psum_tensor(f"{tag}po", [P, 1024], F))
                t_ok, dt_ok, up_ok, silu_ok, hid_ok, down_ok, res_ok, *dmas = sems(
                    ctx, f"{tag}e", "t_ok", "dt_ok", "up_ok", "silu_ok", "hid_ok", "down_ok", "res_ok",
                    "w_in0", "w_in1", "row_in0", "row_in1", "stored0", "stored1")
                w_in, row_in, stored = dmas[0:2], dmas[2:4], dmas[4:6]

                def late(e, k):
                    return not isinstance(e, int) or e >= k

                def slots(buf, e):
                    return buf[bass.ds(e * CAP, CAP), :].rearrange("(j p) c -> p j c", p=P)

                with nc.Block() as block:
                    @block.sync
                    def _(sp):
                        def load(e, p):
                            if late(e, 2):
                                sp.wait_ge(t_ok, e - 1)
                            sp.dma_start(rows[p][:], slots(slots_in, e)).then_inc(row_in[p], 16)
                            if late(e, 2):
                                sp.wait_ge(down_ok, e - 1)
                            sp.dma_start(w1[p][:], W1[bass.ds(e, 1)].squeeze(0)).then_inc(w_in[p], 16)
                            sp.dma_start(w2[p][:], W2[bass.ds(e, 1)].squeeze(0)).then_inc(w_in[p], 16)
                            sp.dma_start(w3[p][:], W3[bass.ds(e, 1)].squeeze(0).rearrange(
                                "(c p) d -> p c d", p=P)).then_inc(w_in[p], 16)

                        load(0, 0)
                        load(1, 1)
                        with sp.Fori(1, E // 2) as m:
                            load(2 * m, 0)
                            load(2 * m + 1, 1)
                        for p in range(2):
                            sp.wait_ge(row_in[p], 16 * (E // 2))
                            sp.wait_ge(w_in[p], 48 * (E // 2))

                    @block.tensor
                    def _(pe):
                        def turn(e, p, m):
                            pe.wait_ge(row_in[p], 16 * m + 16)
                            if late(e, 1):
                                pe.wait_ge(dt_ok, e)
                            for j in range(ST):
                                t = nc.tensor.transpose(pt[:, j * P:(j + 1) * P], rows[p][:, j, :], ident[:])
                            t.then_inc(t_ok, 1)

                        def up(e, p, m):
                            pe.wait_ge(w_in[p], 48 * m + 48)
                            pe.wait_ge(dt_ok, e + 1)
                            for u in range(2 * HC1):
                                c, s = u // 2, slice(u % 2 * HALF, (u % 2 + 1) * HALF)
                                if late(e, 1) or u >= 2:
                                    pe.wait_ge(hid_ok, 2 * HC1 * e + u - 1)
                                w = slice(c * P, (c + 1) * P)
                                nc.tensor.matmul(pg[u % 2][:, 0:HALF], w1[p][:, w], DT[p][:, s], start=True,
                                                 stop=True).then_inc(up_ok, 1)
                                nc.tensor.matmul(pu[u % 2][:, 0:HALF], w2[p][:, w], DT[p][:, s], start=True,
                                                 stop=True).then_inc(up_ok, 1)

                        def down(e, p):
                            pe.wait_ge(hid_ok, 2 * HC1 * (e + 1))
                            if late(e, 1):
                                pe.wait_ge(res_ok, e)
                            for j in range(ST):
                                for c in range(HC1):
                                    d = nc.tensor.matmul(po[:, j * P:(j + 1) * P], hid[:, c, j * P:(j + 1) * P],
                                                         w3[p][:, c, :], start=(c == 0), stop=(c == HC1 - 1))
                            d.then_inc(down_ok, 1)

                        def pair(m):
                            for p in range(2):
                                up(2 * m + p, p, m)
                                turn(2 * m + p + 1, 1 - p, m + p)
                                down(2 * m + p, p)

                        turn(0, 0, 0)
                        pair(0)
                        with pe.Fori(1, E // 2 - 1) as m:
                            pair(m)
                        m = E // 2 - 1
                        up(E - 2, 0, m)
                        turn(E - 1, 1, m)
                        down(E - 2, 0)
                        up(E - 1, 1, m)
                        down(E - 1, 1)

                    @block.scalar
                    def _(act):
                        def turned(e, p):
                            act.wait_ge(t_ok, e + 1)
                            nc.scalar.activation(DT[p][:], pt[:, 0:CAP], ACT.Copy).then_inc(dt_ok, 1)

                        def silu(e):
                            for u in range(2 * HC1):
                                act.wait_ge(up_ok, 2 * (2 * HC1 * e + u) + 1)
                                if late(e, 1) or u >= 2:
                                    act.wait_ge(hid_ok, 2 * HC1 * e + u - 1)
                                nc.scalar.activation(gate[:, u % 2, :], pg[u % 2][:, 0:HALF], ACT.Silu).then_inc(silu_ok, 1)

                        def result(e, p, m):
                            act.wait_ge(down_ok, e + 1)
                            if late(e, 2):
                                act.wait_ge(stored[p], 16 * m)
                            nc.scalar.activation(res[p][:].rearrange("p j c -> p (j c)"), po[:, 0:CAP],
                                                 ACT.Copy).then_inc(res_ok, 1)
                            act.wait_ge(res_ok, e + 1)
                            act.dma_start(slots(slots_out, e), res[p][:]).then_inc(stored[p], 16)

                        turned(0, 0)
                        silu(0)
                        turned(1, 1)
                        result(0, 0, 0)
                        silu(1)
                        turned(2, 0)
                        result(1, 1, 0)
                        with act.Fori(1, E // 2 - 1) as m:
                            for p in range(2):
                                silu(2 * m + p)
                                turned(2 * m + p + 1, 1 - p)
                                result(2 * m + p, p, m)
                        m = E // 2 - 1
                        silu(E - 2)
                        turned(E - 1, 1)
                        result(E - 2, 0, m)
                        silu(E - 1)
                        result(E - 1, 1, m)
                        for p in range(2):
                            act.wait_ge(stored[p], 16 * (E // 2))

                    @block.vector
                    def _(dve):
                        def gated(e):
                            for u in range(2 * HC1):
                                c, s = u // 2, slice(u % 2 * HALF, (u % 2 + 1) * HALF)
                                dve.wait_ge(silu_ok, 2 * HC1 * e + u + 1)
                                dve.wait_ge(up_ok, 2 * (2 * HC1 * e + u) + 2)
                                nc.vector.tensor_tensor(hid[:, c, s], gate[:, u % 2, :], pu[u % 2][:, 0:HALF],
                                                        ALU.mult).then_inc(hid_ok, 1)
                        with dve.Fori(0, E) as e:
                            gated(e)

        def combine(tag, idx, wts):
            PART = 4
            with ExitStack() as ctx:
                got = sbuf(ctx, f"{tag}got", [P, TILES * TOPK, C])
                added, *arrived = sems(ctx, f"{tag}c", "added", *[f"arrived{i}" for i in range(TILES // PART)])
                with nc.Block() as block:
                    @block.gpsimd
                    def _(pool):
                        for t in range(TILES):
                            for k in range(TOPK):
                                n = t * TOPK + k
                                nc.gpsimd.indirect_dma_start(
                                    got[:, n, :], None, slots_out,
                                    bass.IndirectOffsetOnAxis(ap=idx[:, k, t:t + 1], axis=0)).then_inc(arrived[t // PART], 16)

                    @block.vector
                    def _(dve):
                        for t in range(TILES):
                            dve.wait_ge(arrived[t // PART], 16 * TOPK * PART)
                            for k in range(TOPK):
                                if k:
                                    dve.wait_ge(added, t * TOPK + k)
                                nc.vector.scalar_tensor_tensor(x[:, t, :], got[:, t * TOPK + k, :], wts[:, k, t:t + 1],
                                                               x[:, t, :], ALU.mult, ALU.add).then_inc(added, 1)


        layernorm("n1")
        ffn0("f1")
        layernorm("n2")
        attention("a0", D0, 1.0 / 8.0, wqT, wkT, wvT, wp, None, None, None, bp, table, None)
        layernorm("n3")
        ffn0("f2")
        moe("m1")
        layernorm("n5")
        attention("a1", D1, float(1.0 / np.sqrt(np.float32(D1))), kqvT[:, 1], kqvT[:, 0], kqvT[:, 2], wproj.rearrange("(h d) c -> d h c", d=D1), bq, b1, wproj, bproj, None, slopes)
        moe("m2")

        with ExitStack() as ctx:
            (stored,) = sems(ctx, "st", "x")
            with nc.Block() as block:
                @block.sync
                def _(sp):
                    sp.dma_start(out.rearrange("(t p) c -> p t c", p=P), x[:]).then_inc(stored, 16)
                    sp.wait_ge(stored, 16)


def kernel(**inputs):
    import concourse.bacc as bacc
    from concourse.bass_utils import run_bass_kernel_spmd

    a = {k: np.asarray(v) for k, v in inputs.items()}
    kqv = a["L1_attn_W_kqv"].reshape(C, 3, H, D1)
    bkqv = a["L1_attn_b_kqv"].reshape(3, H, D1)
    arrays = {
        "x": a["L0_attn_x"].reshape(TOKENS, C),
        "wqT": a["L0_attn_Wq"].transpose(2, 0, 1),
        "wkT": a["L0_attn_Wk"].transpose(2, 0, 1),
        "wvT": a["L0_attn_Wv"].transpose(2, 0, 1),
        "wp": a["L0_attn_Wp"].reshape(H, D0, C).transpose(1, 0, 2),
        "bp": a["L0_attn_bp"].reshape(1, C),
        "table": a["L0_attn_rel_table"].reshape(1, -1),
        "wg0": a["L0_ffn_w_gate"].T,
        "wu0": a["L0_ffn_w_up"].T,
        "wd0": a["L0_ffn_w_down"].T,
        "kqvT": kqv.transpose(3, 1, 2, 0),
        "b1": bkqv[2].reshape(C, 1),
        "bq": bkqv[1].T,
        "wproj": a["L1_attn_W_proj"],
        "bproj": a["L1_attn_b_proj"].reshape(1, C),
        "slopes": a["L1_attn_slopes"].reshape(1, H),
        "wgate": a["L1_ffn_Wg"],
        "bgate": a["L1_ffn_bg"].reshape(1, E),
        "W1": a["L1_ffn_W1"],
        "W2": a["L1_ffn_W2"],
        "W3": a["L1_ffn_W3"],
    }
    arrays = {k: np.ascontiguousarray(v) for k, v in arrays.items()}
    nc = bacc.Bacc("TRN2", target_bir_lowering=False, num_devices=1)
    handles = [nc.dram_tensor(f"in_{k}", v.shape, mybir.dt.from_np(v.dtype), kind="ExternalInput").ap()
               for k, v in arrays.items()]
    y = nc.dram_tensor("out_y", [TOKENS, C], F, kind="ExternalOutput").ap()
    program(nc, *handles, y)
    r = run_bass_kernel_spmd(nc, [{f"in_{k}": v for k, v in arrays.items()}], core_ids=[0])
    return r.results[0]["out_y"].reshape(B, S, C)
```

```python
from contextlib import ExitStack

import concourse.bass as bass
import concourse.mybir as mybir
import numpy as np

F = mybir.dt.float32
FR = mybir.dt.float32r
I32 = mybir.dt.int32
ALU = mybir.AluOpType
ACT = mybir.ActivationFunctionType
AX = mybir.AxisListType

P = 128
B, S, C = 8, 512, 128
TOKENS = B * S
TILES = TOKENS // P
GROUPS = TOKENS // 512
QT = S // P
H = 16
D0, D1 = 64, 8
HID0 = 384
HC0 = HID0 // P
E, TOPK, HID1 = 8, 2, 512
HC1 = HID1 // P
CAP = int(TOKENS / E * 1.25)
ST = CAP // P
SLOTS = E * CAP
EPS = 1e-5
NEG = -1e30
BAND = 257

ORDER = (3, 2, 0, 1)
START = {3: 0, 2: 512, 0: 896, 1: 1024}
WIDTH = S * (QT + 1) // 2
TGROUPS = ((3,), (2, 0), (1,))


def program(nc, x_in, wqT, wkT, wvT, wp, bp, table, wg0, wu0, wd0,
            wkqv, bdup, b1, wproj, pdup, bproj, pick, slopes, wgate, bgate, W1, W2, W3, out):
    top = ExitStack()

    def sbuf(ctx, name, shape, dt=F):
        return ctx.enter_context(nc.sbuf_tensor(name, shape, dt))

    def banks(ctx, name, n):
        return [ctx.enter_context(nc.psum_tensor(f"{name}{i}", [P, 512], F)) for i in range(n)]

    def sems(ctx, tag, *names):
        made = [nc.alloc_semaphore(name=f"{tag}_{n}") for n in names]

        def clear():
            nc.clear_and_free_semaphores(made)
            nc.all_engine_barrier()
        ctx.callback(clear)
        return made

    slots_in = nc.dram_tensor("slots_in", [SLOTS + P, C], F).ap()
    slots_out = nc.dram_tensor("slots_out", [SLOTS + P, C], F).ap()
    skew = nc.dram_tensor("skew", [H, P, BAND], F)

    with top:
        x = sbuf(top, "x", [P, TILES, C])
        ident = sbuf(top, "ident", [P, P])
        XTh = sbuf(top, "XTh", [P, TOKENS], FR)
        XTl = sbuf(top, "XTl", [P, TOKENS], FR)
        half = sbuf(top, "half", [P, TILES])
        one = sbuf(top, "one", [P, 1])

        with ExitStack() as ctx:
            zeros = sbuf(ctx, "zeros", [P, C])
            loaded, made, zeroed = sems(ctx, "ld", "x", "made", "zeroed")
            with nc.Block() as block:
                @block.sync
                def _(sp):
                    sp.dma_start(x[:], x_in.rearrange("(t p) c -> p t c", p=P)).then_inc(loaded, 16)
                    sp.wait_ge(made, 2)
                    for n in range(SLOTS // P):
                        sp.dma_start(slots_in[n * P:(n + 1) * P, :], zeros[:]).then_inc(zeroed, 16)
                    sp.dma_start(slots_out[SLOTS:SLOTS + P, :], zeros[:]).then_inc(zeroed, 16)
                    sp.wait_ge(loaded, 16)
                    sp.wait_ge(zeroed, 16 * (SLOTS // P + 1))

                @block.gpsimd
                def _(pool):
                    nc.gpsimd.memset(ident[:], 0.0).then_inc(made, 1)
                    nc.gpsimd.memset(zeros[:], 0.0).then_inc(made, 1)
                    nc.gpsimd.memset(half[:], -0.5).then_inc(made, 1)
                    nc.gpsimd.memset(one[:], 1.0).then_inc(made, 1)
                    pool.wait_ge(made, 4)
                    nc.gpsimd.affine_select(out=ident[:], in_=ident[:], compare_op=ALU.not_equal, fill=1.0,
                                            base=0, pattern=[[-1, P]], channel_multiplier=1).then_inc(made, 1)
                    pool.wait_ge(made, 5)

        def layernorm(tag, keep=None):
            with ExitStack() as ctx:
                st = sbuf(ctx, f"{tag}st", [P, TILES, 6])
                mv = sbuf(ctx, f"{tag}mv", [P, TILES, 2])
                ve = sbuf(ctx, f"{tag}ve", [P, TILES])
                rs = sbuf(ctx, f"{tag}rs", [P, TILES])
                t1 = sbuf(ctx, f"{tag}t1", [P, TILES])
                rstd = sbuf(ctx, f"{tag}rstd", [P, TILES])
                xn = sbuf(ctx, f"{tag}xn", [P, 2, 4, C])
                tp = banks(ctx, f"{tag}tp", 2)
                ve_ok, rs_ok, chain, xn_ok, tp_ok, hi_ok, lo_ok, kept = sems(
                    ctx, tag, "ve_ok", "rs_ok", "chain", "xn_ok", "tp_ok", "hi_ok", "lo_ok", "kept")
                with nc.Block() as block:
                    @block.vector
                    def _(dve):
                        for t in range(TILES):
                            nc.vector.bn_stats(st[:, t, :], x[:, t, :]).then_inc(chain, 1)
                        dve.wait_ge(chain, TILES)
                        for t in range(TILES):
                            nc.vector.bn_aggr(mv[:, t, :], st[:, t, :]).then_inc(chain, 1)
                        dve.wait_ge(chain, 2 * TILES)
                        nc.vector.tensor_scalar(ve[:], mv[:, :, 1], EPS, None, ALU.add).then_inc(ve_ok, 1)
                        dve.wait_ge(rs_ok, 1)
                        nc.vector.tensor_tensor(t1[:], rs[:], rs[:], ALU.mult).then_inc(ve_ok, 1)
                        dve.wait_ge(ve_ok, 2)
                        nc.vector.tensor_tensor(t1[:], t1[:], ve[:], ALU.mult).then_inc(ve_ok, 1)
                        dve.wait_ge(ve_ok, 3)
                        nc.vector.tensor_scalar(t1[:], t1[:], -0.5, 1.5, ALU.mult, ALU.add).then_inc(ve_ok, 1)
                        dve.wait_ge(ve_ok, 4)
                        nc.vector.tensor_tensor(rstd[:], rs[:], t1[:], ALU.mult).then_inc(ve_ok, 1)
                        dve.wait_ge(ve_ok, 5)

                        def normalise(g, b):
                            for j in range(4):
                                n = nc.vector.tensor_scalar(
                                    xn[:, b, j, :], x[:, bass.ds(g * 4 + j, 1), :], mv[:, bass.ds(g * 4 + j, 1), 0],
                                    rstd[:, bass.ds(g * 4 + j, 1)], ALU.subtract, ALU.mult)
                            n.then_inc(xn_ok, 1)

                        def low(g, b):
                            dve.wait_ge(hi_ok, g + 1)
                            nc.vector.tensor_tensor(XTl[:, bass.ds(g * 512, 512)], tp[b][:],
                                                    XTh[:, bass.ds(g * 512, 512)].bitcast(F),
                                                    ALU.subtract).then_inc(lo_ok, 1)

                        normalise(0, 0)
                        normalise(1, 1)
                        low(0, 0)
                        low(1, 1)
                        with dve.Fori(1, GROUPS // 2) as m:
                            dve.wait_ge(tp_ok, 2 * m)
                            if keep is not None:
                                dve.wait_ge(kept, 2 * m)
                            normalise(2 * m, 0)
                            normalise(2 * m + 1, 1)
                            low(2 * m, 0)
                            low(2 * m + 1, 1)

                    @block.gpsimd
                    def _(pool):
                        pool.wait_ge(ve_ok, 1)
                        nc.gpsimd.tensor_tensor(rs[:], ve[:], half[:], ALU.pow).then_inc(rs_ok, 1)
                        if keep is not None:
                            with pool.Fori(0, GROUPS // 2) as m:
                                for b in range(2):
                                    pool.wait_ge(xn_ok, 2 * m + b + 1)
                                    nc.gpsimd.tensor_copy(keep[:, bass.ds(8 * m + 4 * b, 4), :],
                                                          xn[:, b, :, :]).then_inc(kept, 1)
                            pool.wait_ge(kept, GROUPS)

                    @block.tensor
                    def _(pe):
                        def turn(g, b):
                            pe.wait_ge(xn_ok, g + 1)
                            for j in range(4):
                                t = nc.tensor.transpose(tp[b][:, j * P:(j + 1) * P], xn[:, b, j, :], ident[:])
                            t.then_inc(tp_ok, 1)
                        turn(0, 0)
                        turn(1, 1)
                        with pe.Fori(1, GROUPS // 2) as m:
                            for b in range(2):
                                pe.wait_ge(lo_ok, 2 * m - 1 + b)
                                turn(2 * m + b, b)

                    @block.scalar
                    def _(act):
                        with act.Fori(0, GROUPS // 2) as m:
                            for b in range(2):
                                act.wait_ge(tp_ok, 2 * m + b + 1)
                                nc.scalar.activation(XTh[:, bass.ds(1024 * m + 512 * b, 512)], tp[b][:],
                                                     ACT.Copy).then_inc(hi_ok, 1)

        def ffn0(tag):
            with ExitStack() as ctx:
                wi = sbuf(ctx, f"{tag}wi", [P, 3, HID0], I32)
                wf = sbuf(ctx, f"{tag}wf", [P, 3, HID0])
                wh = sbuf(ctx, f"{tag}wh", [P, 2, HID0], FR)
                wl = sbuf(ctx, f"{tag}wl", [P, 2, HID0], FR)
                act_sb = sbuf(ctx, f"{tag}act", [P, 2, 512])
                hid = sbuf(ctx, f"{tag}hid", [P, 2, HC0, 512])
                pg = banks(ctx, f"{tag}pg", 2)
                pu = banks(ctx, f"{tag}pu", 2)
                po = banks(ctx, f"{tag}po", 2)
                w_in, w_ok, up_ok, silu_ok, hid_ok, down_ok, x_ok = sems(
                    ctx, tag, "w_in", "w_ok", "up_ok", "silu_ok", "hid_ok", "down_ok", "x_ok")
                with nc.Block() as block:
                    @block.sync
                    def _(sp):
                        sp.dma_start(wi[:, 0, :], wg0).then_inc(w_in, 16)
                        sp.dma_start(wi[:, 1, :], wu0).then_inc(w_in, 16)
                        sp.dma_start(wi[:, 2, :].rearrange("p (c d) -> p c d", c=HC0),
                                     wd0.rearrange("(c p) d -> p c d", p=P)).then_inc(w_in, 16)
                        sp.wait_ge(w_in, 48)

                    @block.tensor
                    def _(pe):
                        pe.wait_ge(w_ok, 3)

                        def up(g, p):
                            for c in range(HC0):
                                b = (HC0 * p + c) % 2
                                cols = bass.ds(g * 512, 512)
                                if isinstance(g, int):
                                    if HC0 * g + c >= 2:
                                        pe.wait_ge(hid_ok, HC0 * g + c - 1)
                                else:
                                    pe.wait_ge(hid_ok, HC0 * g + c - 1)
                                w = slice(c * P, (c + 1) * P)
                                for i, bank in ((0, pg[b]), (1, pu[b])):
                                    nc.tensor.matmul(bank[:], wh[:, i, w], XTh[:, cols], start=True, stop=False)
                                    nc.tensor.matmul(bank[:], wl[:, i, w], XTh[:, cols], start=False, stop=False)
                                    nc.tensor.matmul(bank[:], wh[:, i, w], XTl[:, cols], start=False,
                                                     stop=True).then_inc(up_ok, 1)

                        def down(g, p):
                            pe.wait_ge(hid_ok, HC0 * g + HC0)
                            if not isinstance(g, int) or g >= 2:
                                pe.wait_ge(x_ok, g - 1)
                            for j in range(4):
                                for c in range(HC0):
                                    n = nc.tensor.matmul(po[p][:, j * P:(j + 1) * P], hid[:, p, c, j * P:(j + 1) * P],
                                                         wf[:, 2, c * P:(c + 1) * P], start=(c == 0), stop=(c == HC0 - 1))
                            n.then_inc(down_ok, 1)

                        up(0, 0)
                        up(1, 1)
                        down(0, 0)
                        up(2, 0)
                        down(1, 1)
                        with pe.Fori(1, GROUPS // 2 - 1) as m:
                            up(2 * m + 1, 1)
                            down(2 * m, 0)
                            up(2 * m + 2, 0)
                            down(2 * m + 1, 1)
                        up(GROUPS - 1, 1)
                        down(GROUPS - 2, 0)
                        down(GROUPS - 1, 1)

                    @block.scalar
                    def _(act):
                        def silu(g, p):
                            for c in range(HC0):
                                b = (HC0 * p + c) % 2
                                act.wait_ge(up_ok, 2 * (HC0 * g + c) + 1)
                                if not isinstance(g, int) or HC0 * g + c >= 2:
                                    act.wait_ge(hid_ok, HC0 * g + c - 1)
                                nc.scalar.activation(act_sb[:, b, :], pg[b][:], ACT.Silu).then_inc(silu_ok, 1)
                        silu(0, 0)
                        silu(1, 1)
                        with act.Fori(1, GROUPS // 2) as m:
                            silu(2 * m, 0)
                            silu(2 * m + 1, 1)

                    @block.vector
                    def _(dve):
                        dve.wait_ge(w_in, 48)
                        nc.vector.tensor_scalar(wf[:], wi[:], float(np.float32(1.0 / 127.0)), None, ALU.mult).then_inc(w_ok, 1)
                        dve.wait_ge(w_ok, 1)
                        nc.vector.tensor_copy(wh[:], wf[:, 0:2, :]).then_inc(w_ok, 1)
                        dve.wait_ge(w_ok, 2)
                        nc.vector.tensor_tensor(wl[:], wf[:, 0:2, :], wh[:].bitcast(F), ALU.subtract).then_inc(w_ok, 1)

                        def gated(g, p):
                            for c in range(HC0):
                                b = (HC0 * p + c) % 2
                                dve.wait_ge(silu_ok, HC0 * g + c + 1)
                                dve.wait_ge(up_ok, 2 * (HC0 * g + c) + 2)
                                if c == 0 and (not isinstance(g, int) or g >= 2):
                                    dve.wait_ge(down_ok, g - 1)
                                nc.vector.tensor_tensor(hid[:, p, c, :], act_sb[:, b, :], pu[b][:],
                                                        ALU.mult).then_inc(hid_ok, 1)

                        def add(g, p):
                            dve.wait_ge(down_ok, g + 1)
                            rows = x[:, bass.ds(g * 4, 4), :]
                            nc.vector.scalar_tensor_tensor(rows, po[p][:].rearrange("p (j c) -> p j c", j=4), 0.5, rows,
                                                           ALU.mult, ALU.add).then_inc(x_ok, 1)

                        gated(0, 0)
                        gated(1, 1)
                        add(0, 0)
                        with dve.Fori(1, GROUPS // 2) as m:
                            gated(2 * m, 0)
                            add(2 * m - 1, 1)
                            gated(2 * m + 1, 1)
                            add(2 * m, 0)
                        add(GROUPS - 1, 1)

        def attention(tag, d, scale, q_w, k_w, v_w, p_w, q_bias, v_bias, p_full, p_bias, relative, slope):
            STEPS = B * H
            with ExitStack() as ctx:
                Mh = sbuf(ctx, f"{tag}Mh", [P, H, C], FR)
                Ml = sbuf(ctx, f"{tag}Ml", [P, H, C], FR)
                Nh = sbuf(ctx, f"{tag}Nh", [P, H, C], FR)
                Nl = sbuf(ctx, f"{tag}Nl", [P, H, C], FR)
                gb = sbuf(ctx, f"{tag}gb", [P, H])
                bias = sbuf(ctx, f"{tag}bias", [P, H, S])

                with ExitStack() as pre:
                    wq_sb = sbuf(pre, f"{tag}wq", [d, H, C])
                    wk_sb = sbuf(pre, f"{tag}wk", [d, H, C])
                    wv_sb = sbuf(pre, f"{tag}wv", [d, H, C])
                    wp_sb = sbuf(pre, f"{tag}wp", [d, H, C])
                    row = sbuf(pre, f"{tag}row", [P, C])
                    rel = sbuf(pre, f"{tag}rel", [P, 33 * H if relative is not None else H])
                    dist = sbuf(pre, f"{tag}dist", [P, S])
                    pm = banks(pre, f"{tag}pm", 2)
                    pn = banks(pre, f"{tag}pn", 2)
                    pb = banks(pre, f"{tag}pb", 1)[0]
                    w_in, r_in, mat_ok, hi_ok, lo_ok, b_ok, sk_out, sk_in = sems(
                        pre, f"{tag}p", "w_in", "r_in", "mat_ok", "hi_ok", "lo_ok", "b_ok", "sk_out", "sk_in")
                    if v_bias is not None:
                        bq_sb = sbuf(pre, f"{tag}bq", [d, H])
                        bv_sb = sbuf(pre, f"{tag}bv", [P, 1])
                        bvx = sbuf(pre, f"{tag}bvx", [P, P])
                        pf_sb = sbuf(pre, f"{tag}pf", [P, C])
                    if relative is not None:
                        rows = sbuf(pre, f"{tag}rows", [P, H, BAND])
                    n_w = 4 + (3 if v_bias is not None else 0)
                    with nc.Block() as block:
                        @block.sync
                        def _(sp):
                            for dst, src in ((wq_sb, q_w), (wk_sb, k_w), (wv_sb, v_w), (wp_sb, p_w)):
                                sp.dma_start(dst[:], src).then_inc(w_in, 16)
                            if v_bias is not None:
                                sp.dma_start(bq_sb[:], q_bias).then_inc(w_in, 16)
                                sp.dma_start(bv_sb[:], v_bias).then_inc(w_in, 16)
                                sp.dma_start(pf_sb[:], p_full).then_inc(w_in, 16)
                            sp.dma_start(row[:], p_bias.broadcast_to([P, C])).then_inc(r_in, 16)
                            src = relative if relative is not None else slope
                            sp.dma_start(rel[:], src.broadcast_to([P, src.shape[1]])).then_inc(r_in, 16)
                            sp.wait_ge(r_in, 32)
                            sp.wait_ge(w_in, 16 * n_w)
                            if relative is not None:
                                sp.wait_ge(b_ok, 2)
                                sp.dma_start(skew.ap().rearrange("h p c -> p h c"), rows[:]).then_inc(sk_out, 16)
                                sp.wait_ge(sk_out, 16)
                                shifted = bass.AP(skew, 0, [[BAND - 1, P], [P * BAND, H], [1, BAND - 1]])
                                sp.dma_start(bias[:, :, S - BAND + 1:S], shifted).then_inc(sk_in, 16)
                                sp.wait_ge(sk_in, 16)

                        @block.tensor
                        def _(pe):
                            pe.wait_ge(w_in, 16 * n_w)
                            for h in range(H):
                                b = h % 2
                                if h >= 2:
                                    pe.wait_ge(lo_ok, 2 * (h - 1) + 1)
                                nc.tensor.matmul(pm[b][:, 0:C], wq_sb[:, h, :], wk_sb[:, h, :], start=True,
                                                 stop=True).then_inc(mat_ok, 1)
                                nc.tensor.matmul(pn[b][:, 0:C], wv_sb[:, h, :], wp_sb[:, h, :], start=True,
                                                 stop=True).then_inc(mat_ok, 1)
                            if v_bias is not None:
                                for h in range(H):
                                    nc.tensor.matmul(pb[:, C + h:C + h + 1], wk_sb[:, h, :], bq_sb[:, h:h + 1],
                                                     start=True, stop=True)
                                pe.wait_ge(b_ok, 3)
                                nc.tensor.matmul(pb[:, 0:C], bvx[:], pf_sb[:], start=True, stop=True).then_inc(mat_ok, 1)

                        @block.scalar
                        def _(act):
                            for h in range(H):
                                b = h % 2
                                act.wait_ge(mat_ok, 2 * h + 1)
                                nc.scalar.activation(Mh[:, h, :], pm[b][:, 0:C], ACT.Copy, scale=scale).then_inc(hi_ok, 1)
                                act.wait_ge(mat_ok, 2 * h + 2)
                                nc.scalar.activation(Nh[:, h, :], pn[b][:, 0:C], ACT.Copy).then_inc(hi_ok, 1)

                        @block.vector
                        def _(dve):
                            dve.wait_ge(r_in, 32)
                            if relative is not None:
                                tab = rel[:].rearrange("p (j h) -> p h j", h=H)
                                nc.vector.tensor_copy(rows[:], tab[:, :, 0:1].broadcast_to([P, H, BAND])).then_inc(b_ok, 1)
                                nc.vector.tensor_copy(bias[:, :, 0:S - BAND + 1],
                                                      tab[:, :, 0:1].broadcast_to([P, H, S - BAND + 1])).then_inc(lo_ok, 1)
                                dve.wait_ge(b_ok, 1)
                                nc.vector.tensor_copy(rows[:, :, P - 16 + 1:P + 1], tab[:, :, 1:17]).then_inc(b_ok, 1)
                            else:
                                dve.wait_ge(b_ok, 1)
                                for h in range(H):
                                    nb = nc.vector.tensor_scalar(bias[:, h, :], dist[:], rel[:, h:h + 1], None, ALU.mult)
                                nb.then_inc(b_ok, 1)
                                dve.wait_ge(w_in, 16 * n_w)
                                nc.vector.tensor_copy(bvx[:], bv_sb[:].broadcast_to([P, P])).then_inc(b_ok, 1)
                                nc.vector.tensor_scalar(gb[:, 0:1], row[:, 0:1], 0.0, None, ALU.mult).then_inc(lo_ok, 1)
                            for h in range(H):
                                b = h % 2
                                dve.wait_ge(hi_ok, 2 * h + 1)
                                nc.vector.scalar_tensor_tensor(Ml[:, h, :], pm[b][:, 0:C], scale, Mh[:, h, :].bitcast(F),
                                                               ALU.mult, ALU.subtract).then_inc(lo_ok, 1)
                                dve.wait_ge(hi_ok, 2 * h + 2)
                                nc.vector.tensor_tensor(Nl[:, h, :], pn[b][:, 0:C], Nh[:, h, :].bitcast(F),
                                                        ALU.subtract).then_inc(lo_ok, 1)
                            if v_bias is not None:
                                dve.wait_ge(lo_ok, 1)
                                dve.wait_ge(mat_ok, 2 * H + 1)
                                nc.vector.tensor_scalar(gb[:], pb[:, C:C + H], scale, None, ALU.mult).then_inc(lo_ok, 1)
                                nc.vector.tensor_tensor(row[:], row[:], pb[:, 0:C], ALU.add).then_inc(lo_ok, 1)
                            else:
                                nc.vector.memset(gb[:], 0.0).then_inc(lo_ok, 1)
                                nc.vector.tensor_scalar(row[:], row[:], 1.0, None, ALU.mult).then_inc(lo_ok, 1)
                            dve.wait_ge(lo_ok, 2 * H + 3)
                            nc.vector.tensor_tensor(x[:], x[:], row[:].unsqueeze(1).broadcast_to([P, TILES, C]),
                                                    ALU.add).then_inc(lo_ok, 1)

                        @block.gpsimd
                        def _(pool):
                            if relative is None:
                                nc.gpsimd.iota(dist[:], [[1, S]], base=-(S - P), channel_multiplier=-1,
                                               allow_small_or_imprecise_dtypes=True).then_inc(b_ok, 1)
                                pool.wait_ge(b_ok, 2)
                            else:
                                pool.wait_ge(sk_in, 16)
                            nc.gpsimd.affine_select(out=bias[:, :, S - P:S], in_=bias[:, :, S - P:S], compare_op=ALU.is_ge,
                                                    fill=NEG, base=0, pattern=[[0, H], [-1, P]],
                                                    channel_multiplier=1).then_inc(b_ok, 1)

                Mc = [sbuf(ctx, f"{tag}Mc{i}", [P, 2, C], FR) for i in range(2)]
                XTc = sbuf(ctx, f"{tag}XTc", [P, 2, S], FR)
                Gh = sbuf(ctx, f"{tag}Gh", [P, S], FR)
                Gl = sbuf(ctx, f"{tag}Gl", [P, S], FR)
                bc = [sbuf(ctx, f"{tag}bc{i}", [P, S]) for i in range(2)]
                prob = [sbuf(ctx, f"{tag}prob{i}", [P, WIDTH]) for i in range(2)]
                negmax = [sbuf(ctx, f"{tag}nm{i}", [P, QT]) for i in range(2)]
                total = [sbuf(ctx, f"{tag}tot{i}", [P, QT]) for i in range(2)]
                inv = [sbuf(ctx, f"{tag}inv{i}", [P, QT]) for i in range(2)]
                V = [sbuf(ctx, f"{tag}V{i}", [P, QT, 2, C]) for i in range(2)]
                PT = sbuf(ctx, f"{tag}PT", [P, WIDTH])
                tick = sbuf(ctx, f"{tag}tick", [1, 4])
                ps = banks(ctx, f"{tag}ps", 3)
                pt = banks(ctx, f"{tag}pt", 2)
                pg, pv, py = banks(ctx, f"{tag}pg", 3)
                names = ("bc_ok", "m_ok", "xt_ok", "g_ok", "gh_ok", "gl_ok", "s_ok", "max_ok", "exp_ok", "v_ok", "vc_ok",
                         "t_ok", "tc_ok", "y_ok", "inv_ok", "x_ok")
                (bc_ok, m_ok, xt_ok, g_ok, gh_ok, gl_ok, s_ok, max_ok, exp_ok, v_ok, vc_ok,
                 t_ok, tc_ok, y_ok, inv_ok, x_ok) = sems(ctx, tag, *names)
                bank_of = {3: (ps[0], 0), 2: (ps[1], 0), 0: (ps[1], 384), 1: (ps[2], 0)}

                def first(n, k=1):
                    return isinstance(n, int) and n < k

                with nc.Block() as block:
                    @block.gpsimd
                    def _(pool):
                        def copy(dst, src):
                            return nc.gpsimd.tensor_tensor(dst, src, one[:].broadcast_to([P, dst.shape[-1]]), ALU.mult)

                        def matrix(n, p):
                            if not first(n, 2):
                                pool.wait_ge(g_ok, n - 1)
                            for i, m in enumerate((Mh, Ml)):
                                c = copy(Mc[p][:, i, :], m[:, bass.ds(n % H, 1), :].squeeze(1).bitcast(F))
                            c.then_inc(m_ok, 1)

                        def batch(b):
                            if not first(b):
                                pool.wait_ge(v_ok, b * H)
                            copy(XTc[:, 0, :], XTh[:, bass.ds(b * S, S)].bitcast(F))
                            copy(XTc[:, 1, :], XTl[:, bass.ds(b * S, S)].bitcast(F)).then_inc(xt_ok, 1)

                        def step(n, p, last=False):
                            if not last:
                                matrix(n + 1, 1 - p)
                            if not first(n, 2):
                                pool.wait_ge(max_ok, 4 * n - 4)
                            copy(bc[p][:], bias[:, bass.ds(n % H, 1), :].squeeze(1)).then_inc(bc_ok, 1)

                        def rest(b, to):
                            with pool.Fori(1, to) as k:
                                step(b * H + 2 * k, 0)
                                step(b * H + 2 * k + 1, 1)

                        matrix(0, 0)
                        batch(0)
                        step(0, 0)
                        step(1, 1)
                        rest(0, H // 2)
                        with pool.Fori(1, B - 1) as b:
                            batch(b)
                            step(b * H, 0)
                            step(b * H + 1, 1)
                            rest(b, H // 2)
                        b = B - 1
                        batch(b)
                        step(b * H, 0)
                        step(b * H + 1, 1)
                        rest(b, H // 2 - 1)
                        step(STEPS - 2, 0)
                        step(STEPS - 1, 1, last=True)

                    @block.tensor
                    def _(pe):
                        def queries(n, p):
                            pe.wait_ge(m_ok, n + 1)
                            if not first(n):
                                pe.wait_ge(gl_ok, n)
                            cols = bass.ds((n // H) * S, S)
                            nc.tensor.matmul(pg[:], Mc[p][:, 0, :], XTh[:, cols], start=True, stop=False)
                            nc.tensor.matmul(pg[:], Mc[p][:, 1, :], XTh[:, cols], start=False, stop=False)
                            nc.tensor.matmul(pg[:], Mc[p][:, 0, :], XTl[:, cols], start=False, stop=True).then_inc(g_ok, 1)

                        def scores(n):
                            pe.wait_ge(gl_ok, n + 1)
                            for i in ORDER:
                                if not first(n) and i != 0:
                                    pe.wait_ge(max_ok, 4 * n - {3: 3, 2: 1, 1: 0}[i])
                                bank, at = bank_of[i]
                                q, w = slice(i * P, (i + 1) * P), (i + 1) * P
                                cols = bass.ds((n // H) * S, w)
                                o = bank[:, at:at + w]
                                nc.tensor.matmul(o, Gh[:, q], XTh[:, cols], start=True, stop=False)
                                nc.tensor.matmul(o, Gl[:, q], XTh[:, cols], start=False, stop=False)
                                s = nc.tensor.matmul(o, Gh[:, q], XTl[:, cols], start=False, stop=True)
                                if i != 2:
                                    s.then_inc(s_ok, 1)

                        def values(k, half):
                            pe.wait_ge(xt_ok, k // H + 1)
                            if not first(k):
                                pe.wait_ge(vc_ok, k)
                            h = bass.ds((k // 2 * 2) % H, 2)
                            for j in (2 * half, 2 * half + 1):
                                t = slice(j * P, (j + 1) * P)
                                o = pv[:, (j % 2) * 2 * C:(j % 2 + 1) * 2 * C]
                                nc.tensor.matmul(o, XTc[:, 0, t], Nh[:, h, :], start=True, stop=False)
                                nc.tensor.matmul(o, XTc[:, 1, t], Nh[:, h, :], start=False, stop=False)
                                v = nc.tensor.matmul(o, XTc[:, 0, t], Nl[:, h, :], start=False, stop=True)
                            v.then_inc(v_ok, 1)

                        def turn(n, p, k):
                            pe.wait_ge(exp_ok, 4 * n + (1, 3, 4)[k])
                            if k == 2 or not first(n):
                                pe.wait_ge(tc_ok, 3 * n + (0, 0, 1)[k])
                            o = 0
                            for i in TGROUPS[k]:
                                for j in range(i + 1):
                                    t = nc.tensor.transpose(pt[k % 2][:, o:o + P],
                                                            prob[p][:, START[i] + j * P:START[i] + (j + 1) * P], ident[:])
                                    o += P
                            t.then_inc(t_ok, 1)

                        def mix(n, p, vp, k):
                            if k == 0:
                                pe.wait_ge(vc_ok, n // 2 * 2 + 2)
                                if not first(n):
                                    pe.wait_ge(x_ok, n)
                            pe.wait_ge(tc_ok, 3 * n + k + 1)
                            for i in TGROUPS[k]:
                                o = py[:, i * C:(i + 1) * C]
                                for j in range(i + 1):
                                    b = slice(START[i] + j * P, START[i] + (j + 1) * P)
                                    y = nc.tensor.matmul(o, PT[:, b], V[vp][:, j, p, :], start=(j == 0), stop=(j == i))
                            if k == 2:
                                y.then_inc(y_ok, 1)

                        def step(n, r, last=False):
                            p, q, vp = r % 2, (r - 1) % 2, (r - 1) % 4 // 2
                            scores(n)
                            turn(n - 1, q, 0)
                            turn(n - 1, q, 1)
                            if not last:
                                queries(n + 1, 1 - p)
                            mix(n - 1, q, vp, 0)
                            turn(n - 1, q, 2)
                            if not last:
                                values(n + 1, 1 - p)
                            mix(n - 1, q, vp, 1)
                            mix(n - 1, q, vp, 2)

                        queries(0, 0)
                        scores(0)
                        queries(1, 1)
                        values(0, 0)
                        values(1, 1)
                        for n in range(1, 4):
                            step(n, n)
                        with pe.Fori(1, STEPS // 4 - 1) as m:
                            for r in range(4):
                                step(4 * m + r, r)
                        for r in range(4):
                            step(STEPS - 4 + r, r, last=(r == 3))
                        n = STEPS - 1
                        turn(n, 1, 0)
                        turn(n, 1, 1)
                        mix(n, 1, 1, 0)
                        turn(n, 1, 2)
                        mix(n, 1, 1, 1)
                        mix(n, 1, 1, 2)

                    @block.scalar
                    def _(act):
                        def query_hi(n):
                            act.wait_ge(g_ok, n + 1)
                            nc.scalar.activation(Gh[:], pg[:], ACT.Identity, bias=gb[:, bass.ds(n % H, 1)]).then_inc(gh_ok, 1)

                        def values(k, vp, half):
                            act.wait_ge(v_ok, k + 1)
                            nc.scalar.activation(V[vp][:, 2 * half:2 * half + 2, :, :].rearrange("p j h c -> p (j h c)"),
                                                 pv[:], ACT.Copy).then_inc(vc_ok, 1)

                        def exponentials(n, p, tiles):
                            for i in tiles:
                                act.wait_ge(max_ok, 4 * n + ORDER.index(i) + 1)
                                if i == 3 and not first(n, 2):
                                    act.wait_ge(inv_ok, n - 1)
                                s = prob[p][:, START[i]:START[i] + (i + 1) * P]
                                nc.scalar.activation(s, s, ACT.Exp, bias=negmax[p][:, i:i + 1], scale=-1.0,
                                                     accum_out=total[p][:, i:i + 1]).then_inc(exp_ok, 1)

                        def turned(n, k):
                            act.wait_ge(t_ok, 3 * n + k + 1)
                            w = sum(i + 1 for i in TGROUPS[k]) * P
                            o = START[TGROUPS[k][0]]
                            nc.scalar.activation(PT[:, o:o + w], pt[k % 2][:, 0:w], ACT.Copy).then_inc(tc_ok, 1)

                        def step(n, r, last=False):
                            p = r % 2
                            exponentials(n, p, (3,))
                            turned(n - 1, 0)
                            turned(n - 1, 1)
                            exponentials(n, p, (2,))
                            if not last:
                                query_hi(n + 1)
                            exponentials(n, p, (0, 1))
                            turned(n - 1, 2)
                            if not last:
                                values(n + 1, (r + 1) % 4 // 2, 1 - p)

                        query_hi(0)
                        query_hi(1)
                        exponentials(0, 0, (3, 2))
                        values(0, 0, 0)
                        values(1, 0, 1)
                        exponentials(0, 0, (0, 1))
                        for n in range(1, 4):
                            step(n, n)
                        with act.Fori(1, STEPS // 4 - 1) as m:
                            for r in range(4):
                                step(4 * m + r, r)
                        for r in range(4):
                            step(STEPS - 4 + r, r, last=(r == 3))
                        for k in range(3):
                            turned(STEPS - 1, k)

                    @block.vector
                    def _(dve):
                        def query_lo(n):
                            dve.wait_ge(gh_ok, n + 1)
                            nc.vector.scalar_tensor_tensor(Gl[:], pg[:], gb[:, bass.ds(n % H, 1)], Gh[:].bitcast(F),
                                                           ALU.add, ALU.subtract).then_inc(gl_ok, 1)

                        def maxima(n, p, tiles=ORDER):
                            if tiles[0] == 3:
                                dve.wait_ge(bc_ok, n + 1)
                            for i in tiles:
                                bank, at = bank_of[i]
                                w = (i + 1) * P
                                if i != 0:
                                    dve.wait_ge(s_ok, 3 * n + {3: 1, 2: 2, 1: 3}[i])
                                    nc.vector.memset(tick[:, i:i + 1], 0.0)
                                nc.vector.tensor_tensor_reduce(
                                    out=prob[p][:, START[i]:START[i] + w], in0=bank[:, at:at + w],
                                    in1=bc[p][:, S - w:S], scale=-1.0, scalar=3e38,
                                    op0=ALU.add, op1=ALU.min, accum_out=negmax[p][:, i:i + 1]).then_inc(max_ok, 1)

                        def inverse(n, p):
                            dve.wait_ge(exp_ok, 4 * n + 4)
                            nc.vector.reciprocal(inv[p][:], total[p][:]).then_inc(inv_ok, 1)

                        def add(n, p):
                            dve.wait_ge(inv_ok, n + 1)
                            dve.wait_ge(y_ok, n + 1)
                            for i in range(QT):
                                r = x[:, bass.ds((n // H) * QT + i, 1), :]
                                a = nc.vector.scalar_tensor_tensor(r, py[:, i * C:(i + 1) * C], inv[p][:, i:i + 1], r,
                                                                   ALU.mult, ALU.add)
                            a.then_inc(x_ok, 1)

                        def step(n, p, last=False):
                            maxima(n, p, ORDER[:1])
                            if not first(n, 2):
                                add(n - 2, p)
                            maxima(n, p, ORDER[1:])
                            inverse(n - 1, 1 - p)
                            if not last:
                                query_lo(n + 1)

                        query_lo(0)
                        maxima(0, 0)
                        query_lo(1)
                        step(1, 1)
                        with dve.Fori(1, STEPS // 2 - 1) as m:
                            step(2 * m, 0)
                            step(2 * m + 1, 1)
                        step(STEPS - 2, 0)
                        step(STEPS - 1, 1, last=True)
                        add(STEPS - 2, 0)
                        inverse(STEPS - 1, 1)
                        add(STEPS - 1, 1)

        def narrow_attention(tag, scale, w_kqv, b_dup, v_bias, p_full, p_dup, p_bias, pick, slope):
            G4, HH = 4, 8
            with ExitStack() as ctx:
                Wh = sbuf(ctx, f"{tag}Wh", [P, 2, G4, P], FR)
                Wl = sbuf(ctx, f"{tag}Wl", [P, 2, G4, P], FR)
                Vh = sbuf(ctx, f"{tag}Vwh", [P, C], FR)
                Vl = sbuf(ctx, f"{tag}Vwl", [P, C], FR)
                pd_sb = sbuf(ctx, f"{tag}pd", [P, 2, C])
                bias = sbuf(ctx, f"{tag}bias", [P, H, S])
                bd = sbuf(ctx, f"{tag}bd", [P, 2, G4])
                bz = sbuf(ctx, f"{tag}bz", [P, 2, G4])
                pk = sbuf(ctx, f"{tag}pk", [P, 2])
                Vm = [sbuf(ctx, f"{tag}Vm{i}", [P, QT, HH * (P + 16)], FR) for i in range(2)]

                with ExitStack() as pre:
                    w_sb = sbuf(pre, f"{tag}w", [P, 3 * C])
                    row = sbuf(pre, f"{tag}row", [P, C])
                    rel = sbuf(pre, f"{tag}rel", [P, H])
                    dist = sbuf(pre, f"{tag}dist", [P, S])
                    bv_sb = sbuf(pre, f"{tag}bv", [P, 1])
                    bvx = sbuf(pre, f"{tag}bvx", [P, P])
                    pf_sb = sbuf(pre, f"{tag}pf", [P, C])
                    pb = banks(pre, f"{tag}pb", 1)[0]
                    w_in, b_ok, row_ok, chain = sems(pre, f"{tag}p", "w_in", "b_ok", "row_ok", "chain")
                    with nc.Block() as block:
                        @block.sync
                        def _(sp):
                            sp.dma_start(rel[:], slope.broadcast_to([P, H])).then_inc(w_in, 16)
                            sp.dma_start(w_sb[:], w_kqv).then_inc(w_in, 16)
                            sp.dma_start(bd[:], b_dup).then_inc(w_in, 16)
                            sp.dma_start(pk[:], pick).then_inc(w_in, 16)
                            sp.dma_start(bv_sb[:], v_bias).then_inc(w_in, 16)
                            sp.dma_start(pf_sb[:], p_full).then_inc(w_in, 16)
                            sp.dma_start(pd_sb[:], p_dup).then_inc(w_in, 16)
                            sp.dma_start(row[:], p_bias.broadcast_to([P, C])).then_inc(w_in, 16)
                            sp.wait_ge(w_in, 8 * 16)

                        @block.tensor
                        def _(pe):
                            pe.wait_ge(row_ok, 1)
                            nc.tensor.matmul(pb[:, 0:C], bvx[:], pf_sb[:], start=True, stop=True).then_inc(row_ok, 1)

                        @block.vector
                        def _(dve):
                            for m in Vm:
                                nc.vector.memset(m[:].bitcast(F), 0.0).then_inc(chain, 1)
                            dve.wait_ge(w_in, 8 * 16)
                            nc.vector.tensor_copy(bvx[:], bv_sb[:].broadcast_to([P, P])).then_inc(row_ok, 1)
                            nc.vector.tensor_scalar(bd[:, 1, :], bd[:, 1, :], scale, None, ALU.mult).then_inc(chain, 1)
                            for i in range(2):
                                for g in range(G4):
                                    w = w_sb[:, i * C + g * 32:i * C + g * 32 + 32].rearrange("p (h d) -> p h d", d=D1)
                                    w = w.unsqueeze(2).broadcast_to([P, G4, 4, D1])
                                    hi = Wh[:, i, g, :].rearrange("p (h a d) -> p h a d", h=G4, a=4)
                                    lo = Wl[:, i, g, :].rearrange("p (h a d) -> p h a d", h=G4, a=4)
                                    f = scale if i else 1.0
                                    nc.vector.tensor_scalar(hi, w, f, None, ALU.mult).then_inc(chain, 1)
                                    dve.wait_ge(chain, 4 + i * G4 + g)
                                    for h in range(G4):
                                        nc.vector.scalar_tensor_tensor(lo[:, h], w[:, h], f, hi[:, h].bitcast(F), ALU.mult,
                                                                       ALU.subtract)
                            nc.vector.tensor_copy(Vh[:], w_sb[:, 2 * C:3 * C]).then_inc(chain, 1)
                            dve.wait_ge(chain, 12)
                            nc.vector.tensor_tensor(Vl[:], w_sb[:, 2 * C:3 * C], Vh[:].bitcast(F), ALU.subtract)
                            for i in range(2):
                                nc.vector.tensor_scalar(bz[:, i, :], bd[:, i, :], pk[:, i:i + 1], None, ALU.mult)
                            dve.wait_ge(b_ok, 1)
                            for h in range(H):
                                nb = nc.vector.tensor_scalar(bias[:, h, :], dist[:], rel[:, h:h + 1], None, ALU.mult)
                            nb.then_inc(b_ok, 1)
                            dve.wait_ge(row_ok, 2)
                            nc.vector.tensor_tensor(row[:], row[:], pb[:, 0:C], ALU.add).then_inc(row_ok, 1)
                            dve.wait_ge(row_ok, 3)
                            nc.vector.tensor_tensor(x[:], x[:], row[:].unsqueeze(1).broadcast_to([P, TILES, C]),
                                                    ALU.add).then_inc(row_ok, 1)
                            dve.wait_ge(row_ok, 4)

                        @block.gpsimd
                        def _(pool):
                            nc.gpsimd.iota(dist[:], [[1, S]], base=-(S - P), channel_multiplier=-1,
                                           allow_small_or_imprecise_dtypes=True).then_inc(b_ok, 1)
                            pool.wait_ge(b_ok, 2)
                            nc.gpsimd.affine_select(out=bias[:, :, S - P:S], in_=bias[:, :, S - P:S], compare_op=ALU.is_ge,
                                                    fill=NEG, base=0, pattern=[[0, H], [-1, P]],
                                                    channel_multiplier=1).then_inc(b_ok, 1)

                Z = sbuf(ctx, f"{tag}Z", [P, S], FR)
                st = [sbuf(ctx, f"{tag}st{i}", [P, 2, S], FR) for i in range(2)]
                XTc = sbuf(ctx, f"{tag}XTc", [P, 2, S], FR)
                Vs = sbuf(ctx, f"{tag}Vs", [P, QT, H, D1])
                prob = [sbuf(ctx, f"{tag}prob{i}", [P, WIDTH]) for i in range(2)]
                negmax = [sbuf(ctx, f"{tag}nm{i}", [P, QT]) for i in range(2)]
                total = [sbuf(ctx, f"{tag}tot{i}", [P, QT, HH]) for i in range(2)]
                inv = sbuf(ctx, f"{tag}inv", [P, QT, HH])
                PTh = sbuf(ctx, f"{tag}PTh", [P, QT, S], FR)
                PTl = sbuf(ctx, f"{tag}PTl", [P, QT, S], FR)
                OT = sbuf(ctx, f"{tag}OT", [P, S])
                O = sbuf(ctx, f"{tag}O", [P, QT, HH, 2 * D1])
                OTn = sbuf(ctx, f"{tag}OTn", [P, S])
                tick = sbuf(ctx, f"{tag}tick", [1, 4])
                ps = banks(ctx, f"{tag}ps", 3)
                pt = banks(ctx, f"{tag}pt", 3)
                po = banks(ctx, f"{tag}po", 1)[0]
                pm = banks(ctx, f"{tag}pm", 1)[0]
                names = ("xtc_ok", "proj_ok", "z_ok", "st_ok", "s_ok", "max_ok", "exp_ok", "t_ok", "hi_ok", "lo_ok",
                         "v_ok", "vs_ok", "vm_ok", "mix_ok", "ot_ok", "inv_ok", "back_ok", "o_ok", "fwd_ok", "otn_ok",
                         "y_ok", "x_ok")
                (xtc_ok, proj_ok, z_ok, st_ok, s_ok, max_ok, exp_ok, t_ok, hi_ok, lo_ok, v_ok, vs_ok, vm_ok, mix_ok,
                 ot_ok, inv_ok, back_ok, o_ok, fwd_ok, otn_ok, y_ok, x_ok) = sems(ctx, tag, *names)
                bank_of = {3: (ps[0], 0), 2: (ps[1], 0), 0: (ps[1], 384), 1: (ps[2], 0)}
                COPIES = {0: ((0, 4, 384),), 1: ((0, 3, 256),), 2: ((0, 1, 0), (P, 2, P))}

                def is_first(n, k=1):
                    return isinstance(n, int) and n < k

                def head(b, h):
                    return b + h // H, h % H, b * H + h

                def past(b, h):
                    return isinstance(b, int) and b + h // H >= B

                with nc.Block() as block:
                    @block.gpsimd
                    def _(pool):
                        def copy(dst, src):
                            return nc.gpsimd.tensor_tensor(dst, src, one[:].broadcast_to([P, S]), ALU.mult)

                        def batch(b):
                            if not is_first(b):
                                pool.wait_ge(v_ok, b)
                            copy(XTc[:, 0, :], XTh[:, bass.ds(b * S, S)].bitcast(F))
                            copy(XTc[:, 1, :], XTl[:, bass.ds(b * S, S)].bitcast(F)).then_inc(xtc_ok, 1)

                        def spread(b, u):
                            if not is_first(b):
                                pool.wait_ge(mix_ok, 2 * b + u - 1)
                            if u == 0:
                                pool.wait_ge(vs_ok, b + 1)
                            to = Vm[u][:].rearrange("p j (h c) -> p j h c", h=HH)
                            for j in range(QT):
                                v = nc.gpsimd.tensor_tensor(
                                    to[:, j, :, 0:D1], Vs[:, j, u * HH:(u + 1) * HH, :],
                                    one[:].unsqueeze(2).broadcast_to([P, HH, D1]), ALU.mult)
                            v.then_inc(vm_ok, 1)
                            pool.wait_ge(vm_ok, 4 * b + 2 * u + 1)
                            for j in range(QT):
                                v = nc.gpsimd.tensor_tensor(
                                    to[:, j, :, D1:2 * D1], Vs[:, j, u * HH:(u + 1) * HH, :],
                                    to[:, j, :, 0:D1].bitcast(F), ALU.subtract)
                            v.then_inc(vm_ok, 1)

                        batch(0)
                        spread(0, 0)
                        spread(0, 1)
                        with pool.Fori(1, B) as b:
                            batch(b)
                            spread(b, 0)
                            spread(b, 1)

                    @block.tensor
                    def _(pe):
                        def project(b, g, i):
                            cols = bass.ds(b * S, S)
                            nc.tensor.matmul(pm[:], Wh[:, i, g, :], XTh[:, cols], start=True, stop=False)
                            nc.tensor.matmul(pm[:], Wl[:, i, g, :], XTh[:, cols], start=False, stop=False)
                            nc.tensor.matmul(pm[:], Wh[:, i, g, :], XTl[:, cols], start=False, stop=True).then_inc(proj_ok, 1)

                        def scores(b, h):
                            b, h, n = head(b, h)
                            p, r = h // G4 % 2, slice(h % G4 * 32, h % G4 * 32 + 32)
                            if h % G4 == 0:
                                pe.wait_ge(st_ok, 2 * (4 * b + h // G4) + 2)
                            for i in ORDER:
                                if not is_first(n) and i != 0:
                                    pe.wait_ge(max_ok, 4 * n - {3: 3, 2: 1, 1: 0}[i])
                                bank, at = bank_of[i]
                                w = (i + 1) * P
                                s = nc.tensor.matmul(bank[:, at:at + w], st[p][r, 1, i * P:w], st[p][r, 0, 0:w],
                                                     start=True, stop=True)
                                if i != 2:
                                    s.then_inc(s_ok, 1)

                        def values(b):
                            pe.wait_ge(xtc_ok, b + 1)
                            for j in range(QT):
                                o, t = pm[:, j * C:(j + 1) * C], slice(j * P, (j + 1) * P)
                                nc.tensor.matmul(o, XTc[:, 0, t], Vh[:], start=True, stop=False)
                                nc.tensor.matmul(o, XTc[:, 1, t], Vh[:], start=False, stop=False)
                                v = nc.tensor.matmul(o, XTc[:, 0, t], Vl[:], start=False, stop=True)
                            v.then_inc(v_ok, 1)

                        def turn(n, p, k):
                            pe.wait_ge(exp_ok, 4 * n + (1, 2, 4)[k])
                            if not is_first(n):
                                pe.wait_ge(lo_ok, 3 * n - 2 + k)
                            o = 0
                            for i in ((3,), (2,), (0, 1))[k]:
                                for j in range(i + 1):
                                    t = nc.tensor.transpose(pt[k][:, o:o + P],
                                                            prob[p][:, START[i] + j * P:START[i] + (j + 1) * P], ident[:])
                                    o += P
                            t.then_inc(t_ok, 1)

                        def mix(b, h, n):
                            u, hh = h // HH, h % HH
                            U = 2 * b + u
                            if hh == 0:
                                pe.wait_ge(vm_ok, 2 * U + 2)
                                if not is_first(U):
                                    pe.wait_ge(ot_ok, U)
                            for i, j in [(0, j) for j in (range(QT) if hh == 0 else (3, 2, 1, 0))] + [
                                    (1, j) for j in (3, 2, 1, 0)]:
                                if (hh == 0 and i == 0 and j == 0) or (not (hh == 0 and i == 0) and j in (3, 2, 1)):
                                    k = 3 if hh == 0 and i == 0 else {3: 1, 2: 2, 1: 3}[j]
                                    pe.wait_ge((hi_ok, lo_ok)[i], 3 * n + k)
                                m = nc.tensor.matmul(po[:, j * P:S], Vm[u][:, j, hh * P:(hh + 1) * P],
                                                     (PTh, PTl)[i][:, j, j * P:S], start=(hh == 0 and i == 0 and j == 0),
                                                     stop=(hh == HH - 1 and i == 1 and j == 0))
                            if hh == HH - 1:
                                m.then_inc(mix_ok, 1)

                        def back(U):
                            pe.wait_ge(ot_ok, U + 1)
                            for i in range(QT):
                                t = nc.tensor.transpose(pm[:, i * P:(i + 1) * P], OT[:, i * P:(i + 1) * P], ident[:])
                            t.then_inc(back_ok, 1)

                        def forth(U):
                            pe.wait_ge(o_ok, U + 1)
                            for i in range(QT):
                                t = nc.tensor.transpose(pm[:, i * P:(i + 1) * P],
                                                        O[:, i, :, :].rearrange("p h c -> p (h c)"), ident[:])
                            t.then_inc(fwd_ok, 1)

                        def out_project(U, u):
                            pe.wait_ge(otn_ok, U + 1)
                            for i in range(QT):
                                y = nc.tensor.matmul(pm[:, i * C:(i + 1) * C], OTn[:, i * P:(i + 1) * P], pd_sb[:, u, :],
                                                     start=True, stop=True)
                            y.then_inc(y_ok, 1)

                        def other(b, h):
                            U, hh = 2 * b + h // HH, h % HH
                            before = not is_first(U)
                            G = 2 * U + (1 if hh < 4 else 2)
                            gb, g = b + (h // G4 + 1) // 4, (h // G4 + 1) % 4
                            if hh in (0, 1, 4, 5) and not past(b, h // G4 * G4 + G4):
                                pe.wait_ge(st_ok, 2 * G + hh % 4)
                                if hh == 0 and h == HH and not past(b + 1, 0):
                                    pe.wait_ge(vs_ok, b + 2)
                                if hh == 0 and not is_first(U, 2):
                                    pe.wait_ge(x_ok, U - 1)
                                if hh == 4 and before:
                                    pe.wait_ge(otn_ok, U)
                                project(gb, g, hh % 4)
                            elif hh == 2 and before:
                                pe.wait_ge(st_ok, 4 * U + 4)
                                back(U - 1)
                            elif hh == 3 and before:
                                forth(U - 1)
                            elif hh == 6 and before:
                                if not past(b, h + 2):
                                    pe.wait_ge(st_ok, 4 * U + 6)
                                out_project(U - 1, 1 - h // HH)
                            elif h == 7 and not past(b + 1, 0):
                                pe.wait_ge(st_ok, 4 * U + 6)
                                if before:
                                    pe.wait_ge(x_ok, U)
                                values(b + 1)

                        def batch(b):
                            for h in range(H):
                                n, p = b * H + h, h % 2
                                turn(n, p, 0)
                                turn(n, p, 1)
                                other(b, h)
                                turn(n, p, 2)
                                if not past(b, h + 2):
                                    scores(b, h + 2)
                                mix(b, h, n)

                        project(0, 0, 0)
                        pe.wait_ge(st_ok, 1)
                        project(0, 0, 1)
                        scores(0, 0)
                        values(0)
                        scores(0, 1)
                        batch(0)
                        with pe.Fori(1, B - 1) as b:
                            batch(b)
                        batch(B - 1)
                        U = 2 * B - 1
                        pe.wait_ge(x_ok, U)
                        back(U)
                        forth(U)
                        out_project(U, 1)

                    @block.scalar
                    def _(act):
                        def low(b, g, i):
                            act.wait_ge(proj_ok, 2 * (4 * b + g) + i + 1)
                            nc.scalar.activation(Z[:], pm[:], ACT.Identity, bias=bz[:, i, g:g + 1],
                                                 scale=pk[:, i:i + 1]).then_inc(z_ok, 1)

                        def exponentials(b, h):
                            b, h, n = head(b, h)
                            p, u = h % 2, h // HH
                            for i in ORDER:
                                act.wait_ge(max_ok, 4 * n + ORDER.index(i) + 1)
                                s = prob[p][:, START[i]:START[i] + (i + 1) * P]
                                nc.scalar.activation(s, s, ACT.Exp, bias=negmax[p][:, i:i + 1], scale=-1.0,
                                                     accum_out=total[u][:, i, h % HH:h % HH + 1]).then_inc(exp_ok, 1)

                        def high(n, k):
                            act.wait_ge(t_ok, 3 * n + k + 1)
                            for o, m, at in COPIES[k]:
                                c = nc.scalar.activation(PTh[:, 0:m, at:at + P],
                                                         pt[k][:, o:o + m * P].rearrange("p (j q) -> p j q", j=m), ACT.Copy)
                            c.then_inc(hi_ok, 1)

                        def values(b):
                            act.wait_ge(v_ok, b + 1)
                            if not is_first(b):
                                act.wait_ge(vm_ok, 4 * b)
                            nc.scalar.activation(Vs[:].rearrange("p j h d -> p (j h d)"), pm[:], ACT.Copy).then_inc(vs_ok, 1)

                        def take(U):
                            act.wait_ge(mix_ok, U + 1)
                            nc.scalar.activation(OT[:], po[:], ACT.Copy).then_inc(ot_ok, 1)

                        def take_divided(U):
                            act.wait_ge(fwd_ok, U + 1)
                            nc.scalar.activation(OTn[:], pm[:], ACT.Copy).then_inc(otn_ok, 1)

                        def batch(b):
                            for h in range(H):
                                n, hh, U = b * H + h, h % HH, 2 * b + h // HH
                                before = not is_first(U)
                                if hh == 0 and before:
                                    take(U - 1)
                                high(n, 0)
                                high(n, 1)
                                high(n, 2)
                                if hh in (0, 1, 4, 5) and not past(b, h // G4 * G4 + G4):
                                    low(b + (h // G4 + 1) // 4, (h // G4 + 1) % 4, hh % 4)
                                if hh == 3 and before:
                                    take_divided(U - 1)
                                if h == 7 and not past(b + 1, 0):
                                    values(b + 1)
                                if not past(b, h + 1):
                                    exponentials(b, h + 1)

                        low(0, 0, 0)
                        low(0, 0, 1)
                        values(0)
                        exponentials(0, 0)
                        batch(0)
                        with act.Fori(1, B - 1) as b:
                            batch(b)
                        batch(B - 1)
                        take(2 * B - 1)
                        take_divided(2 * B - 1)

                    @block.vector
                    def _(dve):
                        def stack(b, g, i):
                            dve.wait_ge(z_ok, 2 * (4 * b + g) + i + 1)
                            nc.vector.scalar_tensor_tensor(st[g % 2][:, i, :], pm[:], bd[:, i, g:g + 1], Z[:].bitcast(F),
                                                           ALU.add, ALU.subtract).then_inc(st_ok, 1)

                        def maxima(b, h):
                            b, h, n = head(b, h)
                            p = h % 2
                            for i in ORDER:
                                bank, at = bank_of[i]
                                w = (i + 1) * P
                                if i != 0:
                                    dve.wait_ge(s_ok, 3 * n + {3: 1, 2: 2, 1: 3}[i])
                                    nc.vector.memset(tick[:, i:i + 1], 0.0)
                                nc.vector.tensor_tensor_reduce(
                                    out=prob[p][:, START[i]:START[i] + w], in0=bank[:, at:at + w],
                                    in1=bias[:, h, S - w:S], scale=-1.0, scalar=3e38,
                                    op0=ALU.add, op1=ALU.min, accum_out=negmax[p][:, i:i + 1]).then_inc(max_ok, 1)

                        def low(n, k):
                            dve.wait_ge(hi_ok, 3 * n + k + 1)
                            for o, m, at in COPIES[k]:
                                c = nc.vector.tensor_tensor(PTl[:, 0:m, at:at + P],
                                                            pt[k][:, o:o + m * P].rearrange("p (j q) -> p j q", j=m),
                                                            PTh[:, 0:m, at:at + P].bitcast(F), ALU.subtract)
                            c.then_inc(lo_ok, 1)

                        def divide(b, u):
                            U = 2 * b + u
                            dve.wait_ge(exp_ok, 32 * U + 32)
                            nc.vector.reciprocal(inv[:], total[u][:]).then_inc(inv_ok, 1)
                            dve.wait_ge(inv_ok, U + 1)
                            dve.wait_ge(back_ok, U + 1)
                            nc.vector.tensor_tensor(O[:].rearrange("p j h c -> p (j h) c"),
                                                    pm[:].rearrange("p (m c) -> p m c", c=2 * D1),
                                                    inv[:].rearrange("p j h -> p (j h)").unsqueeze(2).broadcast_to(
                                                        [P, QT * HH, 2 * D1]), ALU.mult).then_inc(o_ok, 1)

                        def add(b, U):
                            dve.wait_ge(y_ok, U + 1)
                            rows = x[:, bass.ds(b * QT, QT), :]
                            nc.vector.tensor_tensor(rows, rows, pm[:].rearrange("p (j c) -> p j c", c=C),
                                                    ALU.add).then_inc(x_ok, 1)
                            dve.wait_ge(x_ok, U + 1)

                        def batch(b):
                            for h in range(H):
                                n, hh, u = b * H + h, h % HH, h // HH
                                U = 2 * b + u
                                before = not is_first(U)
                                low(n, 0)
                                low(n, 1)
                                low(n, 2)
                                if hh in (0, 1, 4, 5) and not past(b, h // G4 * G4 + G4):
                                    stack(b + (h // G4 + 1) // 4, (h // G4 + 1) % 4, hh % 4)
                                if hh == 2 and before:
                                    divide(b - 1 + u, 1 - u)
                                if hh == 6 and before:
                                    add(b - 1 + u, U - 1)
                                if not past(b, h + 2):
                                    maxima(b, h + 2)

                        stack(0, 0, 0)
                        stack(0, 0, 1)
                        maxima(0, 0)
                        maxima(0, 1)
                        batch(0)
                        with dve.Fori(1, B - 1) as b:
                            batch(b)
                        batch(B - 1)
                        divide(B - 1, 1)
                        add(B - 1, 2 * B - 1)

        def moe(tag):
            with ExitStack() as ctx:
                idx = sbuf(ctx, f"{tag}idx", [P, TOPK, TILES], I32)
                wts = sbuf(ctx, f"{tag}wts", [P, TOPK, TILES])
                with ExitStack() as pre:
                    xn = sbuf(pre, f"{tag}rows", [P, TILES, C])
                    layernorm(f"{tag}n", keep=xn)
                    route(tag, pre, idx, wts)
                    dispatch(tag, idx, xn)
                experts(tag)
                combine(tag, idx, wts)

        def route(tag, ctx, idx, wts):
            wg = sbuf(ctx, f"{tag}wg", [P, P])
            wgh = sbuf(ctx, f"{tag}wgh", [P, P], FR)
            wgl = sbuf(ctx, f"{tag}wgl", [P, P], FR)
            bg = sbuf(ctx, f"{tag}bg", [P, E])
            lgT = sbuf(ctx, f"{tag}lgT", [P, 2, 512])
            shape = [P, TILES, E]
            LG, L2, EQ, OH1, OH2, LAB, SEQ, POS, TMP = (
                sbuf(ctx, f"{tag}{n}", shape) for n in ("LG", "L2", "EQ", "OH1", "OH2", "LAB", "SEQ", "POS", "TMP"))
            INC = sbuf(ctx, f"{tag}INC", shape)
            rank = sbuf(ctx, f"{tag}rank", [P, E])
            base = sbuf(ctx, f"{tag}base", [P, E])
            dump = sbuf(ctx, f"{tag}dump", [P, 1])
            upto = sbuf(ctx, f"{tag}upto", [P, P])
            ones = sbuf(ctx, f"{tag}ones", [P, P])
            m1, m2, r1, ex, s1 = (sbuf(ctx, f"{tag}{n}", [P, TILES]) for n in ("m1", "m2", "r1", "ex", "s1"))
            lt = banks(ctx, f"{tag}lt", 2)
            tl = banks(ctx, f"{tag}tl", 2)
            pc = banks(ctx, f"{tag}pc", 1)[0]
            w_in, made, w_ok, l_ok, lc_ok, t_ok, lg_ok, lab_ok, cum_ok, d_ok, e_ok, chain = sems(
                ctx, f"{tag}r", "w_in", "made", "w_ok", "l_ok", "lc_ok", "t_ok", "lg_ok", "lab_ok", "cum_ok", "d_ok",
                "e_ok", "chain")
            with nc.Block() as block:
                @block.sync
                def _(sp):
                    sp.wait_ge(made, 1)
                    sp.dma_start(wg[:, 0:E], wgate).then_inc(w_in, 16)
                    sp.dma_start(bg[:], bgate.broadcast_to([P, E])).then_inc(w_in, 16)
                    sp.wait_ge(w_in, 32)

                @block.gpsimd
                def _(pool):
                    nc.gpsimd.memset(wg[:], 0.0).then_inc(made, 1)
                    nc.gpsimd.memset(ones[:], 1.0).then_inc(made, 1)
                    nc.gpsimd.iota(rank[:], [[-1, E]], base=E, channel_multiplier=0,
                                   allow_small_or_imprecise_dtypes=True).then_inc(made, 1)
                    nc.gpsimd.iota(base[:], [[CAP, E]], base=-1, channel_multiplier=0,
                                   allow_small_or_imprecise_dtypes=True).then_inc(made, 1)
                    nc.gpsimd.iota(dump[:], [[0, 1]], base=SLOTS, channel_multiplier=1,
                                   allow_small_or_imprecise_dtypes=True).then_inc(made, 1)
                    pool.wait_ge(made, 2)
                    nc.gpsimd.affine_select(out=upto[:], in_=ones[:], compare_op=ALU.is_ge, fill=0.0, base=0,
                                            pattern=[[1, P]], channel_multiplier=-1).then_inc(made, 1)
                    pool.wait_ge(made, 6)

                @block.tensor
                def _(pe):
                    pe.wait_ge(w_ok, 2)

                    def logits(g, b):
                        if not isinstance(g, int) or g >= 2:
                            pe.wait_ge(lc_ok, g - 1)
                        cols = bass.ds(g * 512, 512)
                        nc.tensor.matmul(lt[b][:], wgh[:], XTh[:, cols], start=True, stop=False)
                        nc.tensor.matmul(lt[b][:], wgl[:], XTh[:, cols], start=False, stop=False)
                        nc.tensor.matmul(lt[b][:], wgh[:], XTl[:, cols], start=False, stop=True).then_inc(l_ok, 1)

                    def turn(g, b):
                        pe.wait_ge(lc_ok, g + 1)
                        if not isinstance(g, int) or g >= 2:
                            pe.wait_ge(lg_ok, g - 1)
                        for j in range(4):
                            t = nc.tensor.transpose(tl[b][:, j * P:(j + 1) * P], lgT[:, b, j * P:(j + 1) * P], ident[:])
                        t.then_inc(t_ok, 1)

                    logits(0, 0)
                    logits(1, 1)
                    turn(0, 0)
                    turn(1, 1)
                    with pe.Fori(1, GROUPS // 2) as m:
                        logits(2 * m, 0)
                        logits(2 * m + 1, 1)
                        turn(2 * m, 0)
                        turn(2 * m + 1, 1)
                    pe.wait_ge(lab_ok, 1)
                    pe.wait_ge(made, 6)
                    lab = LAB[:].rearrange("p t e -> p (t e)")
                    nc.tensor.matmul(pc[:, 0:256], upto[:], lab, start=True, stop=True)
                    nc.tensor.matmul(pc[:, 256:512], ones[:], lab, start=True, stop=True).then_inc(cum_ok, 1)

                @block.scalar
                def _(act):
                    with act.Fori(0, GROUPS // 2) as m:
                        for b in range(2):
                            act.wait_ge(l_ok, 2 * m + b + 1)
                            nc.scalar.activation(lgT[:, b, :], lt[b][:], ACT.Copy).then_inc(lc_ok, 1)
                    act.wait_ge(d_ok, 1)
                    nc.scalar.activation(ex[:], s1[:], ACT.Exp).then_inc(e_ok, 1)

                @block.vector
                def _(dve):
                    dve.wait_ge(w_in, 32)
                    nc.vector.tensor_copy(wgh[:], wg[:]).then_inc(w_ok, 1)
                    dve.wait_ge(w_ok, 1)
                    nc.vector.tensor_tensor(wgl[:], wg[:], wgh[:].bitcast(F), ALU.subtract).then_inc(w_ok, 1)
                    with dve.Fori(0, GROUPS // 2) as m:
                        for b in range(2):
                            dve.wait_ge(t_ok, 2 * m + b + 1)
                            nc.vector.tensor_tensor(LG[:, bass.ds(8 * m + 4 * b, 4), :],
                                                    tl[b][:].rearrange("p (j e) -> p j e", j=4)[:, :, 0:E],
                                                    bg[:].unsqueeze(1).broadcast_to([P, 4, E]), ALU.add).then_inc(lg_ok, 1)
                    dve.wait_ge(lg_ok, GROUPS)
                    dve.wait_ge(made, 6)
                    done = [0]

                    def link(ins):
                        done[0] += 1
                        ins.then_inc(chain, 1)
                        dve.wait_ge(chain, done[0])

                    def wide(v):
                        return v[:].unsqueeze(2).broadcast_to(shape)

                    def each(v):
                        return v[:].unsqueeze(1).broadcast_to(shape)

                    def best(L, m, OH):
                        link(nc.vector.tensor_reduce(m[:], L[:], AX.X, ALU.max))
                        link(nc.vector.tensor_tensor(EQ[:], L[:], wide(m), ALU.is_equal))
                        link(nc.vector.tensor_tensor(EQ[:], EQ[:], each(rank), ALU.mult))
                        link(nc.vector.tensor_reduce(r1[:], EQ[:], AX.X, ALU.max))
                        link(nc.vector.tensor_tensor(OH[:], EQ[:], wide(r1), ALU.is_equal))

                    best(LG, m1, OH1)
                    link(nc.vector.scalar_tensor_tensor(L2[:], OH1[:], -3e38, LG[:], ALU.mult, ALU.add))
                    best(L2, m2, OH2)
                    nc.vector.tensor_tensor(LAB[:], OH1[:], OH2[:], ALU.add).then_inc(lab_ok, 1)
                    nc.vector.tensor_tensor(s1[:], m2[:], m1[:], ALU.subtract).then_inc(d_ok, 1)
                    dve.wait_ge(e_ok, 1)
                    link(nc.vector.tensor_scalar(s1[:], ex[:], 1.0, None, ALU.add))
                    link(nc.vector.reciprocal(r1[:], s1[:]))
                    link(nc.vector.tensor_scalar(wts[:, 0, :], r1[:], 0.5, None, ALU.mult))
                    link(nc.vector.tensor_tensor(wts[:, 1, :], wts[:, 0, :], ex[:], ALU.mult))
                    dve.wait_ge(cum_ok, 1)
                    cum = pc[:, 0:256].rearrange("p (t e) -> p t e", e=E)
                    tot = pc[:, 256:512].rearrange("p (t e) -> p t e", e=E)
                    for e in range(E):
                        s = nc.vector.tensor_tensor_scan(INC[:, :, e], one[:].broadcast_to([P, TILES]), tot[:, :, e],
                                                         0.0, ALU.mult, ALU.add)
                    link(s)
                    link(nc.vector.tensor_tensor(SEQ[:], INC[:], cum, ALU.add))
                    link(nc.vector.tensor_tensor(SEQ[:], SEQ[:], tot, ALU.subtract))
                    link(nc.vector.tensor_tensor(POS[:], SEQ[:], each(base), ALU.add))
                    link(nc.vector.tensor_scalar(POS[:], POS[:], dump[:], None, ALU.subtract))
                    link(nc.vector.scalar_tensor_tensor(POS[:], SEQ[:], float(CAP), POS[:], ALU.is_le, ALU.mult))
                    link(nc.vector.tensor_scalar(POS[:], POS[:], dump[:], None, ALU.add))
                    for k, OH in ((0, OH1), (1, OH2)):
                        link(nc.vector.tensor_tensor(TMP[:], OH[:], POS[:], ALU.mult))
                        link(nc.vector.tensor_reduce(r1[:], TMP[:], AX.X, ALU.add))
                        link(nc.vector.tensor_copy(idx[:, k, :], r1[:]))

        def dispatch(tag, idx, xn):
            with ExitStack() as ctx:
                (sent,) = sems(ctx, f"{tag}d", "sent")
                with nc.Block() as block:
                    @block.gpsimd
                    def _(pool):
                        for t in range(TILES):
                            for k in range(TOPK):
                                nc.gpsimd.indirect_dma_start(
                                    slots_in, bass.IndirectOffsetOnAxis(ap=idx[:, k, t:t + 1], axis=0), xn[:, t, :], None,
                                    bounds_check=SLOTS - 1, oob_is_err=False).then_inc(sent, 16)
                        pool.wait_ge(sent, 16 * TILES * TOPK)

        def experts(tag):
            HALF = CAP // 2
            with ExitStack() as ctx:
                rows = [sbuf(ctx, f"{tag}in{i}", [P, ST, C]) for i in range(2)]
                DT = [sbuf(ctx, f"{tag}DT{i}", [P, CAP]) for i in range(2)]
                w1 = [sbuf(ctx, f"{tag}w1{i}", [P, HID1]) for i in range(2)]
                w2 = [sbuf(ctx, f"{tag}w2{i}", [P, HID1]) for i in range(2)]
                w3 = [sbuf(ctx, f"{tag}w3{i}", [P, HC1, C]) for i in range(2)]
                gate = sbuf(ctx, f"{tag}gate", [P, 2, HALF])
                hid = sbuf(ctx, f"{tag}hid", [P, HC1, CAP])
                res = [sbuf(ctx, f"{tag}res{i}", [P, ST, C]) for i in range(2)]
                pg = banks(ctx, f"{tag}pg", 2)
                pu = banks(ctx, f"{tag}pu", 2)
                pt = ctx.enter_context(nc.psum_tensor(f"{tag}pt", [P, 1024], F))
                po = ctx.enter_context(nc.psum_tensor(f"{tag}po", [P, 1024], F))
                t_ok, dt_ok, up_ok, silu_ok, hid_ok, down_ok, res_ok, *dmas = sems(
                    ctx, f"{tag}e", "t_ok", "dt_ok", "up_ok", "silu_ok", "hid_ok", "down_ok", "res_ok",
                    "w_in0", "w_in1", "row_in0", "row_in1", "stored0", "stored1")
                w_in, row_in, stored = dmas[0:2], dmas[2:4], dmas[4:6]

                def late(e, k):
                    return not isinstance(e, int) or e >= k

                def slots(buf, e):
                    return buf[bass.ds(e * CAP, CAP), :].rearrange("(j p) c -> p j c", p=P)

                with nc.Block() as block:
                    @block.sync
                    def _(sp):
                        def load(e, p):
                            if late(e, 2):
                                sp.wait_ge(t_ok, e - 1)
                            sp.dma_start(rows[p][:], slots(slots_in, e)).then_inc(row_in[p], 16)
                            if late(e, 2):
                                sp.wait_ge(down_ok, e - 1)
                            sp.dma_start(w1[p][:], W1[bass.ds(e, 1)].squeeze(0)).then_inc(w_in[p], 16)
                            sp.dma_start(w2[p][:], W2[bass.ds(e, 1)].squeeze(0)).then_inc(w_in[p], 16)
                            sp.dma_start(w3[p][:], W3[bass.ds(e, 1)].squeeze(0).rearrange(
                                "(c p) d -> p c d", p=P)).then_inc(w_in[p], 16)

                        load(0, 0)
                        load(1, 1)
                        with sp.Fori(1, E // 2) as m:
                            load(2 * m, 0)
                            load(2 * m + 1, 1)
                        for p in range(2):
                            sp.wait_ge(row_in[p], 16 * (E // 2))
                            sp.wait_ge(w_in[p], 48 * (E // 2))

                    @block.tensor
                    def _(pe):
                        def turn(e, p, m):
                            pe.wait_ge(row_in[p], 16 * m + 16)
                            if late(e, 1):
                                pe.wait_ge(dt_ok, e)
                            for j in range(ST):
                                t = nc.tensor.transpose(pt[:, j * P:(j + 1) * P], rows[p][:, j, :], ident[:])
                            t.then_inc(t_ok, 1)

                        def up(e, p, m):
                            pe.wait_ge(w_in[p], 48 * m + 48)
                            pe.wait_ge(dt_ok, e + 1)
                            for u in range(2 * HC1):
                                c, s = u // 2, slice(u % 2 * HALF, (u % 2 + 1) * HALF)
                                if late(e, 1) or u >= 2:
                                    pe.wait_ge(hid_ok, 2 * HC1 * e + u - 1)
                                w = slice(c * P, (c + 1) * P)
                                nc.tensor.matmul(pg[u % 2][:, 0:HALF], w1[p][:, w], DT[p][:, s], start=True,
                                                 stop=True).then_inc(up_ok, 1)
                                nc.tensor.matmul(pu[u % 2][:, 0:HALF], w2[p][:, w], DT[p][:, s], start=True,
                                                 stop=True).then_inc(up_ok, 1)

                        def down(e, p):
                            pe.wait_ge(hid_ok, 2 * HC1 * (e + 1))
                            if late(e, 1):
                                pe.wait_ge(res_ok, e)
                            for j in range(ST):
                                for c in range(HC1):
                                    d = nc.tensor.matmul(po[:, j * P:(j + 1) * P], hid[:, c, j * P:(j + 1) * P],
                                                         w3[p][:, c, :], start=(c == 0), stop=(c == HC1 - 1))
                            d.then_inc(down_ok, 1)

                        def pair(m):
                            for p in range(2):
                                up(2 * m + p, p, m)
                                turn(2 * m + p + 1, 1 - p, m + p)
                                down(2 * m + p, p)

                        turn(0, 0, 0)
                        pair(0)
                        with pe.Fori(1, E // 2 - 1) as m:
                            pair(m)
                        m = E // 2 - 1
                        up(E - 2, 0, m)
                        turn(E - 1, 1, m)
                        down(E - 2, 0)
                        up(E - 1, 1, m)
                        down(E - 1, 1)

                    @block.scalar
                    def _(act):
                        def turned(e, p):
                            act.wait_ge(t_ok, e + 1)
                            nc.scalar.activation(DT[p][:], pt[:, 0:CAP], ACT.Copy).then_inc(dt_ok, 1)

                        def silu(e):
                            for u in range(2 * HC1):
                                act.wait_ge(up_ok, 2 * (2 * HC1 * e + u) + 1)
                                if late(e, 1) or u >= 2:
                                    act.wait_ge(hid_ok, 2 * HC1 * e + u - 1)
                                nc.scalar.activation(gate[:, u % 2, :], pg[u % 2][:, 0:HALF], ACT.Silu).then_inc(silu_ok, 1)

                        def result(e, p, m):
                            act.wait_ge(down_ok, e + 1)
                            if late(e, 2):
                                act.wait_ge(stored[p], 16 * m)
                            nc.scalar.activation(res[p][:].rearrange("p j c -> p (j c)"), po[:, 0:CAP],
                                                 ACT.Copy).then_inc(res_ok, 1)
                            act.wait_ge(res_ok, e + 1)
                            act.dma_start(slots(slots_out, e), res[p][:]).then_inc(stored[p], 16)

                        turned(0, 0)
                        silu(0)
                        turned(1, 1)
                        result(0, 0, 0)
                        silu(1)
                        turned(2, 0)
                        result(1, 1, 0)
                        with act.Fori(1, E // 2 - 1) as m:
                            for p in range(2):
                                silu(2 * m + p)
                                turned(2 * m + p + 1, 1 - p)
                                result(2 * m + p, p, m)
                        m = E // 2 - 1
                        silu(E - 2)
                        turned(E - 1, 1)
                        result(E - 2, 0, m)
                        silu(E - 1)
                        result(E - 1, 1, m)
                        for p in range(2):
                            act.wait_ge(stored[p], 16 * (E // 2))

                    @block.vector
                    def _(dve):
                        def gated(e):
                            for u in range(2 * HC1):
                                c, s = u // 2, slice(u % 2 * HALF, (u % 2 + 1) * HALF)
                                dve.wait_ge(silu_ok, 2 * HC1 * e + u + 1)
                                dve.wait_ge(up_ok, 2 * (2 * HC1 * e + u) + 2)
                                nc.vector.tensor_tensor(hid[:, c, s], gate[:, u % 2, :], pu[u % 2][:, 0:HALF],
                                                        ALU.mult).then_inc(hid_ok, 1)
                        with dve.Fori(0, E) as e:
                            gated(e)

        def combine(tag, idx, wts):
            PART = 4
            with ExitStack() as ctx:
                got = sbuf(ctx, f"{tag}got", [P, TILES * TOPK, C])
                added, *arrived = sems(ctx, f"{tag}c", "added", *[f"arrived{i}" for i in range(TILES // PART)])
                with nc.Block() as block:
                    @block.gpsimd
                    def _(pool):
                        for t in range(TILES):
                            for k in range(TOPK):
                                n = t * TOPK + k
                                nc.gpsimd.indirect_dma_start(
                                    got[:, n, :], None, slots_out,
                                    bass.IndirectOffsetOnAxis(ap=idx[:, k, t:t + 1], axis=0)).then_inc(arrived[t // PART], 16)

                    @block.vector
                    def _(dve):
                        for t in range(TILES):
                            dve.wait_ge(arrived[t // PART], 16 * TOPK * PART)
                            for k in range(TOPK):
                                if k:
                                    dve.wait_ge(added, t * TOPK + k)
                                nc.vector.scalar_tensor_tensor(x[:, t, :], got[:, t * TOPK + k, :], wts[:, k, t:t + 1],
                                                               x[:, t, :], ALU.mult, ALU.add).then_inc(added, 1)


        layernorm("n1")
        ffn0("f1")
        layernorm("n2")
        attention("a0", D0, 1.0 / 8.0, wqT, wkT, wvT, wp, None, None, None, bp, table, None)
        layernorm("n3")
        ffn0("f2")
        moe("m1")
        layernorm("n5")
        narrow_attention("a1", float(1.0 / np.sqrt(np.float32(D1))), wkqv, bdup, b1, wproj, pdup, bproj, pick, slopes)
        moe("m2")

        with ExitStack() as ctx:
            (stored,) = sems(ctx, "st", "x")
            with nc.Block() as block:
                @block.sync
                def _(sp):
                    sp.dma_start(out.rearrange("(t p) c -> p t c", p=P), x[:]).then_inc(stored, 16)
                    sp.wait_ge(stored, 16)


def kernel(**inputs):
    import concourse.bacc as bacc
    from concourse.bass_utils import run_bass_kernel_spmd

    a = {k: np.asarray(v) for k, v in inputs.items()}
    bkqv = a["L1_attn_b_kqv"].reshape(3, H // 4, 4, 1, D1)
    rows = np.arange(P)
    arrays = {
        "x": a["L0_attn_x"].reshape(TOKENS, C),
        "wqT": a["L0_attn_Wq"].transpose(2, 0, 1),
        "wkT": a["L0_attn_Wk"].transpose(2, 0, 1),
        "wvT": a["L0_attn_Wv"].transpose(2, 0, 1),
        "wp": a["L0_attn_Wp"].reshape(H, D0, C).transpose(1, 0, 2),
        "bp": a["L0_attn_bp"].reshape(1, C),
        "table": a["L0_attn_rel_table"].reshape(1, -1),
        "wg0": a["L0_ffn_w_gate"].T,
        "wu0": a["L0_ffn_w_up"].T,
        "wd0": a["L0_ffn_w_down"].T,
        "wkqv": a["L1_attn_W_kqv"],
        "bdup": np.broadcast_to(bkqv[0:2], (2, H // 4, 4, 4, D1)).reshape(2, H // 4, P).transpose(2, 0, 1),
        "b1": bkqv[2].reshape(C, 1),
        "wproj": a["L1_attn_W_proj"],
        "pdup": np.broadcast_to(a["L1_attn_W_proj"].reshape(2, 8, 1, D1, C), (2, 8, 2, D1, C)).reshape(
            2, P, C).transpose(1, 0, 2),
        "bproj": a["L1_attn_b_proj"].reshape(1, C),
        "pick": np.stack([rows // D1 % 2, rows // D1 // 2 % 2], 1).astype(np.float32),
        "slopes": a["L1_attn_slopes"].reshape(1, H),
        "wgate": a["L1_ffn_Wg"],
        "bgate": a["L1_ffn_bg"].reshape(1, E),
        "W1": a["L1_ffn_W1"],
        "W2": a["L1_ffn_W2"],
        "W3": a["L1_ffn_W3"],
    }
    arrays = {k: np.ascontiguousarray(v) for k, v in arrays.items()}
    nc = bacc.Bacc("TRN2", target_bir_lowering=False, num_devices=1)
    handles = [nc.dram_tensor(f"in_{k}", v.shape, mybir.dt.from_np(v.dtype), kind="ExternalInput").ap()
               for k, v in arrays.items()]
    y = nc.dram_tensor("out_y", [TOKENS, C], F, kind="ExternalOutput").ap()
    program(nc, *handles, y)
    r = run_bass_kernel_spmd(nc, [{f"in_{k}": v for k, v in arrays.items()}], core_ids=[0])
    return r.results[0]["out_y"].reshape(B, S, C)
```

```python
from contextlib import ExitStack

import concourse.bass as bass
import concourse.mybir as mybir
import numpy as np

F = mybir.dt.float32
FR = mybir.dt.float32r
I32 = mybir.dt.int32
ALU = mybir.AluOpType
ACT = mybir.ActivationFunctionType
AX = mybir.AxisListType

P = 128
B, S, C = 8, 512, 128
TOKENS = B * S
TILES = TOKENS // P
GROUPS = TOKENS // 512
QT = S // P
H = 16
D0, D1 = 64, 8
HID0 = 384
HC0 = HID0 // P
E, TOPK, HID1 = 8, 2, 512
HC1 = HID1 // P
CAP = int(TOKENS / E * 1.25)
ST = CAP // P
SLOTS = E * CAP
EPS = 1e-5
NEG = -1e30
BAND = 257

ORDER = (3, 2, 0, 1)
START = {3: 0, 2: 512, 0: 896, 1: 1024}
WIDTH = S * (QT + 1) // 2
TGROUPS = ((3,), (2, 0), (1,))


class Parts:
    pass


def program(nc, x_in, wqT, wkT, wvT, wp, bp, table, wg0, wu0, wd0,
            wkqv, bdup, b1, wproj, pdup, bproj, pick, slopes, wgate, bgate, W1, W2, W3, out):
    top = ExitStack()

    def sbuf(ctx, name, shape, dt=F):
        return ctx.enter_context(nc.sbuf_tensor(name, shape, dt))

    def banks(ctx, name, n):
        return [ctx.enter_context(nc.psum_tensor(f"{name}{i}", [P, 512], F)) for i in range(n)]

    def sems(ctx, tag, *names):
        made = [nc.alloc_semaphore(name=f"{tag}_{n}") for n in names]

        def clear():
            nc.clear_and_free_semaphores(made)
            nc.all_engine_barrier()
        ctx.callback(clear)
        return made

    slots_in = nc.dram_tensor("slots_in", [SLOTS + P, C], F).ap()
    slots_out = nc.dram_tensor("slots_out", [SLOTS + P, C], F).ap()
    skew = nc.dram_tensor("skew", [H, P, BAND], F)

    with top:
        x = sbuf(top, "x", [P, TILES, C])
        ident = sbuf(top, "ident", [P, P])
        XTh = sbuf(top, "XTh", [P, TOKENS], FR)
        XTl = sbuf(top, "XTl", [P, TOKENS], FR)
        half = sbuf(top, "half", [P, TILES])
        one = sbuf(top, "one", [P, 1])

        zeros = sbuf(top, "zeros", [P, C])
        zeroed, *loaded = sems(top, "top", "zeroed", *[f"x{q}" for q in range(4)])

        with ExitStack() as ctx:
            (made,) = sems(ctx, "ld", "made")
            with nc.Block() as block:
                @block.sync
                def _(sp):
                    rows = x_in.rearrange("(t p) c -> p t c", p=P)
                    for q in range(4):
                        sp.dma_start(x[:, 8 * q:8 * q + 8, :], rows[:, 8 * q:8 * q + 8, :]).then_inc(loaded[q], 16)

                @block.gpsimd
                def _(pool):
                    nc.gpsimd.memset(ident[:], 0.0).then_inc(made, 1)
                    nc.gpsimd.memset(zeros[:], 0.0).then_inc(made, 1)
                    nc.gpsimd.memset(half[:], -0.5).then_inc(made, 1)
                    nc.gpsimd.memset(one[:], 1.0).then_inc(made, 1)
                    pool.wait_ge(made, 4)
                    nc.gpsimd.affine_select(out=ident[:], in_=ident[:], compare_op=ALU.not_equal, fill=1.0,
                                            base=0, pattern=[[-1, P]], channel_multiplier=1).then_inc(made, 1)
                    pool.wait_ge(made, 5)

        def norm_parts(ctx, tag, keep=None, pieces=2, loads=None):
            part = TILES // pieces
            st = sbuf(ctx, f"{tag}st", [P, TILES, 6])
            mv = sbuf(ctx, f"{tag}mv", [P, TILES, 2])
            ve = sbuf(ctx, f"{tag}ve", [P, TILES])
            rs = sbuf(ctx, f"{tag}rs", [P, TILES])
            t1 = sbuf(ctx, f"{tag}t1", [P, TILES])
            rstd = sbuf(ctx, f"{tag}rstd", [P, TILES])
            xn = sbuf(ctx, f"{tag}xn", [P, 2, 4, C]) if keep is None else None
            tp = banks(ctx, f"{tag}tp", 2)
            ve_ok, rs_ok, r_ok, chain, xn_ok, tp_ok, hi_ok, lo_ok = sems(
                ctx, tag, "ve_ok", "rs_ok", "r_ok", "chain", "xn_ok", "tp_ok", "hi_ok", "lo_ok")

            def early(g):
                return isinstance(g, int) and g < 2

            def stats(dve, first, end):
                for t in range(first, end):
                    if loads is not None and t % 8 == 0:
                        dve.wait_ge(loads[t // 8], 16)
                    nc.vector.bn_stats(st[:, t, :], x[:, t, :]).then_inc(chain, 1)

            def start(dve, h, with_stats=True):
                tiles = slice(h * part, (h + 1) * part)
                if with_stats:
                    stats(dve, h * part, (h + 1) * part)
                dve.wait_ge(chain, (2 * h + 1) * part)
                for t in range(TILES)[tiles]:
                    nc.vector.bn_aggr(mv[:, t, :], st[:, t, :]).then_inc(chain, 1)
                dve.wait_ge(chain, (2 * h + 2) * part)
                nc.vector.tensor_scalar(ve[:, tiles], mv[:, tiles, 1], EPS, None, ALU.add).then_inc(ve_ok, 1)

            def newton(dve, h):
                tiles = slice(h * part, (h + 1) * part)
                dve.wait_ge(rs_ok, h + 1)
                nc.vector.tensor_tensor(t1[:, tiles], rs[:, tiles], rs[:, tiles], ALU.mult).then_inc(r_ok, 1)
                dve.wait_ge(r_ok, 4 * h + 1)
                nc.vector.tensor_tensor(t1[:, tiles], t1[:, tiles], ve[:, tiles], ALU.mult).then_inc(r_ok, 1)
                dve.wait_ge(r_ok, 4 * h + 2)
                nc.vector.tensor_scalar(t1[:, tiles], t1[:, tiles], -0.5, 1.5, ALU.mult, ALU.add).then_inc(r_ok, 1)
                dve.wait_ge(r_ok, 4 * h + 3)
                nc.vector.tensor_tensor(rstd[:, tiles], rs[:, tiles], t1[:, tiles], ALU.mult).then_inc(r_ok, 1)
                dve.wait_ge(r_ok, 4 * h + 4)

            def power(pool, h):
                tiles = slice(h * part, (h + 1) * part)
                pool.wait_ge(ve_ok, h + 1)
                nc.gpsimd.tensor_tensor(rs[:, tiles], ve[:, tiles], half[:, tiles], ALU.pow).then_inc(rs_ok, 1)

            def normalise(dve, g, b):
                if not early(g) and keep is None:
                    dve.wait_ge(tp_ok, g - 1)
                for j in range(4):
                    dst = xn[:, b, j, :] if keep is None else keep[:, g * 4 + j, :]
                    n = nc.vector.tensor_scalar(dst, x[:, bass.ds(g * 4 + j, 1), :], mv[:, bass.ds(g * 4 + j, 1), 0],
                                                rstd[:, bass.ds(g * 4 + j, 1)], ALU.subtract, ALU.mult)
                n.then_inc(xn_ok, 1)

            def low(dve, g, b):
                dve.wait_ge(hi_ok, g + 1)
                nc.vector.tensor_tensor(XTl[:, bass.ds(g * 512, 512)], tp[b][:],
                                        XTh[:, bass.ds(g * 512, 512)].bitcast(F), ALU.subtract).then_inc(lo_ok, 1)

            def turn(pe, g, b):
                pe.wait_ge(xn_ok, g + 1)
                if not early(g):
                    pe.wait_ge(lo_ok, g - 1)
                for j in range(4):
                    src = xn[:, b, j, :] if keep is None else keep[:, g * 4 + j, :]
                    t = nc.tensor.transpose(tp[b][:, j * P:(j + 1) * P], src, ident[:])
                t.then_inc(tp_ok, 1)

            def high(act, g, b):
                act.wait_ge(tp_ok, g + 1)
                nc.scalar.activation(XTh[:, bass.ds(g * 512, 512)], tp[b][:], ACT.Copy).then_inc(hi_ok, 1)

            parts = Parts()
            parts.stats, parts.start, parts.newton, parts.power = stats, start, newton, power
            parts.normalise, parts.low, parts.turn, parts.high = normalise, low, turn, high
            parts.xn_ok, parts.lo_ok = xn_ok, lo_ok
            return parts

        def ffn0(tag, first=False):
            with ExitStack() as ctx:
                ln = norm_parts(ctx, f"{tag}n", pieces=4, loads=loaded if first else None)
                wi = sbuf(ctx, f"{tag}wi", [P, 3, HID0], I32)
                wf = sbuf(ctx, f"{tag}wf", [P, 3, HID0])
                wh = sbuf(ctx, f"{tag}wh", [P, 2, HID0], FR)
                wl = sbuf(ctx, f"{tag}wl", [P, 2, HID0], FR)
                act_sb = sbuf(ctx, f"{tag}act", [P, 2, 512])
                hid = sbuf(ctx, f"{tag}hid", [P, 2, HC0, 512])
                pg = banks(ctx, f"{tag}pg", 2)
                pu = banks(ctx, f"{tag}pu", 2)
                po = banks(ctx, f"{tag}po", 2)
                w_in, w_ok, up_ok, silu_ok, hid_ok, down_ok, x_ok = sems(
                    ctx, tag, "w_in", "w_ok", "up_ok", "silu_ok", "hid_ok", "down_ok", "x_ok")
                with nc.Block() as block:
                    @block.sync
                    def _(sp):
                        sp.dma_start(wi[:, 0, :], wg0).then_inc(w_in, 16)
                        sp.dma_start(wi[:, 1, :], wu0).then_inc(w_in, 16)
                        sp.dma_start(wi[:, 2, :].rearrange("p (c d) -> p c d", c=HC0),
                                     wd0.rearrange("(c p) d -> p c d", p=P)).then_inc(w_in, 16)
                        sp.wait_ge(w_in, 48)
                        if first:
                            for n in range(SLOTS // P):
                                sp.dma_start(slots_in[n * P:(n + 1) * P, :], zeros[:]).then_inc(zeroed, 16)
                            sp.dma_start(slots_out[SLOTS:SLOTS + P, :], zeros[:]).then_inc(zeroed, 16)

                    @block.gpsimd
                    def _(pool):
                        for q in range(4):
                            ln.power(pool, q)

                    @block.tensor
                    def _(pe):

                        def up(g, p):
                            pe.wait_ge(ln.lo_ok, g + 1)
                            for c in range(HC0):
                                b = (HC0 * p + c) % 2
                                cols = bass.ds(g * 512, 512)
                                if isinstance(g, int):
                                    if HC0 * g + c >= 2:
                                        pe.wait_ge(hid_ok, HC0 * g + c - 1)
                                else:
                                    pe.wait_ge(hid_ok, HC0 * g + c - 1)
                                w = slice(c * P, (c + 1) * P)
                                for i, bank in ((0, pg[b]), (1, pu[b])):
                                    nc.tensor.matmul(bank[:], wh[:, i, w], XTh[:, cols], start=True, stop=False)
                                    nc.tensor.matmul(bank[:], wl[:, i, w], XTh[:, cols], start=False, stop=False)
                                    nc.tensor.matmul(bank[:], wh[:, i, w], XTl[:, cols], start=False,
                                                     stop=True).then_inc(up_ok, 1)

                        def down(g, p):
                            pe.wait_ge(hid_ok, HC0 * g + HC0)
                            if not isinstance(g, int) or g >= 2:
                                pe.wait_ge(x_ok, g - 1)
                            for j in range(4):
                                for c in range(HC0):
                                    n = nc.tensor.matmul(po[p][:, j * P:(j + 1) * P], hid[:, p, c, j * P:(j + 1) * P],
                                                         wf[:, 2, c * P:(c + 1) * P], start=(c == 0), stop=(c == HC0 - 1))
                            n.then_inc(down_ok, 1)

                        ln.turn(pe, 0, 0)
                        ln.turn(pe, 1, 1)
                        pe.wait_ge(w_ok, 3)
                        up(0, 0)
                        ln.turn(pe, 2, 0)
                        up(1, 1)
                        down(0, 0)
                        ln.turn(pe, 3, 1)
                        up(2, 0)
                        down(1, 1)
                        with pe.Fori(1, GROUPS // 2 - 1) as m:
                            ln.turn(pe, 2 * m + 2, 0)
                            up(2 * m + 1, 1)
                            down(2 * m, 0)
                            ln.turn(pe, 2 * m + 3, 1)
                            up(2 * m + 2, 0)
                            down(2 * m + 1, 1)
                        up(GROUPS - 1, 1)
                        down(GROUPS - 2, 0)
                        down(GROUPS - 1, 1)

                    @block.scalar
                    def _(act):
                        def silu(g, p):
                            for c in range(HC0):
                                b = (HC0 * p + c) % 2
                                act.wait_ge(up_ok, 2 * (HC0 * g + c) + 1)
                                if not isinstance(g, int) or HC0 * g + c >= 2:
                                    act.wait_ge(hid_ok, HC0 * g + c - 1)
                                nc.scalar.activation(act_sb[:, b, :], pg[b][:], ACT.Silu).then_inc(silu_ok, 1)
                        ln.high(act, 0, 0)
                        ln.high(act, 1, 1)
                        silu(0, 0)
                        ln.high(act, 2, 0)
                        silu(1, 1)
                        with act.Fori(1, GROUPS // 2 - 1) as m:
                            ln.high(act, 2 * m + 1, 1)
                            silu(2 * m, 0)
                            ln.high(act, 2 * m + 2, 0)
                            silu(2 * m + 1, 1)
                        ln.high(act, GROUPS - 1, 1)
                        silu(GROUPS - 2, 0)
                        silu(GROUPS - 1, 1)

                    @block.vector
                    def _(dve):
                        ln.start(dve, 0)
                        ln.newton(dve, 0)
                        ln.normalise(dve, 0, 0)
                        ln.normalise(dve, 1, 1)
                        dve.wait_ge(w_in, 48)
                        nc.vector.tensor_scalar(wf[:], wi[:], float(np.float32(1.0 / 127.0)), None, ALU.mult).then_inc(w_ok, 1)
                        dve.wait_ge(w_ok, 1)
                        nc.vector.tensor_copy(wh[:], wf[:, 0:2, :]).then_inc(w_ok, 1)
                        dve.wait_ge(w_ok, 2)
                        nc.vector.tensor_tensor(wl[:], wf[:, 0:2, :], wh[:].bitcast(F), ALU.subtract).then_inc(w_ok, 1)

                        def gated(g, p, beside=None, chunks=range(HC0)):
                            for c in chunks:
                                if beside is not None:
                                    ln.stats(dve, beside + 3 * c, min(beside + 3 * c + 3, beside + 8))
                                b = (HC0 * p + c) % 2
                                dve.wait_ge(silu_ok, HC0 * g + c + 1)
                                dve.wait_ge(up_ok, 2 * (HC0 * g + c) + 2)
                                if c == 0 and (not isinstance(g, int) or g >= 2):
                                    dve.wait_ge(down_ok, g - 1)
                                nc.vector.tensor_tensor(hid[:, p, c, :], act_sb[:, b, :], pu[b][:],
                                                        ALU.mult).then_inc(hid_ok, 1)

                        def add(g, p):
                            dve.wait_ge(down_ok, g + 1)
                            rows = x[:, bass.ds(g * 4, 4), :]
                            nc.vector.scalar_tensor_tensor(rows, po[p][:].rearrange("p (j c) -> p j c", j=4), 0.5, rows,
                                                           ALU.mult, ALU.add).then_inc(x_ok, 1)

                        ln.low(dve, 0, 0)
                        ln.low(dve, 1, 1)
                        ln.start(dve, 1)
                        gated(0, 0, 16, range(HC0 - 1))
                        ln.newton(dve, 1)
                        ln.normalise(dve, 2, 0)
                        gated(0, 0, 16, range(HC0 - 1, HC0))
                        ln.start(dve, 2, with_stats=False)
                        ln.normalise(dve, 3, 1)
                        ln.low(dve, 2, 0)
                        gated(1, 1, 24)
                        ln.start(dve, 3, with_stats=False)
                        add(0, 0)
                        ln.newton(dve, 2)
                        ln.newton(dve, 3)
                        with dve.Fori(1, GROUPS // 2 - 1) as m:
                            gated(2 * m, 0)
                            ln.normalise(dve, 2 * m + 2, 0)
                            ln.low(dve, 2 * m + 1, 1)
                            add(2 * m - 1, 1)
                            gated(2 * m + 1, 1)
                            ln.normalise(dve, 2 * m + 3, 1)
                            ln.low(dve, 2 * m + 2, 0)
                            add(2 * m, 0)
                        ln.low(dve, GROUPS - 1, 1)
                        gated(GROUPS - 2, 0)
                        add(GROUPS - 3, 1)
                        gated(GROUPS - 1, 1)
                        add(GROUPS - 2, 0)
                        add(GROUPS - 1, 1)

        def add_row(pool, ln, row, done):
            for g in range(GROUPS):
                pool.wait_ge(ln.xn_ok, g + 1)
                r = x[:, g * 4:g * 4 + 4, :]
                nc.gpsimd.tensor_tensor(r, r, row[:].unsqueeze(1).broadcast_to([P, 4, C]), ALU.add).then_inc(done, 1)

        def wide_attention(tag, d, scale, q_w, k_w, v_w, p_w, p_bias, relative):
            STEPS = B * H
            with ExitStack() as ctx:
                Mh = sbuf(ctx, f"{tag}Mh", [P, H, C], FR)
                Ml = sbuf(ctx, f"{tag}Ml", [P, H, C], FR)
                Nh = sbuf(ctx, f"{tag}Nh", [P, H, C], FR)
                Nl = sbuf(ctx, f"{tag}Nl", [P, H, C], FR)
                bias = sbuf(ctx, f"{tag}bias", [P, H, S])

                with ExitStack() as pre:
                    ln = norm_parts(pre, f"{tag}n", pieces=4)
                    wq_sb = sbuf(pre, f"{tag}wq", [d, H, C])
                    wk_sb = sbuf(pre, f"{tag}wk", [d, H, C])
                    wv_sb = sbuf(pre, f"{tag}wv", [d, H, C])
                    wp_sb = sbuf(pre, f"{tag}wp", [d, H, C])
                    row = sbuf(pre, f"{tag}row", [P, C])
                    rel = sbuf(pre, f"{tag}rel", [P, 33 * H])
                    rows = sbuf(pre, f"{tag}rows", [P, H, BAND])
                    pm = banks(pre, f"{tag}pm", 2)
                    pn = banks(pre, f"{tag}pn", 2)
                    w_in, r_in, mat_ok, hi_ok, lo_ok, rows_ok, left_ok, b_ok, sk_out, sk_in = sems(
                        pre, f"{tag}p", "w_in", "r_in", "mat_ok", "hi_ok", "lo_ok", "rows_ok", "left_ok", "b_ok",
                        "sk_out", "sk_in")
                    tab = rel[:].rearrange("p (j h) -> p h j", h=H)
                    with nc.Block() as block:
                        @block.sync
                        def _(sp):
                            sp.dma_start(rel[:], relative.broadcast_to([P, relative.shape[1]])).then_inc(r_in, 16)
                            sp.dma_start(row[:], p_bias.broadcast_to([P, C])).then_inc(r_in, 16)
                            for dst, src in ((wq_sb, q_w), (wk_sb, k_w), (wv_sb, v_w), (wp_sb, p_w)):
                                sp.dma_start(dst[:], src).then_inc(w_in, 16)
                            sp.wait_ge(r_in, 32)
                            sp.wait_ge(w_in, 64)
                            sp.wait_ge(rows_ok, 2)
                            sp.dma_start(skew.ap().rearrange("h p c -> p h c"), rows[:]).then_inc(sk_out, 16)
                            sp.wait_ge(sk_out, 16)
                            shifted = bass.AP(skew, 0, [[BAND - 1, P], [P * BAND, H], [1, BAND - 1]])
                            sp.wait_ge(left_ok, 1)
                            sp.dma_start(bias[:, :, S - BAND + 1:S], shifted).then_inc(sk_in, 16)
                            sp.wait_ge(sk_in, 16)

                        @block.tensor
                        def _(pe):
                            ln.turn(pe, 0, 0)
                            ln.turn(pe, 1, 1)
                            pe.wait_ge(w_in, 64)
                            for g in range(GROUPS):
                                for b in range(2):
                                    h = 2 * g + b
                                    if h >= 2:
                                        pe.wait_ge(lo_ok, 2 * (h - 1))
                                    nc.tensor.matmul(pm[b][:, 0:C], wq_sb[:, h, :], wk_sb[:, h, :], start=True,
                                                     stop=True).then_inc(mat_ok, 1)
                                    nc.tensor.matmul(pn[b][:, 0:C], wv_sb[:, h, :], wp_sb[:, h, :], start=True,
                                                     stop=True).then_inc(mat_ok, 1)
                                if g + 2 < GROUPS:
                                    ln.turn(pe, g + 2, g % 2)

                        @block.scalar
                        def _(act):
                            act.wait_ge(r_in, 32)
                            nc.scalar.activation(bias[:, :, 0:S - BAND + 1],
                                                 tab[:, :, 0:1].broadcast_to([P, H, S - BAND + 1]),
                                                 ACT.Copy).then_inc(left_ok, 1)
                            for g in range(GROUPS):
                                ln.high(act, g, g % 2)
                                for b in range(2):
                                    h = 2 * g + b
                                    act.wait_ge(mat_ok, 2 * h + 1)
                                    nc.scalar.activation(Mh[:, h, :], pm[b][:, 0:C], ACT.Copy, scale=scale).then_inc(hi_ok, 1)
                                    act.wait_ge(mat_ok, 2 * h + 2)
                                    nc.scalar.activation(Nh[:, h, :], pn[b][:, 0:C], ACT.Copy).then_inc(hi_ok, 1)

                        @block.vector
                        def _(dve):
                            ln.start(dve, 0)
                            dve.wait_ge(r_in, 32)
                            nc.vector.tensor_copy(rows[:], tab[:, :, 0:1].broadcast_to([P, H, BAND])).then_inc(rows_ok, 1)
                            dve.wait_ge(rows_ok, 1)
                            nc.vector.tensor_copy(rows[:, :, P - 16 + 1:P + 1], tab[:, :, 1:17]).then_inc(rows_ok, 1)
                            ln.start(dve, 1)
                            ln.newton(dve, 0)
                            ln.normalise(dve, 0, 0)
                            ln.normalise(dve, 1, 1)
                            ln.start(dve, 2)
                            ln.newton(dve, 1)
                            for g in range(GROUPS):
                                if g == 1:
                                    ln.start(dve, 3)
                                elif g in (2, 4):
                                    ln.newton(dve, g // 2 + 1)
                                ln.low(dve, g, g % 2)
                                if g + 2 < GROUPS:
                                    ln.normalise(dve, g + 2, g % 2)
                                for b in range(2):
                                    h = 2 * g + b
                                    dve.wait_ge(hi_ok, 2 * h + 1)
                                    nc.vector.scalar_tensor_tensor(Ml[:, h, :], pm[b][:, 0:C], scale, Mh[:, h, :].bitcast(F),
                                                                   ALU.mult, ALU.subtract).then_inc(lo_ok, 1)
                                    dve.wait_ge(hi_ok, 2 * h + 2)
                                    nc.vector.tensor_tensor(Nl[:, h, :], pn[b][:, 0:C], Nh[:, h, :].bitcast(F),
                                                            ALU.subtract).then_inc(lo_ok, 1)

                        @block.gpsimd
                        def _(pool):
                            for q in range(4):
                                ln.power(pool, q)
                            pool.wait_ge(r_in, 32)
                            add_row(pool, ln, row, b_ok)
                            pool.wait_ge(sk_in, 16)
                            nc.gpsimd.affine_select(out=bias[:, :, S - P:S], in_=bias[:, :, S - P:S], compare_op=ALU.is_ge,
                                                    fill=NEG, base=0, pattern=[[0, H], [-1, P]],
                                                    channel_multiplier=1).then_inc(b_ok, 1)

                Mc = [sbuf(ctx, f"{tag}Mc{i}", [P, 2, C], FR) for i in range(2)]
                XTc = sbuf(ctx, f"{tag}XTc", [P, 2, S], FR)
                Gh = sbuf(ctx, f"{tag}Gh", [P, S], FR)
                Gl = sbuf(ctx, f"{tag}Gl", [P, S], FR)
                bc = [sbuf(ctx, f"{tag}bc{i}", [P, S]) for i in range(2)]
                prob = [sbuf(ctx, f"{tag}prob{i}", [P, WIDTH]) for i in range(2)]
                negmax = [sbuf(ctx, f"{tag}nm{i}", [P, QT]) for i in range(2)]
                total = [sbuf(ctx, f"{tag}tot{i}", [P, QT]) for i in range(2)]
                inv = [sbuf(ctx, f"{tag}inv{i}", [P, QT]) for i in range(2)]
                V = [sbuf(ctx, f"{tag}V{i}", [P, QT, 2, C]) for i in range(2)]
                PT = sbuf(ctx, f"{tag}PT", [P, WIDTH])
                tick = sbuf(ctx, f"{tag}tick", [1, 4])
                ps = banks(ctx, f"{tag}ps", 3)
                pt = banks(ctx, f"{tag}pt", 2)
                pg, pv, py = banks(ctx, f"{tag}pg", 3)
                names = ("bc_ok", "m_ok", "xt_ok", "g_ok", "gh_ok", "gl_ok", "s_ok", "max_ok", "exp_ok", "v_ok", "vc_ok",
                         "t_ok", "tc_ok", "y_ok", "inv_ok", "x_ok")
                (bc_ok, m_ok, xt_ok, g_ok, gh_ok, gl_ok, s_ok, max_ok, exp_ok, v_ok, vc_ok,
                 t_ok, tc_ok, y_ok, inv_ok, x_ok) = sems(ctx, tag, *names)
                bank_of = {3: (ps[0], 0), 2: (ps[1], 0), 0: (ps[1], 384), 1: (ps[2], 0)}

                def first(n, k=1):
                    return isinstance(n, int) and n < k

                with nc.Block() as block:
                    @block.gpsimd
                    def _(pool):
                        def copy(dst, src):
                            return nc.gpsimd.tensor_tensor(dst, src, one[:].broadcast_to([P, dst.shape[-1]]), ALU.mult)

                        def matrix(n, p):
                            if not first(n, 2):
                                pool.wait_ge(g_ok, n - 1)
                            for i, m in enumerate((Mh, Ml)):
                                c = copy(Mc[p][:, i, :], m[:, bass.ds(n % H, 1), :].squeeze(1).bitcast(F))
                            c.then_inc(m_ok, 1)

                        def batch(b):
                            if not first(b):
                                pool.wait_ge(v_ok, b * H)
                            copy(XTc[:, 0, :], XTh[:, bass.ds(b * S, S)].bitcast(F))
                            copy(XTc[:, 1, :], XTl[:, bass.ds(b * S, S)].bitcast(F)).then_inc(xt_ok, 1)

                        def step(n, p, last=False):
                            if not last:
                                matrix(n + 1, 1 - p)
                            if not first(n, 2):
                                pool.wait_ge(max_ok, 4 * n - 4)
                            copy(bc[p][:], bias[:, bass.ds(n % H, 1), :].squeeze(1)).then_inc(bc_ok, 1)

                        def rest(b, to):
                            with pool.Fori(1, to) as k:
                                step(b * H + 2 * k, 0)
                                step(b * H + 2 * k + 1, 1)

                        matrix(0, 0)
                        batch(0)
                        step(0, 0)
                        step(1, 1)
                        rest(0, H // 2)
                        with pool.Fori(1, B - 1) as b:
                            batch(b)
                            step(b * H, 0)
                            step(b * H + 1, 1)
                            rest(b, H // 2)
                        b = B - 1
                        batch(b)
                        step(b * H, 0)
                        step(b * H + 1, 1)
                        rest(b, H // 2 - 1)
                        step(STEPS - 2, 0)
                        step(STEPS - 1, 1, last=True)

                    @block.tensor
                    def _(pe):
                        def queries(n, p):
                            pe.wait_ge(m_ok, n + 1)
                            if not first(n):
                                pe.wait_ge(gl_ok, n)
                            cols = bass.ds((n // H) * S, S)
                            nc.tensor.matmul(pg[:], Mc[p][:, 0, :], XTh[:, cols], start=True, stop=False)
                            nc.tensor.matmul(pg[:], Mc[p][:, 1, :], XTh[:, cols], start=False, stop=False)
                            nc.tensor.matmul(pg[:], Mc[p][:, 0, :], XTl[:, cols], start=False, stop=True).then_inc(g_ok, 1)

                        def scores(n):
                            pe.wait_ge(gl_ok, n + 1)
                            for i in ORDER:
                                if not first(n) and i != 0:
                                    pe.wait_ge(max_ok, 4 * n - {3: 3, 2: 1, 1: 0}[i])
                                bank, at = bank_of[i]
                                q, w = slice(i * P, (i + 1) * P), (i + 1) * P
                                cols = bass.ds((n // H) * S, w)
                                o = bank[:, at:at + w]
                                nc.tensor.matmul(o, Gh[:, q], XTh[:, cols], start=True, stop=False)
                                nc.tensor.matmul(o, Gl[:, q], XTh[:, cols], start=False, stop=False)
                                s = nc.tensor.matmul(o, Gh[:, q], XTl[:, cols], start=False, stop=True)
                                if i != 2:
                                    s.then_inc(s_ok, 1)

                        def values(k, half):
                            pe.wait_ge(xt_ok, k // H + 1)
                            if not first(k):
                                pe.wait_ge(vc_ok, k)
                            h = bass.ds((k // 2 * 2) % H, 2)
                            for j in (2 * half, 2 * half + 1):
                                t = slice(j * P, (j + 1) * P)
                                o = pv[:, (j % 2) * 2 * C:(j % 2 + 1) * 2 * C]
                                nc.tensor.matmul(o, XTc[:, 0, t], Nh[:, h, :], start=True, stop=False)
                                nc.tensor.matmul(o, XTc[:, 1, t], Nh[:, h, :], start=False, stop=False)
                                v = nc.tensor.matmul(o, XTc[:, 0, t], Nl[:, h, :], start=False, stop=True)
                            v.then_inc(v_ok, 1)

                        def turn(n, p, k):
                            pe.wait_ge(exp_ok, 4 * n + (1, 3, 4)[k])
                            if k == 2 or not first(n):
                                pe.wait_ge(tc_ok, 3 * n + (0, 0, 1)[k])
                            o = 0
                            for i in TGROUPS[k]:
                                for j in range(i + 1):
                                    t = nc.tensor.transpose(pt[k % 2][:, o:o + P],
                                                            prob[p][:, START[i] + j * P:START[i] + (j + 1) * P], ident[:])
                                    o += P
                            t.then_inc(t_ok, 1)

                        def mix(n, p, vp, k):
                            if k == 0:
                                pe.wait_ge(vc_ok, n // 2 * 2 + 2)
                                if not first(n):
                                    pe.wait_ge(x_ok, n)
                            pe.wait_ge(tc_ok, 3 * n + k + 1)
                            for i in TGROUPS[k]:
                                o = py[:, i * C:(i + 1) * C]
                                for j in range(i + 1):
                                    b = slice(START[i] + j * P, START[i] + (j + 1) * P)
                                    y = nc.tensor.matmul(o, PT[:, b], V[vp][:, j, p, :], start=(j == 0), stop=(j == i))
                            if k == 2:
                                y.then_inc(y_ok, 1)

                        def step(n, r, last=False):
                            p, q, vp = r % 2, (r - 1) % 2, (r - 1) % 4 // 2
                            scores(n)
                            turn(n - 1, q, 0)
                            turn(n - 1, q, 1)
                            if not last:
                                queries(n + 1, 1 - p)
                            mix(n - 1, q, vp, 0)
                            turn(n - 1, q, 2)
                            if not last:
                                values(n + 1, 1 - p)
                            mix(n - 1, q, vp, 1)
                            mix(n - 1, q, vp, 2)

                        queries(0, 0)
                        scores(0)
                        queries(1, 1)
                        values(0, 0)
                        values(1, 1)
                        for n in range(1, 4):
                            step(n, n)
                        with pe.Fori(1, STEPS // 4 - 1) as m:
                            for r in range(4):
                                step(4 * m + r, r)
                        for r in range(4):
                            step(STEPS - 4 + r, r, last=(r == 3))
                        n = STEPS - 1
                        turn(n, 1, 0)
                        turn(n, 1, 1)
                        mix(n, 1, 1, 0)
                        turn(n, 1, 2)
                        mix(n, 1, 1, 1)
                        mix(n, 1, 1, 2)

                    @block.scalar
                    def _(act):
                        def query_hi(n):
                            act.wait_ge(g_ok, n + 1)
                            nc.scalar.activation(Gh[:], pg[:], ACT.Copy).then_inc(gh_ok, 1)

                        def values(k, vp, half):
                            act.wait_ge(v_ok, k + 1)
                            nc.scalar.activation(V[vp][:, 2 * half:2 * half + 2, :, :].rearrange("p j h c -> p (j h c)"),
                                                 pv[:], ACT.Copy).then_inc(vc_ok, 1)

                        def exponentials(n, p, tiles):
                            for i in tiles:
                                act.wait_ge(max_ok, 4 * n + ORDER.index(i) + 1)
                                if i == 3 and not first(n, 2):
                                    act.wait_ge(inv_ok, n - 1)
                                s = prob[p][:, START[i]:START[i] + (i + 1) * P]
                                nc.scalar.activation(s, s, ACT.Exp, bias=negmax[p][:, i:i + 1], scale=-1.0,
                                                     accum_out=total[p][:, i:i + 1]).then_inc(exp_ok, 1)

                        def turned(n, k):
                            act.wait_ge(t_ok, 3 * n + k + 1)
                            w = sum(i + 1 for i in TGROUPS[k]) * P
                            o = START[TGROUPS[k][0]]
                            nc.scalar.activation(PT[:, o:o + w], pt[k % 2][:, 0:w], ACT.Copy).then_inc(tc_ok, 1)

                        def step(n, r, last=False):
                            p = r % 2
                            exponentials(n, p, (3,))
                            turned(n - 1, 0)
                            turned(n - 1, 1)
                            exponentials(n, p, (2,))
                            if not last:
                                query_hi(n + 1)
                            exponentials(n, p, (0, 1))
                            turned(n - 1, 2)
                            if not last:
                                values(n + 1, (r + 1) % 4 // 2, 1 - p)

                        query_hi(0)
                        query_hi(1)
                        exponentials(0, 0, (3, 2))
                        values(0, 0, 0)
                        values(1, 0, 1)
                        exponentials(0, 0, (0, 1))
                        for n in range(1, 4):
                            step(n, n)
                        with act.Fori(1, STEPS // 4 - 1) as m:
                            for r in range(4):
                                step(4 * m + r, r)
                        for r in range(4):
                            step(STEPS - 4 + r, r, last=(r == 3))
                        for k in range(3):
                            turned(STEPS - 1, k)

                    @block.vector
                    def _(dve):
                        def query_lo(n):
                            dve.wait_ge(gh_ok, n + 1)
                            nc.vector.tensor_tensor(Gl[:], pg[:], Gh[:].bitcast(F), ALU.subtract).then_inc(gl_ok, 1)

                        def maxima(n, p, tiles=ORDER):
                            if tiles[0] == 3:
                                dve.wait_ge(bc_ok, n + 1)
                            for i in tiles:
                                bank, at = bank_of[i]
                                w = (i + 1) * P
                                if i != 0:
                                    dve.wait_ge(s_ok, 3 * n + {3: 1, 2: 2, 1: 3}[i])
                                    nc.vector.memset(tick[:, i:i + 1], 0.0)
                                nc.vector.tensor_tensor_reduce(
                                    out=prob[p][:, START[i]:START[i] + w], in0=bank[:, at:at + w],
                                    in1=bc[p][:, S - w:S], scale=-1.0, scalar=3e38,
                                    op0=ALU.add, op1=ALU.min, accum_out=negmax[p][:, i:i + 1]).then_inc(max_ok, 1)

                        def inverse(n, p):
                            dve.wait_ge(exp_ok, 4 * n + 4)
                            nc.vector.reciprocal(inv[p][:], total[p][:]).then_inc(inv_ok, 1)

                        def add(n, p):
                            dve.wait_ge(inv_ok, n + 1)
                            dve.wait_ge(y_ok, n + 1)
                            for i in range(QT):
                                r = x[:, bass.ds((n // H) * QT + i, 1), :]
                                a = nc.vector.scalar_tensor_tensor(r, py[:, i * C:(i + 1) * C], inv[p][:, i:i + 1], r,
                                                                   ALU.mult, ALU.add)
                            a.then_inc(x_ok, 1)

                        def step(n, p, last=False):
                            maxima(n, p, ORDER[:1])
                            if not first(n, 2):
                                add(n - 2, p)
                            maxima(n, p, ORDER[1:])
                            inverse(n - 1, 1 - p)
                            if not last:
                                query_lo(n + 1)

                        query_lo(0)
                        maxima(0, 0)
                        query_lo(1)
                        step(1, 1)
                        with dve.Fori(1, STEPS // 2 - 1) as m:
                            step(2 * m, 0)
                            step(2 * m + 1, 1)
                        step(STEPS - 2, 0)
                        step(STEPS - 1, 1, last=True)
                        add(STEPS - 2, 0)
                        inverse(STEPS - 1, 1)
                        add(STEPS - 1, 1)

        def narrow_attention(tag, scale, w_kqv, b_dup, v_bias, p_full, p_dup, p_bias, pick, slope, combining):
            G4, HH = 4, 8
            with ExitStack() as ctx:
                Wh = sbuf(ctx, f"{tag}Wh", [P, 2, G4, P], FR)
                Wl = sbuf(ctx, f"{tag}Wl", [P, 2, G4, P], FR)
                Vh = sbuf(ctx, f"{tag}Vwh", [P, C], FR)
                Vl = sbuf(ctx, f"{tag}Vwl", [P, C], FR)
                pd_sb = sbuf(ctx, f"{tag}pd", [P, 2, C])
                bias = sbuf(ctx, f"{tag}bias", [P, H, S])
                bd = sbuf(ctx, f"{tag}bd", [P, 2, G4])
                bz = sbuf(ctx, f"{tag}bz", [P, 2, G4])
                pk = sbuf(ctx, f"{tag}pk", [P, 2])
                Vm = [sbuf(ctx, f"{tag}Vm{i}", [P, QT, HH * (P + 16)], FR) for i in range(2)]

                with ExitStack() as pre:
                    sums = combining(pre)
                    ln = norm_parts(pre, f"{tag}n", pieces=4)
                    w_sb = sbuf(pre, f"{tag}w", [P, 3 * C])
                    row = sbuf(pre, f"{tag}row", [P, C])
                    rel = sbuf(pre, f"{tag}rel", [P, H])
                    dist = sbuf(pre, f"{tag}dist", [P, S])
                    bv_sb = sbuf(pre, f"{tag}bv", [P, 1])
                    bvx = sbuf(pre, f"{tag}bvx", [P, P])
                    pf_sb = sbuf(pre, f"{tag}pf", [P, C])
                    pb = banks(pre, f"{tag}pb", 1)[0]
                    w_in, b_ok, row_ok, chain = sems(pre, f"{tag}p", "w_in", "b_ok", "row_ok", "chain")
                    with nc.Block() as block:
                        @block.sync
                        def _(sp):
                            sp.dma_start(rel[:], slope.broadcast_to([P, H])).then_inc(w_in, 16)
                            sp.dma_start(w_sb[:], w_kqv).then_inc(w_in, 16)
                            sp.dma_start(bd[:], b_dup).then_inc(w_in, 16)
                            sp.dma_start(pk[:], pick).then_inc(w_in, 16)
                            sp.dma_start(bv_sb[:], v_bias).then_inc(w_in, 16)
                            sp.dma_start(pf_sb[:], p_full).then_inc(w_in, 16)
                            sp.dma_start(pd_sb[:], p_dup).then_inc(w_in, 16)
                            sp.dma_start(row[:], p_bias.broadcast_to([P, C])).then_inc(w_in, 16)
                            sp.wait_ge(w_in, 8 * 16)

                        @block.tensor
                        def _(pe):
                            pe.wait_ge(row_ok, 1)
                            nc.tensor.matmul(pb[:, 0:C], bvx[:], pf_sb[:], start=True, stop=True).then_inc(row_ok, 1)
                            for g in range(GROUPS):
                                ln.turn(pe, g, g % 2)

                        @block.scalar
                        def _(act):
                            for g in range(GROUPS):
                                ln.high(act, g, g % 2)

                        @block.vector
                        def _(dve):
                            for m in Vm:
                                nc.vector.memset(m[:].bitcast(F), 0.0).then_inc(chain, 1)
                            dve.wait_ge(w_in, 8 * 16)
                            nc.vector.tensor_copy(bvx[:], bv_sb[:].broadcast_to([P, P])).then_inc(row_ok, 1)
                            nc.vector.tensor_scalar(bd[:, 1, :], bd[:, 1, :], scale, None, ALU.mult).then_inc(chain, 1)
                            for i in range(2):
                                for g in range(G4):
                                    w = w_sb[:, i * C + g * 32:i * C + g * 32 + 32].rearrange("p (h d) -> p h d", d=D1)
                                    w = w.unsqueeze(2).broadcast_to([P, G4, 4, D1])
                                    hi = Wh[:, i, g, :].rearrange("p (h a d) -> p h a d", h=G4, a=4)
                                    lo = Wl[:, i, g, :].rearrange("p (h a d) -> p h a d", h=G4, a=4)
                                    f = scale if i else 1.0
                                    nc.vector.tensor_scalar(hi, w, f, None, ALU.mult).then_inc(chain, 1)
                                    dve.wait_ge(chain, 4 + i * G4 + g)
                                    for h in range(G4):
                                        nc.vector.scalar_tensor_tensor(lo[:, h], w[:, h], f, hi[:, h].bitcast(F), ALU.mult,
                                                                       ALU.subtract)
                            nc.vector.tensor_copy(Vh[:], w_sb[:, 2 * C:3 * C]).then_inc(chain, 1)
                            dve.wait_ge(chain, 12)
                            nc.vector.tensor_tensor(Vl[:], w_sb[:, 2 * C:3 * C], Vh[:].bitcast(F), ALU.subtract)
                            for i in range(2):
                                nc.vector.tensor_scalar(bz[:, i, :], bd[:, i, :], pk[:, i:i + 1], None, ALU.mult)
                            dve.wait_ge(b_ok, 1)
                            for h in range(H):
                                nb = nc.vector.tensor_scalar(bias[:, h, :], dist[:], rel[:, h:h + 1], None, ALU.mult)
                            nb.then_inc(b_ok, 1)
                            dve.wait_ge(row_ok, 2)
                            nc.vector.tensor_tensor(row[:], row[:], pb[:, 0:C], ALU.add).then_inc(row_ok, 1)

                            def piece(q):
                                ln.newton(dve, q)
                                for g in (2 * q, 2 * q + 1):
                                    ln.normalise(dve, g, g % 2)
                                for g in (2 * q, 2 * q + 1):
                                    dve.wait_ge(ln.xn_ok, g + 1)
                                    r = x[:, g * 4:g * 4 + 4, :]
                                    nc.vector.tensor_tensor(r, r, row[:].unsqueeze(1).broadcast_to([P, 4, C]),
                                                            ALU.add).then_inc(row_ok, 1)
                                    ln.low(dve, g, g % 2)

                            for q in range(4):
                                for part in (2 * q, 2 * q + 1):
                                    sums.add(dve, part)
                                    ln.stats(dve, part * 4, part * 4 + 4)
                                ln.start(dve, q, with_stats=False)
                                if q > 0:
                                    piece(q - 1)
                            piece(3)

                        @block.gpsimd
                        def _(pool):
                            nc.gpsimd.iota(dist[:], [[1, S]], base=-(S - P), channel_multiplier=-1,
                                           allow_small_or_imprecise_dtypes=True).then_inc(b_ok, 1)
                            for q in range(4):
                                sums.gather(pool, 8 * q, 8 * q + 8)
                                if q > 0:
                                    ln.power(pool, q - 1)
                            pool.wait_ge(b_ok, 2)
                            nc.gpsimd.affine_select(out=bias[:, :, S - P:S], in_=bias[:, :, S - P:S], compare_op=ALU.is_ge,
                                                    fill=NEG, base=0, pattern=[[0, H], [-1, P]],
                                                    channel_multiplier=1).then_inc(b_ok, 1)
                            ln.power(pool, 3)

                Z = sbuf(ctx, f"{tag}Z", [P, S], FR)
                st = [sbuf(ctx, f"{tag}st{i}", [P, 2, S], FR) for i in range(2)]
                XTc = sbuf(ctx, f"{tag}XTc", [P, 2, S], FR)
                Vs = sbuf(ctx, f"{tag}Vs", [P, QT, H, D1])
                prob = [sbuf(ctx, f"{tag}prob{i}", [P, WIDTH]) for i in range(2)]
                negmax = [sbuf(ctx, f"{tag}nm{i}", [P, QT]) for i in range(2)]
                total = [sbuf(ctx, f"{tag}tot{i}", [P, QT, HH]) for i in range(2)]
                inv = sbuf(ctx, f"{tag}inv", [P, QT, HH])
                LATE = S // 2
                PTh = sbuf(ctx, f"{tag}PTh", [P, QT, S - LATE], FR)
                PTl = sbuf(ctx, f"{tag}PTl", [P, QT, S - LATE], FR)
                PTf = sbuf(ctx, f"{tag}PTf", [P, 3 * P])
                OT = sbuf(ctx, f"{tag}OT", [P, S])
                O = sbuf(ctx, f"{tag}O", [P, QT, HH, 2 * D1])
                OTn = sbuf(ctx, f"{tag}OTn", [P, S])
                tick = sbuf(ctx, f"{tag}tick", [1, 4])
                ps = banks(ctx, f"{tag}ps", 3)
                pt = banks(ctx, f"{tag}pt", 3)
                po = banks(ctx, f"{tag}po", 1)[0]
                pm = banks(ctx, f"{tag}pm", 1)[0]
                names = ("xtc_ok", "proj_ok", "z_ok", "st_ok", "s_ok", "max_ok", "exp_ok", "t_ok", "hi_ok", "lo_ok",
                         "full_ok0", "full_ok1", "v_ok", "vs_ok", "vm_ok", "mix_ok", "ot_ok", "inv_ok", "back_ok", "o_ok", "fwd_ok", "otn_ok",
                         "y_ok", "x_ok")
                (xtc_ok, proj_ok, z_ok, st_ok, s_ok, max_ok, exp_ok, t_ok, hi_ok, lo_ok, full_ok0, full_ok1, v_ok, vs_ok, vm_ok, mix_ok,
                 ot_ok, inv_ok, back_ok, o_ok, fwd_ok, otn_ok, y_ok, x_ok) = sems(ctx, tag, *names)
                bank_of = {3: (ps[0], 0), 2: (ps[1], 0), 0: (ps[1], 384), 1: (ps[2], 0)}
                full_ok = (full_ok0, full_ok1)
                COPIES = {0: (4, 3 * P - LATE), 1: (3, 2 * P - LATE)}

                def is_first(n, k=1):
                    return isinstance(n, int) and n < k

                def head(b, h):
                    return b + h // H, h % H, b * H + h

                def past(b, h):
                    return isinstance(b, int) and b + h // H >= B

                with nc.Block() as block:
                    @block.gpsimd
                    def _(pool):
                        def copy(dst, src):
                            return nc.gpsimd.tensor_tensor(dst, src, one[:].broadcast_to([P, S]), ALU.mult)

                        def batch(b):
                            if not is_first(b):
                                pool.wait_ge(v_ok, b)
                            copy(XTc[:, 0, :], XTh[:, bass.ds(b * S, S)].bitcast(F))
                            copy(XTc[:, 1, :], XTl[:, bass.ds(b * S, S)].bitcast(F)).then_inc(xtc_ok, 1)

                        def spread(b, u):
                            if not is_first(b):
                                pool.wait_ge(mix_ok, 2 * b + u - 1)
                            if u == 0:
                                pool.wait_ge(vs_ok, b + 1)
                            to = Vm[u][:].rearrange("p j (h c) -> p j h c", h=HH)
                            for j in range(QT):
                                v = nc.gpsimd.tensor_tensor(
                                    to[:, j, :, 0:D1], Vs[:, j, u * HH:(u + 1) * HH, :],
                                    one[:].unsqueeze(2).broadcast_to([P, HH, D1]), ALU.mult)
                            v.then_inc(vm_ok, 1)
                            pool.wait_ge(vm_ok, 4 * b + 2 * u + 1)
                            for j in range(QT):
                                v = nc.gpsimd.tensor_tensor(
                                    to[:, j, :, D1:2 * D1], Vs[:, j, u * HH:(u + 1) * HH, :],
                                    to[:, j, :, 0:D1].bitcast(F), ALU.subtract)
                            v.then_inc(vm_ok, 1)

                        batch(0)
                        spread(0, 0)
                        spread(0, 1)
                        with pool.Fori(1, B) as b:
                            batch(b)
                            spread(b, 0)
                            spread(b, 1)

                    @block.tensor
                    def _(pe):
                        def project(b, g, i):
                            cols = bass.ds(b * S, S)
                            nc.tensor.matmul(pm[:], Wh[:, i, g, :], XTh[:, cols], start=True, stop=False)
                            nc.tensor.matmul(pm[:], Wl[:, i, g, :], XTh[:, cols], start=False, stop=False)
                            nc.tensor.matmul(pm[:], Wh[:, i, g, :], XTl[:, cols], start=False, stop=True).then_inc(proj_ok, 1)

                        def scores(b, h):
                            b, h, n = head(b, h)
                            p, r = h // G4 % 2, slice(h % G4 * 32, h % G4 * 32 + 32)
                            if h % G4 == 0:
                                pe.wait_ge(st_ok, 2 * (4 * b + h // G4) + 2)
                            for i in ORDER:
                                if not is_first(n) and i != 0:
                                    pe.wait_ge(max_ok, 4 * n - {3: 3, 2: 1, 1: 0}[i])
                                bank, at = bank_of[i]
                                w = (i + 1) * P
                                s = nc.tensor.matmul(bank[:, at:at + w], st[p][r, 1, i * P:w], st[p][r, 0, 0:w],
                                                     start=True, stop=True)
                                if i != 2:
                                    s.then_inc(s_ok, 1)

                        def values(b):
                            pe.wait_ge(xtc_ok, b + 1)
                            for j in range(QT):
                                o, t = pm[:, j * C:(j + 1) * C], slice(j * P, (j + 1) * P)
                                nc.tensor.matmul(o, XTc[:, 0, t], Vh[:], start=True, stop=False)
                                nc.tensor.matmul(o, XTc[:, 1, t], Vh[:], start=False, stop=False)
                                v = nc.tensor.matmul(o, XTc[:, 0, t], Vl[:], start=False, stop=True)
                            v.then_inc(v_ok, 1)

                        def turn(n, p, k, full=None):
                            pe.wait_ge(exp_ok, 4 * n + (1, 2, 4)[k])
                            if not is_first(n):
                                if k < 2:
                                    pe.wait_ge(lo_ok, 2 * n - 1 + k)
                                else:
                                    pe.wait_ge(full_ok[1 - p], full - 1 + p)
                            o = 0
                            for i in ((3,), (2,), (0, 1))[k]:
                                for j in range(i + 1):
                                    t = nc.tensor.transpose(pt[k][:, o:o + P],
                                                            prob[p][:, START[i] + j * P:START[i] + (j + 1) * P], ident[:])
                                    o += P
                            t.then_inc(t_ok, 1)

                        def mix(b, h, n):
                            u, hh = h // HH, h % HH
                            U = 2 * b + u
                            if hh == 0:
                                pe.wait_ge(vm_ok, 2 * U + 2)
                                if not is_first(U):
                                    pe.wait_ge(ot_ok, U)
                            for PT, ready in ((PTh, hi_ok), (PTl, lo_ok)):
                                for j in (0, 1, 2, 3) if hh == 0 and PT is PTh else (3, 2, 1, 0):
                                    if j == 3 and not (hh == 0 and PT is PTh):
                                        pe.wait_ge(ready, 2 * n + 1)
                                    elif j in (0, 2):
                                        pe.wait_ge(ready, 2 * n + 2)
                                    at = max(LATE, j * P)
                                    nc.tensor.matmul(po[:, at:S], Vm[u][:, j, hh * P:(hh + 1) * P], PT[:, j, at - LATE:],
                                                     start=(hh == 0 and PT is PTh and j == 0),
                                                     stop=False)
                            pe.wait_ge(full_ok[h % 2], 8 * b + h // 2 + 1)
                            for j in range(2):
                                m = nc.tensor.matmul(po[:, j * P:LATE], Vm[u][:, j, hh * P:(hh + 1) * P].bitcast(F),
                                                     PTf[:, 2 * j * P:(2 + j) * P], start=False,
                                                     stop=(hh == HH - 1 and j == 1))
                            if hh == HH - 1:
                                m.then_inc(mix_ok, 1)

                        def back(U):
                            pe.wait_ge(ot_ok, U + 1)
                            for i in range(QT):
                                t = nc.tensor.transpose(pm[:, i * P:(i + 1) * P], OT[:, i * P:(i + 1) * P], ident[:])
                            t.then_inc(back_ok, 1)

                        def forth(U):
                            pe.wait_ge(o_ok, U + 1)
                            for i in range(QT):
                                t = nc.tensor.transpose(pm[:, i * P:(i + 1) * P],
                                                        O[:, i, :, :].rearrange("p h c -> p (h c)"), ident[:])
                            t.then_inc(fwd_ok, 1)

                        def out_project(U, u):
                            pe.wait_ge(otn_ok, U + 1)
                            for i in range(QT):
                                y = nc.tensor.matmul(pm[:, i * C:(i + 1) * C], OTn[:, i * P:(i + 1) * P], pd_sb[:, u, :],
                                                     start=True, stop=True)
                            y.then_inc(y_ok, 1)

                        def other(b, h):
                            U, hh = 2 * b + h // HH, h % HH
                            before = not is_first(U)
                            G = 2 * U + (1 if hh < 4 else 2)
                            gb, g = b + (h // G4 + 1) // 4, (h // G4 + 1) % 4
                            if hh in (0, 1, 4, 5) and not past(b, h // G4 * G4 + G4):
                                pe.wait_ge(st_ok, 2 * G + hh % 4)
                                if hh == 0 and not before:
                                    pe.wait_ge(vs_ok, 1)
                                if hh == 0 and h == HH and not past(b + 1, 0):
                                    pe.wait_ge(vs_ok, b + 2)
                                if hh == 0 and not is_first(U, 2):
                                    pe.wait_ge(x_ok, U - 1)
                                if hh == 4 and before:
                                    pe.wait_ge(otn_ok, U)
                                project(gb, g, hh % 4)
                            elif hh == 2 and before:
                                pe.wait_ge(st_ok, 4 * U + 4)
                                back(U - 1)
                            elif hh == 3 and before:
                                forth(U - 1)
                            elif hh == 6 and before:
                                if not past(b, h + 2):
                                    pe.wait_ge(st_ok, 4 * U + 6)
                                out_project(U - 1, 1 - h // HH)
                            elif h == 7 and not past(b + 1, 0):
                                pe.wait_ge(st_ok, 4 * U + 6)
                                if before:
                                    pe.wait_ge(x_ok, U)
                                values(b + 1)

                        def batch(b):
                            for h in range(H):
                                n, p = b * H + h, h % 2
                                turn(n, p, 0)
                                turn(n, p, 1)
                                other(b, h)
                                turn(n, p, 2, 8 * b + h // 2 + 1)
                                if not past(b, h + 2):
                                    scores(b, h + 2)
                                mix(b, h, n)

                        project(0, 0, 0)
                        pe.wait_ge(st_ok, 1)
                        project(0, 0, 1)
                        scores(0, 0)
                        values(0)
                        scores(0, 1)
                        batch(0)
                        with pe.Fori(1, B - 1) as b:
                            batch(b)
                        batch(B - 1)
                        U = 2 * B - 1
                        pe.wait_ge(x_ok, U)
                        back(U)
                        forth(U)
                        out_project(U, 1)

                    @block.scalar
                    def _(act):
                        def low(b, g, i):
                            act.wait_ge(proj_ok, 2 * (4 * b + g) + i + 1)
                            nc.scalar.activation(Z[:], pm[:], ACT.Identity, bias=bz[:, i, g:g + 1],
                                                 scale=pk[:, i:i + 1]).then_inc(z_ok, 1)

                        def exponentials(b, h):
                            b, h, n = head(b, h)
                            p, u = h % 2, h // HH
                            for i in ORDER:
                                act.wait_ge(max_ok, 4 * n + ORDER.index(i) + 1)
                                s = prob[p][:, START[i]:START[i] + (i + 1) * P]
                                nc.scalar.activation(s, s, ACT.Exp, bias=negmax[p][:, i:i + 1], scale=-1.0,
                                                     accum_out=total[u][:, i, h % HH:h % HH + 1]).then_inc(exp_ok, 1)

                        def high(n, k):
                            act.wait_ge(t_ok, 3 * n + k + 1)
                            m, at = COPIES[k]
                            c = nc.scalar.activation(PTh[:, 0:m, at:at + P],
                                                     pt[k][:, 0:m * P].rearrange("p (j q) -> p j q", j=m), ACT.Copy)
                            c.then_inc(hi_ok, 1)

                        def values(b):
                            act.wait_ge(v_ok, b + 1)
                            if not is_first(b):
                                act.wait_ge(vm_ok, 4 * b)
                            nc.scalar.activation(Vs[:].rearrange("p j h d -> p (j h d)"), pm[:], ACT.Copy).then_inc(vs_ok, 1)

                        def take(U):
                            act.wait_ge(mix_ok, U + 1)
                            nc.scalar.activation(OT[:], po[:], ACT.Copy).then_inc(ot_ok, 1)

                        def take_divided(U):
                            act.wait_ge(fwd_ok, U + 1)
                            nc.scalar.activation(OTn[:], pm[:], ACT.Copy).then_inc(otn_ok, 1)

                        def batch(b):
                            for h in range(H):
                                n, hh, U = b * H + h, h % HH, 2 * b + h // HH
                                before = not is_first(U)
                                if hh == 0 and before:
                                    take(U - 1)
                                high(n, 0)
                                high(n, 1)
                                if h % 4 == 2:
                                    act.wait_ge(t_ok, 3 * n + 3)
                                    nc.scalar.activation(PTf[:], pt[2][:, 0:3 * P], ACT.Copy).then_inc(full_ok[0], 1)
                                if hh in (0, 1, 4, 5) and not past(b, h // G4 * G4 + G4):
                                    low(b + (h // G4 + 1) // 4, (h // G4 + 1) % 4, hh % 4)
                                if hh == 3 and before:
                                    take_divided(U - 1)
                                if h == 7 and not past(b + 1, 0):
                                    values(b + 1)
                                if not past(b, h + 1):
                                    exponentials(b, h + 1)

                        low(0, 0, 0)
                        low(0, 0, 1)
                        exponentials(0, 0)
                        values(0)
                        batch(0)
                        with act.Fori(1, B - 1) as b:
                            batch(b)
                        batch(B - 1)
                        take(2 * B - 1)
                        take_divided(2 * B - 1)

                    @block.vector
                    def _(dve):
                        def stack(b, g, i):
                            dve.wait_ge(z_ok, 2 * (4 * b + g) + i + 1)
                            nc.vector.scalar_tensor_tensor(st[g % 2][:, i, :], pm[:], bd[:, i, g:g + 1], Z[:].bitcast(F),
                                                           ALU.add, ALU.subtract).then_inc(st_ok, 1)

                        def maxima(b, h):
                            b, h, n = head(b, h)
                            p = h % 2
                            for i in ORDER:
                                bank, at = bank_of[i]
                                w = (i + 1) * P
                                if i != 0:
                                    dve.wait_ge(s_ok, 3 * n + {3: 1, 2: 2, 1: 3}[i])
                                    nc.vector.memset(tick[:, i:i + 1], 0.0)
                                nc.vector.tensor_tensor_reduce(
                                    out=prob[p][:, START[i]:START[i] + w], in0=bank[:, at:at + w],
                                    in1=bias[:, h, S - w:S], scale=-1.0, scalar=3e38,
                                    op0=ALU.add, op1=ALU.min, accum_out=negmax[p][:, i:i + 1]).then_inc(max_ok, 1)

                        def low(n, k):
                            dve.wait_ge(hi_ok, 2 * n + k + 1)
                            m, at = COPIES[k]
                            c = nc.vector.tensor_tensor(PTl[:, 0:m, at:at + P],
                                                        pt[k][:, 0:m * P].rearrange("p (j q) -> p j q", j=m),
                                                        PTh[:, 0:m, at:at + P].bitcast(F), ALU.subtract)
                            c.then_inc(lo_ok, 1)

                        def divide(b, u):
                            U = 2 * b + u
                            dve.wait_ge(exp_ok, 32 * U + 32)
                            nc.vector.reciprocal(inv[:], total[u][:]).then_inc(inv_ok, 1)
                            dve.wait_ge(inv_ok, U + 1)
                            dve.wait_ge(back_ok, U + 1)
                            nc.vector.tensor_tensor(O[:].rearrange("p j h c -> p (j h) c"),
                                                    pm[:].rearrange("p (m c) -> p m c", c=2 * D1),
                                                    inv[:].rearrange("p j h -> p (j h)").unsqueeze(2).broadcast_to(
                                                        [P, QT * HH, 2 * D1]), ALU.mult).then_inc(o_ok, 1)

                        def add(b, U):
                            dve.wait_ge(y_ok, U + 1)
                            rows = x[:, bass.ds(b * QT, QT), :]
                            nc.vector.tensor_tensor(rows, rows, pm[:].rearrange("p (j c) -> p j c", c=C),
                                                    ALU.add).then_inc(x_ok, 1)
                            dve.wait_ge(x_ok, U + 1)

                        def batch(b):
                            for h in range(H):
                                n, hh, u = b * H + h, h % HH, h // HH
                                U = 2 * b + u
                                before = not is_first(U)
                                low(n, 0)
                                low(n, 1)
                                if h % 4 != 2:
                                    dve.wait_ge(t_ok, 3 * n + 3)
                                    nc.vector.tensor_copy(PTf[:], pt[2][:, 0:3 * P]).then_inc(full_ok[h % 2], 1)
                                if hh in (0, 1, 4, 5) and not past(b, h // G4 * G4 + G4):
                                    stack(b + (h // G4 + 1) // 4, (h // G4 + 1) % 4, hh % 4)
                                if hh == 2 and before:
                                    divide(b - 1 + u, 1 - u)
                                if hh == 6 and before:
                                    add(b - 1 + u, U - 1)
                                if not past(b, h + 2):
                                    maxima(b, h + 2)

                        stack(0, 0, 0)
                        stack(0, 0, 1)
                        maxima(0, 0)
                        maxima(0, 1)
                        batch(0)
                        with dve.Fori(1, B - 1) as b:
                            batch(b)
                        batch(B - 1)
                        divide(B - 1, 1)
                        add(B - 1, 2 * B - 1)

        def moe(tag, follow):
            with ExitStack() as ctx:
                idx = sbuf(ctx, f"{tag}idx", [P, TOPK, TILES], I32)
                wts = sbuf(ctx, f"{tag}wts", [P, TOPK, TILES])
                with ExitStack() as pre:
                    xn = sbuf(pre, f"{tag}rows", [P, TILES, C])
                    (sent,) = sems(pre, f"{tag}s", "sent")

                    def send(pool, first, end):
                        for t in range(first, end):
                            for k in range(TOPK):
                                nc.gpsimd.indirect_dma_start(
                                    slots_in, bass.IndirectOffsetOnAxis(ap=idx[:, k, t:t + 1], axis=0), xn[:, t, :], None,
                                    bounds_check=SLOTS - 1, oob_is_err=False).then_inc(sent, 16)
                    with ExitStack() as routing:
                        route(tag, routing, xn, idx, wts, send)
                    experts(tag, sent, send)
                follow(lambda c: combine_parts(c, tag, idx, wts))

        def route(tag, ctx, xn, idx, wts, send):
            QUARTERS, PER = 4, TILES // 4
            ln = norm_parts(ctx, f"{tag}n", keep=xn, pieces=QUARTERS)
            wg = sbuf(ctx, f"{tag}wg", [P, P])
            wgh = sbuf(ctx, f"{tag}wgh", [P, P], FR)
            wgl = sbuf(ctx, f"{tag}wgl", [P, P], FR)
            bg = sbuf(ctx, f"{tag}bg", [P, E])
            lgT = sbuf(ctx, f"{tag}lgT", [P, 2, 512])
            shape = [P, TILES, E]
            LG, L2, EQ, OH1, OH2, LAB, SEQ, POS, TMP = (
                sbuf(ctx, f"{tag}{n}", shape) for n in ("LG", "L2", "EQ", "OH1", "OH2", "LAB", "SEQ", "POS", "TMP"))
            INC = sbuf(ctx, f"{tag}INC", shape)
            rank = sbuf(ctx, f"{tag}rank", [P, E])
            base = sbuf(ctx, f"{tag}base", [P, E])
            dump = sbuf(ctx, f"{tag}dump", [P, 1])
            upto = sbuf(ctx, f"{tag}upto", [P, P])
            ones = sbuf(ctx, f"{tag}ones", [P, P])
            m1, m2, r1, ex, s1 = (sbuf(ctx, f"{tag}{n}", [P, TILES]) for n in ("m1", "m2", "r1", "ex", "s1"))
            lt = banks(ctx, f"{tag}lt", 2)
            tl = banks(ctx, f"{tag}tl", 2)
            pc = banks(ctx, f"{tag}pc", 2)
            w_in, made, w_ok, l_ok, lc_ok, t_ok, lg_ok, lab_ok, cum_ok, idx_ok, d_ok, e_ok, chain = sems(
                ctx, f"{tag}r", "w_in", "made", "w_ok", "l_ok", "lc_ok", "t_ok", "lg_ok", "lab_ok", "cum_ok", "idx_ok", "d_ok",
                "e_ok", "chain")
            with nc.Block() as block:
                @block.sync
                def _(sp):
                    sp.wait_ge(made, 1)
                    sp.dma_start(wg[:, 0:E], wgate).then_inc(w_in, 16)
                    sp.dma_start(bg[:], bgate.broadcast_to([P, E])).then_inc(w_in, 16)
                    sp.wait_ge(w_in, 32)

                @block.gpsimd
                def _(pool):
                    nc.gpsimd.memset(wg[:], 0.0).then_inc(made, 1)
                    nc.gpsimd.memset(ones[:], 1.0).then_inc(made, 1)
                    nc.gpsimd.iota(rank[:], [[-1, E]], base=E, channel_multiplier=0,
                                   allow_small_or_imprecise_dtypes=True).then_inc(made, 1)
                    nc.gpsimd.iota(base[:], [[CAP, E]], base=-1, channel_multiplier=0,
                                   allow_small_or_imprecise_dtypes=True).then_inc(made, 1)
                    nc.gpsimd.iota(dump[:], [[0, 1]], base=SLOTS, channel_multiplier=1,
                                   allow_small_or_imprecise_dtypes=True).then_inc(made, 1)
                    pool.wait_ge(made, 2)
                    nc.gpsimd.affine_select(out=upto[:], in_=ones[:], compare_op=ALU.is_ge, fill=0.0, base=0,
                                            pattern=[[1, P]], channel_multiplier=-1).then_inc(made, 1)
                    pool.wait_ge(made, 6)
                    ln.power(pool, 0)
                    ln.power(pool, 1)
                    ln.power(pool, 2)
                    pool.wait_ge(zeroed, 16 * (SLOTS // P + 1))
                    for q in range(QUARTERS - 1):
                        pool.wait_ge(idx_ok, q + 1)
                        send(pool, q * PER, (q + 1) * PER)
                        if q == 0:
                            ln.power(pool, 3)

                @block.tensor
                def _(pe):
                    def logits(g, b):
                        if not isinstance(g, int) or g >= 2:
                            pe.wait_ge(lc_ok, g - 1)
                        pe.wait_ge(ln.lo_ok, g + 1)
                        cols = bass.ds(g * 512, 512)
                        nc.tensor.matmul(lt[b][:], wgh[:], XTh[:, cols], start=True, stop=False)
                        nc.tensor.matmul(lt[b][:], wgl[:], XTh[:, cols], start=False, stop=False)
                        nc.tensor.matmul(lt[b][:], wgh[:], XTl[:, cols], start=False, stop=True).then_inc(l_ok, 1)

                    def turn(g, b):
                        pe.wait_ge(lc_ok, g + 1)
                        if not isinstance(g, int) or g >= 2:
                            pe.wait_ge(lg_ok, g - 1)
                        for j in range(4):
                            t = nc.tensor.transpose(tl[b][:, j * P:(j + 1) * P], lgT[:, b, j * P:(j + 1) * P], ident[:])
                        t.then_inc(t_ok, 1)

                    for q in range(QUARTERS):
                        for g in (2 * q, 2 * q + 1):
                            ln.turn(pe, g, g % 2)
                        if q == 0:
                            pe.wait_ge(w_ok, 2)
                        for g in (2 * q, 2 * q + 1):
                            logits(g, g % 2)
                        for g in (2 * q, 2 * q + 1):
                            turn(g, g % 2)
                        pe.wait_ge(lab_ok, q + 1)
                        if q == 0:
                            pe.wait_ge(made, 6)
                        lab = LAB[:, q * PER:(q + 1) * PER, :].rearrange("p t e -> p (t e)")
                        o = pc[q % 2]
                        nc.tensor.matmul(o[:, 0:PER * E], upto[:], lab, start=True, stop=True)
                        nc.tensor.matmul(o[:, PER * E:2 * PER * E], ones[:], lab, start=True, stop=True).then_inc(cum_ok, 1)

                @block.scalar
                def _(act):
                    for q in range(QUARTERS):
                        for g in (2 * q, 2 * q + 1):
                            ln.high(act, g, g % 2)
                        for g in (2 * q, 2 * q + 1):
                            act.wait_ge(l_ok, g + 1)
                            if g >= 2:
                                act.wait_ge(t_ok, g - 1)
                            nc.scalar.activation(lgT[:, g % 2, :], lt[g % 2][:], ACT.Copy).then_inc(lc_ok, 1)
                    act.wait_ge(d_ok, 1)
                    nc.scalar.activation(ex[:], s1[:], ACT.Exp).then_inc(e_ok, 1)

                @block.vector
                def _(dve):
                    ln.start(dve, 0)
                    dve.wait_ge(w_in, 32)
                    nc.vector.tensor_copy(wgh[:], wg[:]).then_inc(w_ok, 1)
                    dve.wait_ge(w_ok, 1)
                    nc.vector.tensor_tensor(wgl[:], wg[:], wgh[:].bitcast(F), ALU.subtract).then_inc(w_ok, 1)
                    done = [0]

                    def link(ins):
                        done[0] += 1
                        ins.then_inc(chain, 1)
                        dve.wait_ge(chain, done[0])

                    def places(q):
                        T = slice(q * PER, (q + 1) * PER)
                        shape = [P, PER, E]

                        def wide(v):
                            return v[:, T].unsqueeze(2).broadcast_to(shape)

                        def each(v):
                            return v.unsqueeze(1).broadcast_to(shape)

                        def best(L, m, OH):
                            link(nc.vector.tensor_reduce(m[:, T], L[:, T], AX.X, ALU.max))
                            link(nc.vector.tensor_tensor(EQ[:, T], L[:, T], wide(m), ALU.is_equal))
                            link(nc.vector.tensor_tensor(EQ[:, T], EQ[:, T], each(rank[:]), ALU.mult))
                            link(nc.vector.tensor_reduce(r1[:, T], EQ[:, T], AX.X, ALU.max))
                            link(nc.vector.tensor_tensor(OH[:, T], EQ[:, T], wide(r1), ALU.is_equal))

                        best(LG, m1, OH1)
                        link(nc.vector.scalar_tensor_tensor(L2[:, T], OH1[:, T], -3e38, LG[:, T], ALU.mult, ALU.add))
                        best(L2, m2, OH2)
                        nc.vector.tensor_tensor(LAB[:, T], OH1[:, T], OH2[:, T], ALU.add).then_inc(lab_ok, 1)
                        dve.wait_ge(cum_ok, q + 1)
                        cum = pc[q % 2][:, 0:PER * E].rearrange("p (t e) -> p t e", e=E)
                        tot = pc[q % 2][:, PER * E:2 * PER * E].rearrange("p (t e) -> p t e", e=E)
                        for e in range(E):
                            s = nc.vector.tensor_tensor_scan(INC[:, T, e], one[:].broadcast_to([P, PER]), tot[:, :, e],
                                                             0.0, ALU.mult, ALU.add)
                        link(s)
                        if q > 0:
                            link(nc.vector.tensor_tensor(INC[:, T], INC[:, T], each(INC[:, q * PER - 1, :]), ALU.add))
                        link(nc.vector.tensor_tensor(SEQ[:, T], INC[:, T], cum, ALU.add))
                        link(nc.vector.tensor_tensor(SEQ[:, T], SEQ[:, T], tot, ALU.subtract))
                        link(nc.vector.tensor_tensor(POS[:, T], SEQ[:, T], each(base[:]), ALU.add))
                        link(nc.vector.tensor_scalar(POS[:, T], POS[:, T], dump[:], None, ALU.subtract))
                        link(nc.vector.scalar_tensor_tensor(POS[:, T], SEQ[:, T], float(CAP), POS[:, T], ALU.is_le, ALU.mult))
                        link(nc.vector.tensor_scalar(POS[:, T], POS[:, T], dump[:], None, ALU.add))
                        for k, OH in ((0, OH1), (1, OH2)):
                            link(nc.vector.tensor_tensor(TMP[:, T], OH[:, T], POS[:, T], ALU.mult))
                            link(nc.vector.tensor_reduce(r1[:, T], TMP[:, T], AX.X, ALU.add))
                            i = nc.vector.tensor_copy(idx[:, k, T], r1[:, T])
                            if k == 0:
                                link(i)
                        i.then_inc(idx_ok, 1)

                    ln.start(dve, 1)
                    for q in range(QUARTERS):
                        ln.newton(dve, q)
                        for g in (2 * q, 2 * q + 1):
                            ln.normalise(dve, g, g % 2)
                        for g in (2 * q, 2 * q + 1):
                            ln.low(dve, g, g % 2)
                        if q + 2 < QUARTERS:
                            ln.start(dve, q + 2)
                        if q == 0:
                            dve.wait_ge(made, 6)
                        for g in (2 * q, 2 * q + 1):
                            dve.wait_ge(t_ok, g + 1)
                            nc.vector.tensor_tensor(LG[:, g * 4:g * 4 + 4, :],
                                                    tl[g % 2][:].rearrange("p (j e) -> p j e", j=4)[:, :, 0:E],
                                                    bg[:].unsqueeze(1).broadcast_to([P, 4, E]), ALU.add).then_inc(lg_ok, 1)
                        dve.wait_ge(lg_ok, 2 * q + 2)
                        places(q)
                    nc.vector.tensor_tensor(s1[:], m2[:], m1[:], ALU.subtract).then_inc(d_ok, 1)
                    dve.wait_ge(idx_ok, QUARTERS)
                    dve.wait_ge(e_ok, 1)
                    link(nc.vector.tensor_scalar(s1[:], ex[:], 1.0, None, ALU.add))
                    link(nc.vector.reciprocal(r1[:], s1[:]))
                    link(nc.vector.tensor_scalar(wts[:, 0, :], r1[:], 0.5, None, ALU.mult))
                    link(nc.vector.tensor_tensor(wts[:, 1, :], wts[:, 0, :], ex[:], ALU.mult))

        def experts(tag, sent, send):
            HALF = CAP // 2
            UNITS = 2 * HC1
            with ExitStack() as ctx:
                rows = [sbuf(ctx, f"{tag}in{i}", [P, ST, C]) for i in range(2)]
                DTh = [sbuf(ctx, f"{tag}DTh{i}", [P, CAP], FR) for i in range(2)]
                DTl = [sbuf(ctx, f"{tag}DTl{i}", [P, CAP], FR) for i in range(2)]
                w12 = [sbuf(ctx, f"{tag}w12{i}", [P, 2, HID1]) for i in range(2)]
                wh = [sbuf(ctx, f"{tag}wh{i}", [P, 2, HID1], FR) for i in range(2)]
                wl = [sbuf(ctx, f"{tag}wl{i}", [P, 2, HID1], FR) for i in range(2)]
                w3 = [sbuf(ctx, f"{tag}w3{i}", [P, HC1, C]) for i in range(2)]
                gate = sbuf(ctx, f"{tag}gate", [P, 2, HALF])
                hid = sbuf(ctx, f"{tag}hid", [P, HC1, CAP])
                res = [sbuf(ctx, f"{tag}res{i}", [P, ST, C]) for i in range(2)]
                pg = banks(ctx, f"{tag}pg", 2)
                pu = banks(ctx, f"{tag}pu", 2)
                pt = ctx.enter_context(nc.psum_tensor(f"{tag}pt", [P, 1024], F))
                po = ctx.enter_context(nc.psum_tensor(f"{tag}po", [P, 1024], F))
                t_ok, dth_ok, dtl_ok, wh_ok, wl_ok, up_ok, silu_ok, hid_ok, down_ok, res_ok, *dmas = sems(
                    ctx, f"{tag}e", "t_ok", "dth_ok", "dtl_ok", "wh_ok", "wl_ok", "up_ok", "silu_ok", "hid_ok",
                    "down_ok", "res_ok", "w_in0", "w_in1", "row_in0", "row_in1", "stored0", "stored1")
                w_in, row_in, stored = dmas[0:2], dmas[2:4], dmas[4:6]

                def late(e, k):
                    return not isinstance(e, int) or e >= k

                def slots(buf, e):
                    return buf[bass.ds(e * CAP, CAP), :].rearrange("(j p) c -> p j c", p=P)

                with nc.Block() as block:
                    @block.gpsimd
                    def _(pool):
                        send(pool, TILES * 3 // 4, TILES)
                        pool.wait_ge(sent, 16 * TILES * TOPK)

                    @block.sync
                    def _(sp):
                        def load_rows(e, p):
                            if late(e, 2):
                                sp.wait_ge(t_ok, e - 1)
                            sp.dma_start(rows[p][:], slots(slots_in, e)).then_inc(row_in[p], 16)

                        def load_weights(e, p):
                            if late(e, 2):
                                sp.wait_ge(wl_ok, e - 1)
                            sp.dma_start(w12[p][:, 0, :], W1[bass.ds(e, 1)].squeeze(0)).then_inc(w_in[p], 16)
                            sp.dma_start(w12[p][:, 1, :], W2[bass.ds(e, 1)].squeeze(0)).then_inc(w_in[p], 16)
                            if late(e, 2):
                                sp.wait_ge(down_ok, e - 1)
                            sp.dma_start(w3[p][:], W3[bass.ds(e, 1)].squeeze(0).rearrange(
                                "(c p) d -> p c d", p=P)).then_inc(w_in[p], 16)

                        def store(e, p):
                            sp.wait_ge(res_ok, e + 1)
                            sp.dma_start(slots(slots_out, e), res[p][:]).then_inc(stored[p], 16)

                        load_weights(0, 0)
                        load_weights(1, 1)
                        sp.wait_ge(sent, 16 * TILES * TOPK)
                        load_rows(0, 0)
                        load_rows(1, 1)
                        with sp.Fori(1, E // 2) as m:
                            for p in range(2):
                                load_rows(2 * m + p, p)
                                load_weights(2 * m + p, p)
                                store(2 * m - 2 + p, p)
                        store(E - 2, 0)
                        store(E - 1, 1)
                        for p in range(2):
                            sp.wait_ge(row_in[p], 16 * (E // 2))
                            sp.wait_ge(w_in[p], 48 * (E // 2))
                            sp.wait_ge(stored[p], 16 * (E // 2))

                    @block.tensor
                    def _(pe):
                        def turn(e, p, m):
                            pe.wait_ge(row_in[p], 16 * m + 16)
                            if late(e, 1):
                                pe.wait_ge(dtl_ok, e)
                            for j in range(ST):
                                t = nc.tensor.transpose(pt[:, j * P:(j + 1) * P], rows[p][:, j, :], ident[:])
                            t.then_inc(t_ok, 1)

                        def up(e, p):
                            pe.wait_ge(wl_ok, e + 1)
                            pe.wait_ge(dtl_ok, e + 1)
                            for u in range(UNITS):
                                c, s = u // 2, slice(u % 2 * HALF, (u % 2 + 1) * HALF)
                                w = slice(c * P, (c + 1) * P)
                                for i, bank, read in ((0, pg[u % 2], silu_ok), (1, pu[u % 2], hid_ok)):
                                    if late(e, 1) or u >= 2:
                                        pe.wait_ge(read, UNITS * e + u - 1)
                                    o = bank[:, 0:HALF]
                                    nc.tensor.matmul(o, wh[p][:, i, w], DTh[p][:, s], start=True, stop=False)
                                    nc.tensor.matmul(o, wl[p][:, i, w], DTh[p][:, s], start=False, stop=False)
                                    nc.tensor.matmul(o, wh[p][:, i, w], DTl[p][:, s], start=False,
                                                     stop=True).then_inc(up_ok, 1)

                        def down(e, p):
                            pe.wait_ge(hid_ok, UNITS * (e + 1))
                            if late(e, 1):
                                pe.wait_ge(res_ok, e)
                            for j in range(ST):
                                for c in range(HC1):
                                    d = nc.tensor.matmul(po[:, j * P:(j + 1) * P], hid[:, c, j * P:(j + 1) * P],
                                                         w3[p][:, c, :], start=(c == 0), stop=(c == HC1 - 1))
                            d.then_inc(down_ok, 1)

                        def pair(m):
                            for p in range(2):
                                up(2 * m + p, p)
                                turn(2 * m + p + 1, 1 - p, m + p)
                                down(2 * m + p, p)

                        turn(0, 0, 0)
                        pair(0)
                        with pe.Fori(1, E // 2 - 1) as m:
                            pair(m)
                        m = E // 2 - 1
                        up(E - 2, 0)
                        turn(E - 1, 1, m)
                        down(E - 2, 0)
                        up(E - 1, 1)
                        down(E - 1, 1)

                    @block.scalar
                    def _(act):
                        def weights_high(e, p, m):
                            act.wait_ge(w_in[p], 48 * m + 48)
                            nc.scalar.activation(wh[p][:], w12[p][:], ACT.Copy).then_inc(wh_ok, 1)

                        def turned_high(e, p):
                            act.wait_ge(t_ok, e + 1)
                            nc.scalar.activation(DTh[p][:], pt[:, 0:CAP], ACT.Copy).then_inc(dth_ok, 1)

                        def silu(e):
                            for u in range(UNITS):
                                act.wait_ge(up_ok, 2 * (UNITS * e + u) + 1)
                                if late(e, 1) or u >= 2:
                                    act.wait_ge(hid_ok, UNITS * e + u - 1)
                                nc.scalar.activation(gate[:, u % 2, :], pg[u % 2][:, 0:HALF], ACT.Silu).then_inc(silu_ok, 1)

                        def result(e, p, m):
                            act.wait_ge(down_ok, e + 1)
                            if late(e, 2):
                                act.wait_ge(stored[p], 16 * m)
                            nc.scalar.activation(res[p][:].rearrange("p j c -> p (j c)"), po[:, 0:CAP],
                                                 ACT.Copy).then_inc(res_ok, 1)

                        def expert(m, p):
                            e = 2 * m + p
                            if late(e, 1):
                                result(e - 1, 1 - p, m - 1 + p)
                            silu(e)
                            if not isinstance(e, int) or e < E - 1:
                                turned_high(e + 1, 1 - p)
                                weights_high(e + 1, 1 - p, m + p)

                        weights_high(0, 0, 0)
                        turned_high(0, 0)
                        expert(0, 0)
                        expert(0, 1)
                        with act.Fori(1, E // 2 - 1) as m:
                            expert(m, 0)
                            expert(m, 1)
                        expert(E // 2 - 1, 0)
                        expert(E // 2 - 1, 1)
                        result(E - 1, 1, E // 2 - 1)

                    @block.vector
                    def _(dve):
                        def weights_low(e, p):
                            dve.wait_ge(wh_ok, e + 1)
                            nc.vector.tensor_tensor(wl[p][:], w12[p][:], wh[p][:].bitcast(F), ALU.subtract).then_inc(wl_ok, 1)

                        def turned_low(e, p):
                            dve.wait_ge(dth_ok, e + 1)
                            nc.vector.tensor_tensor(DTl[p][:], pt[:, 0:CAP], DTh[p][:].bitcast(F),
                                                    ALU.subtract).then_inc(dtl_ok, 1)

                        def gated(e):
                            for u in range(UNITS):
                                c, s = u // 2, slice(u % 2 * HALF, (u % 2 + 1) * HALF)
                                dve.wait_ge(silu_ok, UNITS * e + u + 1)
                                dve.wait_ge(up_ok, 2 * (UNITS * e + u) + 2)
                                nc.vector.tensor_tensor(hid[:, c, s], gate[:, u % 2, :], pu[u % 2][:, 0:HALF],
                                                        ALU.mult).then_inc(hid_ok, 1)

                        def expert(e, p):
                            gated(e)
                            turned_low(e + 1, 1 - p)
                            weights_low(e + 1, 1 - p)

                        weights_low(0, 0)
                        turned_low(0, 0)
                        with dve.Fori(0, E // 2 - 1) as m:
                            expert(2 * m, 0)
                            expert(2 * m + 1, 1)
                        expert(E - 2, 0)
                        gated(E - 1)

        def combine_parts(ctx, tag, idx, wts):
            PART = TILES // GROUPS
            got = sbuf(ctx, f"{tag}got", [P, TILES * TOPK, C])
            added, *arrived = sems(ctx, f"{tag}c", "added", *[f"arrived{i}" for i in range(GROUPS)])

            def gather(pool, first=0, end=TILES):
                for t in range(first, end):
                    for k in range(TOPK):
                        n = t * TOPK + k
                        nc.gpsimd.indirect_dma_start(
                            got[:, n, :], None, slots_out,
                            bass.IndirectOffsetOnAxis(ap=idx[:, k, t:t + 1], axis=0)).then_inc(arrived[t // PART], 16)

            def add(dve, part):
                dve.wait_ge(arrived[part], 16 * TOPK * PART)
                for k in range(TOPK):
                    if k:
                        dve.wait_ge(added, TOPK * PART * part + PART)
                    for t in range(part * PART, (part + 1) * PART):
                        nc.vector.scalar_tensor_tensor(x[:, t, :], got[:, t * TOPK + k, :], wts[:, k, t:t + 1],
                                                       x[:, t, :], ALU.mult, ALU.add).then_inc(added, 1)
                dve.wait_ge(added, TOPK * PART * (part + 1))

            parts = Parts()
            parts.gather, parts.add, parts.added, parts.per_part = gather, add, added, TOPK * PART
            return parts

        def store(combining):
            with ExitStack() as ctx:
                sums = combining(ctx)
                (stored,) = sems(ctx, "st", "x")
                with nc.Block() as block:
                    @block.gpsimd
                    def _(pool):
                        sums.gather(pool)

                    @block.vector
                    def _(dve):
                        for part in range(GROUPS):
                            sums.add(dve, part)

                    @block.sync
                    def _(sp):
                        rows = out.rearrange("(t p) c -> p t c", p=P)
                        for part in range(GROUPS):
                            sp.wait_ge(sums.added, sums.per_part * (part + 1))
                            sp.dma_start(rows[:, part * 4:part * 4 + 4, :], x[:, part * 4:part * 4 + 4, :]).then_inc(stored, 16)
                        sp.wait_ge(stored, 16 * GROUPS)

        ffn0("f1", first=True)
        wide_attention("a0", D0, 1.0 / 8.0, wqT, wkT, wvT, wp, bp, table)
        ffn0("f2")

        def second(combining):
            narrow_attention("a1", float(1.0 / np.sqrt(np.float32(D1))), wkqv, bdup, b1, wproj, pdup, bproj, pick, slopes,
                             combining)

        moe("m1", second)
        moe("m2", store)


def kernel(**inputs):
    import concourse.bacc as bacc
    from concourse.bass_utils import run_bass_kernel_spmd

    a = {k: np.asarray(v) for k, v in inputs.items()}
    bkqv = a["L1_attn_b_kqv"].reshape(3, H // 4, 4, 1, D1)
    rows = np.arange(P)
    arrays = {
        "x": a["L0_attn_x"].reshape(TOKENS, C),
        "wqT": a["L0_attn_Wq"].transpose(2, 0, 1),
        "wkT": a["L0_attn_Wk"].transpose(2, 0, 1),
        "wvT": a["L0_attn_Wv"].transpose(2, 0, 1),
        "wp": a["L0_attn_Wp"].reshape(H, D0, C).transpose(1, 0, 2),
        "bp": a["L0_attn_bp"].reshape(1, C),
        "table": a["L0_attn_rel_table"].reshape(1, -1),
        "wg0": a["L0_ffn_w_gate"].T,
        "wu0": a["L0_ffn_w_up"].T,
        "wd0": a["L0_ffn_w_down"].T,
        "wkqv": a["L1_attn_W_kqv"],
        "bdup": np.broadcast_to(bkqv[0:2], (2, H // 4, 4, 4, D1)).reshape(2, H // 4, P).transpose(2, 0, 1),
        "b1": bkqv[2].reshape(C, 1),
        "wproj": a["L1_attn_W_proj"],
        "pdup": np.broadcast_to(a["L1_attn_W_proj"].reshape(2, 8, 1, D1, C), (2, 8, 2, D1, C)).reshape(
            2, P, C).transpose(1, 0, 2),
        "bproj": a["L1_attn_b_proj"].reshape(1, C),
        "pick": np.stack([rows // D1 % 2, rows // D1 // 2 % 2], 1).astype(np.float32),
        "slopes": a["L1_attn_slopes"].reshape(1, H),
        "wgate": a["L1_ffn_Wg"],
        "bgate": a["L1_ffn_bg"].reshape(1, E),
        "W1": a["L1_ffn_W1"],
        "W2": a["L1_ffn_W2"],
        "W3": a["L1_ffn_W3"],
    }
    arrays = {k: np.ascontiguousarray(v) for k, v in arrays.items()}
    nc = bacc.Bacc("TRN2", target_bir_lowering=False, num_devices=1)
    handles = [nc.dram_tensor(f"in_{k}", v.shape, mybir.dt.from_np(v.dtype), kind="ExternalInput").ap()
               for k, v in arrays.items()]
    y = nc.dram_tensor("out_y", [TOKENS, C], F, kind="ExternalOutput").ap()
    program(nc, *handles, y)
    r = run_bass_kernel_spmd(nc, [{f"in_{k}": v for k, v in arrays.items()}], core_ids=[0])
    return r.results[0]["out_y"].reshape(B, S, C)
```
